# Optimizing a Trainium2 kernel written in Bass

```python
import numpy as np
import jax
import jax.numpy as jnp

def _softmax(x, axis=-1):
    return jax.nn.softmax(x, axis=axis)

def _gelu(x):
    return jax.nn.gelu(x, approximate=True)

def _silu(x):
    return jax.nn.silu(x)

def _sigmoid(x):
    return jax.nn.sigmoid(x)

def _layernorm(x, axis=-1, eps=1e-05):
    m = jnp.mean(x, axis=axis, keepdims=True)
    v = jnp.var(x, axis=axis, keepdims=True)
    return (x - m) / jnp.sqrt(v + eps)

def _scatter_add(tgt, idx, src, axis=0):
    return tgt.at[idx].add(src)

def _segment_sum(src, seg, n):
    return jax.ops.segment_sum(src, seg, n)
kernel_name = 'mk_xattn_ffn_d1_seqx_r4_d99a1c'

def setup_inputs(seed: int=0):
    np.random.seed(seed)
    _w = jnp.asarray

    def _rec_inputs():
        import jax
        import jax.numpy as jnp
        _rk = jax.random.key(seed)
        x = -0.0005207 + 1.001 * jax.random.normal(jax.random.fold_in(_rk, 1), (2, 1024, 256), jnp.float32)
        _lenS = 1024 - jax.random.randint(jax.random.fold_in(_rk, 7), (2,), 0, max(1, 1024 // 4) + 1, jnp.int32)
        _lenS2 = 154 - jax.random.randint(jax.random.fold_in(_rk, 8), (2,), 0, max(1, 154 // 4) + 1, jnp.int32)
        _ctx_1024P = jax.random.normal(jax.random.fold_in(_rk, 11), (2, 16, 256), jnp.float32)
        _ctx_1024c = jax.random.dirichlet(jax.random.fold_in(_rk, 511), 0.3 * jnp.ones((16,), jnp.float32), (2, 154))
        _ctx_1024t = jnp.einsum('bsk,bkd->bsd', _ctx_1024c, _ctx_1024P)
        _ctx_1024t = _ctx_1024t * jax.lax.rsqrt(jnp.mean(jnp.square(_ctx_1024t)) + 1e-12) * 0.953939
        ctx_1024 = 4.13588e-05 + 0.999923 * (_ctx_1024t + 0.3 * jax.random.normal(jax.random.fold_in(_rk, 611), (2, 154, 256), jnp.float32))
        _validS = jnp.arange(1024)[None, :] < _lenS[:, None]
        _validS2 = jnp.arange(154)[None, :] < _lenS2[:, None]
        _causal = jnp.tril(jnp.ones((1024, 1024), dtype=bool))
        mask_BxSxS2_bk0 = jnp.logical_not(jnp.broadcast_to(_validS2[:, None, :], (2, 1024, 154)))
        return (x, ctx_1024, mask_BxSxS2_bk0)
    x, ctx_1024, mask_BxSxS2_bk0 = _rec_inputs()

    def _L0_xattn_setup():
        import jax, jax.numpy as jnp
        import numpy as np
        NUM_HEADS = 16

        def softmax1(attn):
            padded = jnp.pad(attn, ((0, 0), (0, 0), (0, 0), (0, 1)))
            return jax.nn.softmax(padded, axis=-1)[..., :-1]
        key = jax.random.key(seed)
        ks = jax.random.split(key, 7)
        B, N, M, C = (2, 256, 1024, 256)
        x = jax.random.normal(ks[0], (B, N, C), dtype=jnp.float32)
        context = jax.random.normal(ks[1], (B, M, C), dtype=jnp.float32)
        mask = jax.random.randint(ks[2], (B, N, M), 0, 2) > 0
        s = 1.0 / np.sqrt(C)
        Wq = jax.random.normal(ks[3], (C, C), dtype=jnp.float32) * s
        Wkv = jax.random.normal(ks[4], (C, 2 * C), dtype=jnp.float32) * s
        Wproj = jax.random.normal(ks[5], (C, C), dtype=jnp.float32) * s
        bproj = jnp.zeros((C,), dtype=jnp.float32)
        return {'x': x, 'context': context, 'mask': mask, 'Wq': Wq, 'Wkv': Wkv, 'Wproj': Wproj, 'bproj': bproj}
    _L0_xattn_all = _L0_xattn_setup()
    _L0_xattn_in = {k: v for k, v in _L0_xattn_all.items() if k in ('Wq', 'Wkv', 'Wproj', 'bproj')}
    del _L0_xattn_all

    def _L0_ffn_setup():
        import math
        import jax, jax.numpy as jnp
        import numpy as np
        NUM_EXPERTS = 8
        CAPACITY_FACTOR = 1.5
        key = jax.random.key(seed)
        ks = jax.random.split(key, 4)
        B, T, D, F, E = (4, 512, 256, 1024, NUM_EXPERTS)
        scale = 0.02
        return {'x': jax.random.normal(ks[0], (B, T, D), dtype=jnp.float32), 'router_w': jax.random.normal(ks[1], (E, D), dtype=jnp.float32) * scale, 'w1': jax.random.normal(ks[2], (E, D, F), dtype=jnp.float32) * scale, 'b1': jnp.zeros((E, F), dtype=jnp.float32), 'w2': jax.random.normal(ks[3], (E, F, D), dtype=jnp.float32) * scale, 'b2': jnp.zeros((E, D), dtype=jnp.float32)}
    _L0_ffn_all = _L0_ffn_setup()
    _L0_ffn_in = {k: v for k, v in _L0_ffn_all.items() if k in ('router_w', 'w1', 'b1', 'w2', 'b2')}
    del _L0_ffn_all
    return {'x': x, 'ctx_1024': ctx_1024, 'mask_BxSxS2_bk0': mask_BxSxS2_bk0, 'L0_xattn_Wq': _L0_xattn_in['Wq'], 'L0_xattn_Wkv': _L0_xattn_in['Wkv'], 'L0_xattn_Wproj': _L0_xattn_in['Wproj'], 'L0_xattn_bproj': _L0_xattn_in['bproj'], 'L0_ffn_router_w': _L0_ffn_in['router_w'], 'L0_ffn_w1': _L0_ffn_in['w1'], 'L0_ffn_b1': _L0_ffn_in['b1'], 'L0_ffn_w2': _L0_ffn_in['w2'], 'L0_ffn_b2': _L0_ffn_in['b2']}

def reference(x, ctx_1024, mask_BxSxS2_bk0, L0_xattn_Wq, L0_xattn_Wkv, L0_xattn_Wproj, L0_xattn_bproj, L0_ffn_router_w, L0_ffn_w1, L0_ffn_b1, L0_ffn_w2, L0_ffn_b2):
    import jax
    import jax.numpy as jnp

    def _L0_xattn_ref(x, context, mask, Wq, Wkv, Wproj, bproj):
        import jax, jax.numpy as jnp
        import numpy as np
        NUM_HEADS = 16

        def softmax1(attn):
            padded = jnp.pad(attn, ((0, 0), (0, 0), (0, 0), (0, 1)))
            return jax.nn.softmax(padded, axis=-1)[..., :-1]
        B, N, C = x.shape
        M = context.shape[1]
        H = NUM_HEADS
        d = C // H
        scale = d ** (-0.5)
        q = (x @ Wq).reshape(B, N, H, d).transpose(0, 2, 1, 3)
        kv = (context @ Wkv).reshape(B, M, 2, H, d)
        k = kv[:, :, 0].transpose(0, 2, 1, 3)
        v = kv[:, :, 1].transpose(0, 2, 1, 3)
        attn = jnp.einsum('bhnd,bhmd->bhnm', q, k) * scale
        neg = -jnp.finfo(attn.dtype).max
        attn = jnp.where(mask[:, None, :, :], neg, attn)
        attn = softmax1(attn)
        out = jnp.einsum('bhnm,bhmd->bhnd', attn, v)
        out = out.transpose(0, 2, 1, 3).reshape(B, N, C)
        return out @ Wproj + bproj

    def _L0_ffn_ref(x, router_w, w1, b1, w2, b2):
        import math
        import jax, jax.numpy as jnp
        import numpy as np
        NUM_EXPERTS = 8
        CAPACITY_FACTOR = 1.5
        B, T, D = x.shape
        E = router_w.shape[0]
        N = B * T
        C = max(math.ceil(CAPACITY_FACTOR * N / E), 1)
        x_flat = x.reshape(N, D)
        logits = x_flat @ router_w.T
        probs = jax.nn.softmax(logits, axis=-1)
        chosen_e = jnp.argmax(probs, axis=-1)
        chosen_p = jnp.max(probs, axis=-1)
        onehot = jax.nn.one_hot(chosen_e, E, dtype=jnp.float32)
        pos = jnp.take_along_axis(jnp.cumsum(onehot, axis=0), chosen_e[:, None], axis=1)[:, 0] - 1.0
        pos = pos.astype(jnp.int32)
        kept = pos < C
        pos_c = jnp.clip(pos, 0, C - 1)
        buf = jnp.zeros((E, C, D), dtype=x.dtype).at[chosen_e, pos_c].add(x_flat * kept[:, None].astype(x.dtype))
        h = jax.nn.gelu(jnp.einsum('ecd,edf->ecf', buf, w1) + b1[:, None, :], approximate=False)
        eo = jnp.einsum('ecf,efd->ecd', h, w2) + b2[:, None, :]
        y = eo[chosen_e, pos_c] * (chosen_p * kept.astype(x.dtype))[:, None]
        return y.reshape(B, T, D)
    x = x + _L0_xattn_ref(_layernorm(x, axis=-1), ctx_1024, mask_BxSxS2_bk0, L0_xattn_Wq, L0_xattn_Wkv, L0_xattn_Wproj, L0_xattn_bproj)
    x = x + _L0_ffn_ref(_layernorm(x, axis=-1), L0_ffn_router_w, L0_ffn_w1, L0_ffn_b1, L0_ffn_w2, L0_ffn_b2)
    return x

_drawn_inputs = setup_inputs


def setup_inputs(seed=0):
    import zlib

    import numpy as np

    out = dict(_drawn_inputs(seed))
    spreads = {'L0_xattn_bproj': (0.0, 0.1), 'L0_ffn_b1': (0.0, 0.8), 'L0_ffn_b2': (0.0, 0.46)}
    factors = {'L0_ffn_w1': 3.005, 'L0_ffn_w2': 2.817}
    for name, (base, spread) in spreads.items():
        noise = np.random.default_rng([zlib.crc32(name.encode()), seed]).standard_normal(out[name].shape)
        drawn = base * np.exp(spread * noise) if base else spread * noise
        out[name] = jnp.asarray(drawn.astype(out[name].dtype))
    for name, factor in factors.items():
        out[name] = (out[name] * factor).astype(out[name].dtype)
    return out
```

```python
from contextlib import ExitStack

import concourse.bass as bass
from concourse import mybir

F32 = mybir.dt.float32
F32R = mybir.dt.float32r
BF16 = mybir.dt.bfloat16
I32 = mybir.dt.int32
U8 = mybir.dt.uint8
ALU = mybir.AluOpType
ACT = mybir.ActivationFunctionType
AX_X = mybir.AxisListType.X

P = 128
NEG = -1.0e30
EPS = 1e-5
HEADS = 16

STAGES = [
    ("proj", 0), ("keys", 0), ("mask", 0), ("scan", 0), ("proj", 1), ("mask", 1), ("small", 0),
    ("mix", 0), ("keys", 1), ("proj", 2), ("mask", 2), ("fold", 0),
    ("mix", 1), ("proj", 3), ("mask", 3), ("fold", 1),
    ("mix", 2), ("fold", 2), ("mix", 3), ("fold", 3), ("route", 3), ("assign", 0),
]
ROUTE_AT = 8


class Count:

    def __init__(self, engine, semaphore):
        self.engine, self.semaphore, self.n = engine, semaphore, 0

    def up(self, instruction):
        instruction.then_inc(self.semaphore, 1)
        self.n += 1

    def settle(self):
        self.engine.wait_ge(self.semaphore, self.n)


def small_jobs(tiles):
    jobs = []
    for stage, c in STAGES:
        if stage == "proj":
            jobs += [(("xT", c, k), "act") for k in range(2)] + [(("q", c, k), "dve") for k in range(2)]
        if stage == "keys":
            jobs += [(("ctxT", c), "act"), (("k", c, 0), "dve"), (("k", c, 1), "dve"), (("v", c), "dve"), (("vr", c), "dve")]
        if stage == "mask":
            jobs += [(("maskT", c), "act")]
        if stage == "scan":
            jobs += [(("max", c), "act")]
        if stage == "small":
            jobs += [(("rT",), "act"), (("b1T",), "act")]
        if stage == "mix":
            if c:
                jobs += route_jobs(c - 1, tiles)
            if c < 3:
                jobs += [(("max", c + 1), "act")]
        if stage == "fold":
            jobs += [(("fold", c, t), "dve") for t in range(tiles)]
        if stage == "route":
            jobs += route_jobs(c, tiles)
        if stage == "assign":
            jobs += [(("cum",), "dve"), (("slots",), "dve")]
    return jobs


def route_jobs(c, tiles):
    return [(("nT", c, t), "act") for t in range(tiles)] + [(("logits", c), "dve")]


def build(nc, x, ctx, mask, wq, wkv, wproj, bproj, router, w1, b1, w2, b2, out):
    B, N, D = x.shape
    M = ctx.shape[1]
    H = HEADS
    DH = D // H
    E, _, F = w1.shape
    KC = D // P
    HH = H // KC
    G = H // 2
    CH = 512
    NCH = B * N // CH
    PER_B = N // CH
    TT = CH // P
    T = B * N // P
    MR = M - P
    RP = 32
    MP = P + RP
    UN = 10
    AU = 5
    CAP = max(-(-3 * B * N // (2 * E)), 1)
    JT = CAP // P
    J = E * JT
    FC = F // P
    ROW = D + 4
    NTOK = B * N
    SCALE = float(DH) ** -0.5
    assert D == 256 and NCH == 4 and 0 < MR < RP and CAP % P == 0 and E % 2 == 0 and H * DH == D
    FAR = float(2 * NTOK)

    x_t = x.rearrange("b (t p) d -> p (b t) d", p=P)
    mask_t = mask.rearrange("b (t p) m -> p (b t) m", p=P)
    out_rows = out.rearrange("b n d -> (b n) d")
    out_t = out.rearrange("b (t p) d -> p (b t) d", p=P)
    rows = nc.dram_tensor("rows", [NTOK, ROW], F32, kind="Internal").ap()
    rows_t = rows.rearrange("(t p) d -> p t d", p=P)

    jobs = small_jobs(TT)
    job_at = {name: n for n, (name, _) in enumerate(jobs)}

    with ExitStack() as stack:
        def make(scope):
            def sb(name, shape, dt=F32):
                return scope.enter_context(nc.sbuf_tensor(name, shape, dt))
            return sb

        sb = make(stack)

        def sem(name):
            return stack.enter_context(nc.semaphore(name))

        bank = [stack.enter_context(nc.psum_tensor(f"bank{i}", [P, 512], F32)) for i in range(8)]
        a_bank, st_bank, o_bank, z_bank, small_bank = bank[0:2], bank[2:4], bank[4], bank[5], bank[6:8]
        t_bank, y_bank, h_bank = bank[0:2], bank[2:4], bank[4:8]

        ident = sb("ident", [P, P])
        xr = sb("xr", [P, T, ROW])
        b1T = sb("b1T", [P, E * FC])
        tok = sb("tok", [P, J])
        tokfar = sb("tokfar", [P, J])
        tok_store = sb("tok_store", [P, J], I32)
        tok_load = sb("tok_load", [P, J], I32)
        w1_sb = [sb("w1_sb0", [P, KC, F])]
        w2_sb = [sb("w2_sb0", [P, FC, D])]

        attention = ExitStack()
        sa = make(attention)
        identb = sa("identb", [P, P], BF16)
        onesb = sa("onesb", [P, P], BF16)
        trib = sa("trib", [P, P], BF16)
        wq_sb = sa("wq_sb", [P, KC, D])
        wkv_sb = sa("wkv_sb", [P, KC, 2 * D])
        wp_sb = sa("wp_sb", [P, KC, D])
        bp_sb = sa("bp_sb", [P, D])
        r_sb = sa("r_sb", [E, D])
        rT = sa("rT", [P, KC, E])
        b1_sb = sa("b1_sb", [E * FC, P])
        headsel = sa("headsel", [P, HH])
        pairsel = sa("pairsel", [P, 2, P])
        z_main = sa("z_main", [P, 2, RP])
        z_rest = sa("z_rest", [P, 2, RP])
        neghalf = sa("neghalf", [P, TT])
        lane = sa("lane", [P, P])
        part = sa("part", [P, 1])
        tileno = sa("tileno", [P, T, J])
        first = sa("first", [P, TT, E])
        ebase = sa("ebase", [P, T, E])

        ctx_sb = sa("ctx_sb", [P, B, 2, D])
        ctxT = sa("ctxT", [P, KC, MP])
        k_hi = sa("k_hi", [P, KC, MP], F32R)
        k_lo = sa("k_lo", [P, KC, MP], F32R)
        kd_hi = sa("kd_hi", [P, KC, HH, MP], F32R)
        kd_lo = sa("kd_lo", [P, KC, HH, MP], F32R)
        ks_main = [sa(f"ks_main{b}", [P, G, 2, P], F32R) for b in range(B)]
        ks_rest = [sa(f"ks_rest{b}", [P, G, P], F32R) for b in range(B)]
        v_main = [sa(f"v_main{b}", [P, H, RP]) for b in range(B)]
        v_rest = [sa(f"v_rest{b}", [P, H // 4, 2, RP]) for b in range(B)]
        mask_sb = sa("mask_sb", [P, T, M], U8)
        negm = sa("negm", [P, T, P + 4 * RP], BF16)
        maskT = [sa(f"maskT{i}", [P, 2, CH], BF16) for i in range(2)]
        stats = sa("stats", [P, TT, 6])
        mv = sa("mv", [P, TT, 2])
        var = sa("var", [P, TT])
        rstd = sa("rstd", [P, TT])
        var2 = sa("var2", [P, TT])
        xn = sa("xn", [P, TT, D])
        xT = sa("xT", [P, KC, CH])
        q_hi = sa("q_hi", [P, KC, CH], F32R)
        q_lo = sa("q_lo", [P, KC, CH], F32R)
        qs = [sa(f"qs{i}", [P, G, CH], F32R) for i in range(2)]
        mx = sa("mx", [P, TT, H])
        mxr = sa("mxr", [P, TT, H])
        mxx = sa("mxx", [P, TT, H])
        nmT = sa("nmT", [H, CH], F32R)
        pt = sa("pt", [P, UN, CH])
        rz = sa("rz", [P, CH])
        att = sa("att", [P, KC, CH])
        xn2 = sa("xn2", [P, 2, D])
        xn2T = sa("xn2T", [P, TT, KC, P])

        lg = sa("lg", [P, TT, E])
        lmax = sa("lmax", [P, TT])
        below = sa("below", [P, TT, E])
        lex = sa("lex", [P, TT, E])
        lsum = sa("lsum", [P, TT])
        rank = sa("rank", [P, TT, E])
        best = sa("best", [P, TT])
        onehot = sa("onehot", [P, T, E], BF16)
        cum = sa("cum", [P, T, E])
        ebs = sa("ebs", [P, T, E])
        pos = sa("pos", [P, T])
        jslot = sa("jslot", [P, T])
        over = sa("over", [P, T, JT])
        pslot = sa("pslot", [P, T])
        spare = negm[:, :, :].rearrange("p t m -> p (t m)")
        psel = spare[:, 0:T * P].rearrange("p (t m) -> p t m", t=T)
        what = spare[:, T * P:T * (P + 3 * J)].rearrange("p (t c j) -> p t c j", t=T, c=3)
        jsel = spare[:, T * (P + 3 * J):T * (P + 4 * J)].rearrange("p (t j) -> p t j", t=T)
        slots = sa("slots", [P, 3, J])
        attention.close()

        w1_sb.append(sb("w1_sb1", [P, KC, F]))
        w2_sb.append(sb("w2_sb1", [P, FC, D]))
        xg = sb("xg", [P, J, ROW])
        b2_sb = sb("b2_sb", [P, E, D])
        gn = sb("gn", [P, 2, JT, D])
        gT = sb("gT", [P, 2, KC, CAP])
        hT = sb("hT", [P, FC, CAP])
        y1 = sb("y1", [P, JT, D])

        l_x = [sem(f"l_x{c}") for c in range(NCH)]
        l_ctx, l_wq, l_mask, l_small = sem("l_ctx"), sem("l_wq"), sem("l_mask"), sem("l_small")
        l_ks = [sem(f"l_ks{b}") for b in range(B)]
        l_qs = [sem(f"l_qs{i}") for i in range(2)]
        l_max = [sem(f"l_max{i}") for i in range(2)]
        l_rows, l_out, l_b2 = sem("l_rows"), sem("l_out"), sem("l_b2")
        l_w = [sem(f"l_w{s}") for s in range(2)]
        l_gather = [sem(f"l_gather{s}") for s in range(2)]
        l_store = [sem(f"l_store{j}") for j in range(JT)]
        pool_step, dve_step = sem("pool_step"), sem("dve_step")
        consts_made, mask_made, xn_made, rstd_made, xb_made, kdlo_made = (
            sem("consts_made"), sem("mask_made"), sem("xn_made"), sem("rstd_made"), sem("xb_made"), sem("kdlo_made"))
        small_full, small_act, small_dve = sem("small_full"), sem("small_act"), sem("small_dve")
        scan_full, scan_read = sem("scan_full"), sem("scan_read")
        st_full, exp_done, pv_done, att_made = sem("st_full"), sem("exp_done"), sem("pv_done"), sem("att_made")
        stats_made, qhi_made, qlo_made, khi_made, kdhi_made, klo_made = (
            sem("stats_made"), sem("qhi_made"), sem("qlo_made"), sem("khi_made"), sem("kdhi_made"), sem("klo_made"))
        v_made, sel_made, max_made, x1_made, xn2_made = sem("v_made"), sem("sel_made"), sem("max_made"), sem("x1_made"), sem("xn2_made")
        below_made, lex_made, gate_made, onehot_made, what_made, tok_made = (
            sem("below_made"), sem("lex_made"), sem("gate_made"), sem("onehot_made"), sem("what_made"), sem("tok_made"))
        gn_made, t_full, gT_made = sem("gn_made"), sem("t_full"), sem("gT_made")
        h_full, h_made, y_full, y_read, y_made = sem("h_full"), sem("h_made"), sem("y_full"), sem("y_read"), sem("y_made")

        def unit_of(u):
            return (u // 4, u % 4) if u < 8 else (None, u - 8)

        def pv_batch_of(u):
            return min(u // 4, 2)

        def act_count(name):
            return sum(who == "act" for _, who in jobs[:job_at[name] + 1])

        def dve_count(name):
            return sum(who == "dve" for _, who in jobs[:job_at[name] + 1])

        def small(name):
            return small_bank[job_at[name] % 2]

        block = stack.enter_context(nc.Block())

        @block.sync
        def _(sp):
            def load_x(c):
                sp.dma_start(xr[:, c * TT:(c + 1) * TT, 0:D], x_t[:, c * TT:(c + 1) * TT, :]).then_inc(l_x[c], 16)

            def keys(b):
                for half in range(KC):
                    sp.wait_ge(kdhi_made, b * KC + half + 1)
                    sp.wait_ge(kdlo_made, b * KC + half + 1)
                    if b == 0 and half == 0:
                        sp.wait_ge(consts_made, 1)
                    for gg in range(G // KC):
                        g = half * (G // KC) + gg
                        for blk, kd in enumerate((kd_hi, kd_hi, kd_lo)):
                            src = kd[32 * gg:32 * gg + 32, half, 2 * gg:2 * gg + 2, :].bitcast(F32)
                            to = slice(32 * blk, 32 * blk + 32)
                            sp.dma_start(ks_main[b][to, g, :, :].bitcast(F32), src[:, :, 0:P]).then_inc(l_ks[b], 16)
                            c0 = 2 * RP * (g % 2)
                            rest = ks_rest[b][to, g, c0:c0 + 2 * RP].bitcast(F32).rearrange("p (a m) -> p a m", a=2)
                            sp.dma_start(rest, src[:, :, P:MP]).then_inc(l_ks[b], 16)

            def proj(c):
                sp.wait_ge(qlo_made, KC * (c + 1))
                if c >= 2:
                    sp.wait_ge(st_full, 2 * UN * (c - 1))
                else:
                    sp.wait_ge(consts_made, 1)
                for g in range(G):
                    half, gg = g // (G // KC), g % (G // KC)
                    for blk, q in enumerate((q_hi, q_lo, q_hi)):
                        sp.dma_start(qs[c % 2][32 * blk:32 * blk + 32, g, :].bitcast(F32),
                                     q[32 * gg:32 * gg + 32, half, :].bitcast(F32)).then_inc(l_qs[c % 2], 16)

            def maxima(c):
                sp.wait_ge(small_act, act_count(("max", c)))
                if c >= 2:
                    sp.wait_ge(st_full, 2 * UN * (c - 1))
                for g in range(G):
                    sp.dma_start(qs[c % 2][96:98, g, :].bitcast(F32),
                                 nmT[2 * g:2 * g + 2, :].bitcast(F32)).then_inc(l_max[c % 2], 16)

            def store_rows(c):
                sp.wait_ge(gate_made, c + 1)
                sl = slice(c * TT, (c + 1) * TT)
                sp.dma_start(rows_t[:, sl, :], xr[:, sl, :]).then_inc(l_rows, 16)
                sp.dma_start(out_t[:, sl, :], xr[:, sl, 0:D]).then_inc(l_out, 16)

            def load_expert(e, s):
                e_ = bass.ds(e, 1) if not isinstance(e, int) else slice(e, e + 1)
                sp.dma_start(w1_sb[s][:, :, :], w1[e_].rearrange("e (k p) f -> p (e k) f", p=P)).then_inc(l_w[s], 16)
                sp.dma_start(w2_sb[s][:, :, :], w2[e_].rearrange("e (k p) d -> p (e k) d", p=P)).then_inc(l_w[s], 16)

            load_x(0)
            sp.dma_start(wq_sb[:, :, :], wq.rearrange("(k p) d -> p k d", p=P)).then_inc(l_wq, 16)
            sp.dma_start(ctx_sb[:, :, 0, :], ctx[:, 0:P, :].rearrange("b p d -> p b d")).then_inc(l_ctx, 16)
            sp.dma_start(ctx_sb[0:MR, :, 1, :], ctx[:, P:M, :].rearrange("b p d -> p b d")).then_inc(l_ctx, 16)
            sp.dma_start(wkv_sb[:, :, :], wkv.rearrange("(k p) d -> p k d", p=P)).then_inc(l_ctx, 16)
            sp.dma_start(mask_sb[:, :, :], mask_t).then_inc(l_mask, 16)
            load_x(1)
            sp.dma_start(wp_sb[:, :, :], wproj.rearrange("(k p) d -> p k d", p=P)).then_inc(l_small, 16)
            sp.dma_start(bp_sb[:, :], bproj.rearrange("(a d) -> a d", a=1).to_broadcast([P, D])).then_inc(l_small, 16)
            sp.dma_start(r_sb[:, :], router).then_inc(l_small, 16)
            sp.dma_start(b1_sb[:, :], b1.rearrange("e (f p) -> (e f) p", p=P)).then_inc(l_small, 16)
            load_x(2)
            load_x(3)
            load_expert(0, 0)
            for stage, c in STAGES:
                if stage == "keys":
                    keys(c)
                if stage == "proj":
                    proj(c)
                if stage == "scan":
                    maxima(c)
                if stage == "mix":
                    if c:
                        store_rows(c - 1)
                    if c < NCH - 1:
                        maxima(c + 1)
                if stage == "route":
                    store_rows(c)
            sp.wait_ge(tok_made, 1)
            sp.dma_start(b2_sb[:, :, :], b2.rearrange("(a e) d -> a e d", a=1).to_broadcast([P, E, D])).then_inc(l_b2, 16)
            load_expert(1, 1)
            with sp.Fori(1, E // 2) as it:
                for s in range(2):
                    sp.wait_ge(y_full, it * (2 * JT) + (s - 1) * JT)
                    load_expert(it * 2 + s, s)

        @block.gpsimd
        def _(pool):
            steps = Count(pool, pool_step)
            p = nc.gpsimd

            def make_consts():
                steps.up(p.memset(ident[:, :], 0.0))
                steps.up(p.memset(neghalf[:, :], -0.5))
                steps.settle()
                steps.up(p.affine_select(out=ident[:, :], in_=ident[:, :], compare_op=ALU.not_equal, fill=1.0,
                                         base=0, pattern=[[-1, P]], channel_multiplier=1))
                steps.up(p.memset(onesb[:, :], 1.0))
                steps.up(p.memset(headsel[:, :], 1.0))
                steps.up(p.memset(pairsel[:, :, :], 1.0))
                steps.settle()
                steps.up(p.tensor_copy(identb[:, :], ident[:, :]))
                steps.up(p.affine_select(out=trib[:, :], in_=onesb[:, :], compare_op=ALU.is_ge, fill=0.0,
                                         base=-1, pattern=[[1, P]], channel_multiplier=-1))
                steps.up(p.affine_select(out=headsel[:, :], in_=headsel[:, :], compare_op=ALU.is_ge, fill=0.0,
                                         base=0, pattern=[[-DH, HH]], channel_multiplier=1))
                steps.up(p.affine_select(out=pairsel[:, :, :], in_=pairsel[:, :, :], compare_op=ALU.is_equal, fill=0.0,
                                         base=-96, pattern=[[-1, 2], [0, P]], channel_multiplier=1))
                steps.settle()
                steps.up(p.affine_select(out=headsel[:, :], in_=headsel[:, :], compare_op=ALU.is_ge, fill=0.0,
                                         base=DH - 1, pattern=[[DH, HH]], channel_multiplier=-1))
                for t in (z_main, z_rest):
                    steps.up(p.memset(t[:, :, :], 0.0))
                steps.up(p.memset(ctxT[:, :, M:MP], 0.0))
                for t in v_main + v_rest:
                    steps.up(p.memset(t[:], 0.0))
                for t in ks_rest:
                    steps.up(p.memset(t[:].bitcast(F32), 0.0))
                for t in ks_main:
                    steps.up(p.memset(t[:].bitcast(F32), 0.0))
                for i in range(2):
                    steps.settle()
                    steps.up(p.memset(qs[i][96:P, :, :].bitcast(F32), 0.0))
                steps.settle()
                steps.up(p.memset(negm[:, :, P:], 0.0))
                steps.settle()
                for a in range(2):
                    steps.up(p.memset(z_main[:, a, DH * a:DH * a + DH], 1.0))
                for i in range(4):
                    steps.settle()
                    steps.up(p.memset(z_rest[32 * i:32 * i + MR + 1, i // 2, DH * (i % 2):DH * (i % 2) + DH], 1.0))
                steps.settle()
                p.memset(var2[:, :], 0.0).then_inc(consts_made, 1)

            def make_late_consts():
                steps.up(p.iota(lane[:, :], pattern=[[1, P]], base=0, channel_multiplier=0,
                                allow_small_or_imprecise_dtypes=True))
                steps.up(p.iota(part[:, :], pattern=[[0, 1]], base=0, channel_multiplier=1,
                                allow_small_or_imprecise_dtypes=True))
                steps.up(p.iota(tileno[:, :, :], pattern=[[1, T], [0, J]], base=0, channel_multiplier=0,
                                allow_small_or_imprecise_dtypes=True))
                steps.up(p.iota(first[:, :, :], pattern=[[0, TT], [-1, E]], base=E, channel_multiplier=0,
                                allow_small_or_imprecise_dtypes=True))
                steps.up(p.iota(ebase[:, :, :], pattern=[[0, T], [JT, E]], base=0, channel_multiplier=0,
                                allow_small_or_imprecise_dtypes=True))
                steps.up(p.memset(xr[:, :, D + 2:ROW], 0.0))
                steps.settle()
                p.memset(var2[:, :], 0.0).then_inc(consts_made, 1)

            def make_mask(c):
                sl = slice(c * TT, (c + 1) * TT)
                if c == 0:
                    pool.wait_ge(l_mask, 16)
                p.tensor_scalar(negm[:, sl, 0:P], mask_sb[:, sl, 0:P], NEG, None, ALU.mult)
                for i in range(4):
                    ins = p.tensor_scalar(negm[:, sl, P + RP * i:P + RP * i + MR], mask_sb[:, sl, P:M], NEG, None, ALU.mult)
                ins.then_inc(mask_made, 1)

            def proj(c):
                pool.wait_ge(stats_made, c + 1)
                steps.up(p.tensor_scalar(var[:, :], mv[:, :, 1], EPS, None, ALU.add))
                steps.settle()
                steps.up(p.tensor_tensor(rstd[:, :], var[:, :], neghalf[:, :], ALU.pow))
                steps.settle()
                if c:
                    pool.wait_ge(small_full, job_at[("xT", c - 1, KC - 1)] + 1)
                for t in range(TT):
                    ins = p.tensor_scalar(xn[:, t, :], xr[:, c * TT + t, 0:D], mv[:, t, 0:1], rstd[:, t:t + 1],
                                          ALU.subtract, ALU.mult)
                ins.then_inc(xn_made, 1)
                if c == 0:
                    make_mask(0)
                if c == 1:
                    make_mask(1)
                    make_mask(2)
                    make_mask(3)
                    pool.wait_ge(l_small, 64)
                for cc in {0: [], 1: [0, 1], 2: [2], 3: [3]}[c]:
                    pool.wait_ge(xn_made, cc + 1)
                    for t in range(cc * TT, (cc + 1) * TT):
                        ins = p.tensor_tensor(xr[:, t, 0:D], xr[:, t, 0:D], bp_sb[:, :], ALU.add)
                    ins.then_inc(xb_made, 1)

            def keys(b):
                for half in range(KC):
                    pool.wait_ge(klo_made, b * KC + half + 1)
                    if b:
                        pool.wait_ge(l_ks[b - 1], 16 * 6 * G)
                    ins = p.tensor_tensor(kd_lo[:, half], k_lo[:, half, :].bitcast(F32).unsqueeze(1).to_broadcast([P, HH, MP]),
                                          headsel[:, :].unsqueeze(2).to_broadcast([P, HH, MP]), ALU.mult)
                    ins.then_inc(kdlo_made, 1)

            def fold(c):
                sl = slice(c * TT, (c + 1) * TT)
                pool.wait_ge(x1_made, c + 1)
                steps.up(p.tensor_scalar(var2[:, :], xr[:, sl, D + 1], EPS, None, ALU.add))
                steps.settle()
                p.tensor_tensor(xr[:, sl, D + 1], var2[:, :], neghalf[:, :], ALU.pow).then_inc(rstd_made, 1)

            make_consts()
            for stage, c in STAGES:
                if stage == "proj":
                    proj(c)
                if stage == "keys":
                    keys(c)
                if stage == "scan":
                    make_late_consts()
                if stage == "fold":
                    fold(c)

            pool.wait_ge(tok_made, 1)
            pool.wait_ge(l_rows, 16 * NCH)

            def gather(e):
                if e >= 2:
                    pool.wait_ge(l_gather[e % 2], 16 * JT * (e // 2))
                for j in range(JT * e, JT * (e + 1)):
                    p.indirect_dma_start(xg[:, j, :], None, rows, bass.IndirectOffsetOnAxis(ap=tok_load[:, j:j + 1], axis=0),
                                         bounds_check=NTOK - 1, oob_is_err=False).then_inc(l_gather[e % 2], 16)

            gather(0)
            gather(1)
            pool.wait_ge(l_out, 16 * NCH)
            for e in range(E):
                if e + 2 < E:
                    gather(e + 2)
                for j in range(JT):
                    pool.wait_ge(y_made, JT * (e + 1) + j + 1)
                    p.indirect_dma_start(out_rows, bass.IndirectOffsetOnAxis(ap=tok_store[:, JT * e + j:JT * e + j + 1], axis=0),
                                         xg[:, JT * e + j, 0:D], None, bounds_check=NTOK - 1, oob_is_err=False).then_inc(l_store[j], 16)
            for j in range(JT):
                pool.wait_ge(l_store[j], 16 * E)

        @block.tensor
        def _(pe):
            mm, tr = nc.tensor.matmul, nc.tensor.transpose

            def open_small(name):
                n = job_at[name]
                if n >= 2:
                    before = jobs[n - 2][0]
                    if jobs[n - 2][1] == "act":
                        pe.wait_ge(small_act, act_count(before))
                    else:
                        pe.wait_ge(small_dve, dve_count(before))
                return small(name)

            def proj(c):
                pe.wait_ge(xn_made, c + 1)
                if c == 0:
                    pe.wait_ge(consts_made, 1)
                for k in range(KC):
                    ps = open_small(("xT", c, k))
                    for t in range(TT):
                        ins = tr(ps[:, t * P:(t + 1) * P], xn[:, t, k * P:(k + 1) * P], ident[:, :])
                    ins.then_inc(small_full, 1)
                if c == 0:
                    pe.wait_ge(l_wq, 16)
                pe.wait_ge(small_act, act_count(("xT", c, KC - 1)))
                for half in range(KC):
                    ps = open_small(("q", c, half))
                    for k in range(KC):
                        ins = mm(ps[:, :], wq_sb[:, k, half * P:(half + 1) * P], xT[:, k, :], start=(k == 0), stop=(k == KC - 1))
                    ins.then_inc(small_full, 1)

            def keys(b):
                if b == 0:
                    pe.wait_ge(l_ctx, 48)
                ps = open_small(("ctxT", b))
                for k in range(KC):
                    tr(ps[:, k * MP:k * MP + P], ctx_sb[:, b, 0, k * P:(k + 1) * P], ident[:, :])
                    ins = tr(ps[:, k * MP + P:k * MP + M], ctx_sb[0:MR, b, 1, k * P:(k + 1) * P], ident[0:MR, 0:MR])
                ins.then_inc(small_full, 1)
                pe.wait_ge(small_act, act_count(("ctxT", b)))
                for half in range(KC):
                    ps = open_small(("k", b, half))
                    for k in range(KC):
                        ins = mm(ps[:, 0:MP], wkv_sb[:, k, half * P:(half + 1) * P], ctxT[:, k, :], start=(k == 0), stop=(k == KC - 1))
                    ins.then_inc(small_full, 1)
                ps = open_small(("v", b))
                for k in range(KC):
                    ins = mm(ps[:, 0:D], ctxT[:, k, 0:P], wkv_sb[:, k, D:2 * D], start=(k == 0), stop=(k == KC - 1))
                ins.then_inc(small_full, 1)
                ps = open_small(("vr", b))
                for k in range(KC):
                    ins = mm(ps[0:RP, 0:D], ctxT[:, k, P:MP], wkv_sb[:, k, D:2 * D], start=(k == 0), stop=(k == KC - 1))
                ins.then_inc(small_full, 1)

            def turn_mask(c):
                pe.wait_ge(mask_made, c + 1)
                ps = open_small(("maskT", c))[:, :].bitcast(BF16)
                for t in range(TT):
                    for r in range(2):
                        ins = tr(ps[:, r * CH + t * P:r * CH + (t + 1) * P], negm[:, c * TT + t, r * P:(r + 1) * P], identb[:, :])
                ins.then_inc(small_full, 1)

            def scan(c, i):
                t, u = divmod(i, AU)
                n = c * TT * AU + i
                if i == 0:
                    pe.wait_ge(qhi_made, KC * (c + 1))
                    pe.wait_ge(kdhi_made, KC * (c // PER_B + 1))
                    pe.wait_ge(mask_made, c + 1)
                if n >= 2:
                    pe.wait_ge(scan_read, n - 1)
                ps = a_bank[n % 2]
                tok_ = slice(t * P, (t + 1) * P)
                if u < 4:
                    half, h4 = divmod(u, 2)
                    m_ = negm[:, c * TT + t, 0:P].unsqueeze(1).to_broadcast([P, 4, P])
                    mm(ps[:, :], identb[:, :], m_, start=True, stop=False)
                    ins = mm(ps[:, :], q_hi[:, half, tok_], kd_hi[:, half, 4 * h4:4 * h4 + 4, 0:P], start=False, stop=True)
                else:
                    m_ = negm[:, c * TT + t, P:MP].unsqueeze(1).to_broadcast([P, H, RP])
                    mm(ps[:, :], identb[:, :], m_, start=True, stop=False)
                    for half in range(KC):
                        ins = mm(ps[:, half * HH * RP:(half + 1) * HH * RP], q_hi[:, half, tok_],
                                 kd_hi[:, half, :, P:MP], start=False, stop=(half == KC - 1))
                ins.then_inc(scan_full, 1)

            def maxima(c):
                pe.wait_ge(max_made, c + 1)
                ps = open_small(("max", c))
                for t in range(TT):
                    ins = tr(ps[0:H, t * P:(t + 1) * P], mxx[:, t, :], ident[:, :])
                ins.then_inc(small_full, 1)

            def scores(c, i):
                b, n = c // PER_B, 2 * UN * c + i
                half, u = divmod(i, UN)
                a, pair = unit_of(u)
                if i == 0:
                    pe.wait_ge(l_qs[c % 2], 16 * 3 * G * (c // 2 + 1))
                    pe.wait_ge(l_max[c % 2], 16 * G * (c // 2 + 1))
                    pe.wait_ge(small_act, act_count(("maskT", c)))
                    if c % PER_B == 0:
                        pe.wait_ge(l_ks[b], 16 * 6 * G)
                        pe.wait_ge(sel_made, b + 1)
                if n >= 2:
                    pe.wait_ge(exp_done, n - 1)
                ps = st_bank[n % 2]
                mm(ps[:, :], identb[:, :], maskT[c % 2][:, 0 if a is not None else 1, :], start=True, stop=False)
                if a is not None:
                    g = half * (G // KC) + pair
                    ins = mm(ps[:, :], ks_main[b][:, g, a, :], qs[c % 2][:, g, :], start=False, stop=True)
                else:
                    for k in range(2):
                        g = half * (G // KC) + 2 * pair + k
                        ins = mm(ps[:, :], ks_rest[b][:, g, :], qs[c % 2][:, g, :], start=False, stop=(k == 1))
                ins.then_inc(st_full, 1)

            def values(c, half, batch):
                b, hf = c // PER_B, 2 * c + half
                pe.wait_ge(exp_done, UN * hf + (4, 8, 10)[batch])
                if batch == 0:
                    if hf:
                        pe.wait_ge(att_made, hf)
                    if c % PER_B == 0 and half == 0:
                        pe.wait_ge(v_made, b + 1)
                for ps, main, rest in ((o_bank, v_main[b], v_rest[b]), (z_bank, None, None)):
                    for pair in range(G // KC):
                        rows_ = ps[32 * pair:32 * pair + 32, :]
                        if batch < 2:
                            h = half * HH + 2 * pair + batch
                            w = z_main[:, batch, :] if main is None else main[:, h, :]
                            ins = mm(rows_, w, pt[:, (UN * hf + 4 * batch + pair) % UN, :], start=(batch == 0), stop=False,
                                     skip_group_check=True)
                        else:
                            r = pair // 2
                            w = z_rest[:, pair % 2, :] if rest is None else rest[:, half * 2 + r, pair % 2, :]
                            ins = mm(rows_, w, pt[:, (UN * hf + 8 + r) % UN, :], start=False, stop=True, skip_group_check=True)
                ins.then_inc(pv_done, 1)

            def route(c):
                for t in range(TT):
                    pe.wait_ge(xn2_made, c * TT + t + 1)
                    ps = open_small(("nT", c, t))
                    for k in range(KC):
                        ins = tr(ps[:, k * P:(k + 1) * P], xn2[:, t % 2, k * P:(k + 1) * P], ident[:, :])
                    ins.then_inc(small_full, 1)
                pe.wait_ge(small_act, act_count(("nT", c, TT - 1)))
                ps = open_small(("logits", c))
                for t in range(TT):
                    for k in range(KC):
                        ins = mm(ps[:, t * E:(t + 1) * E], xn2T[:, t, k, :], rT[:, k, :], start=(k == 0), stop=(k == KC - 1))
                ins.then_inc(small_full, 1)

            def mix(c):
                late = {(0, 0): 5, (0, 1): 9, (0, 2): 11, (1, 0): 15, (1, 1): 19}
                for i in range(2 * UN):
                    scores(c, i)
                    if c < NCH - 1:
                        scan(c + 1, i)
                    if c and i == ROUTE_AT:
                        route(c - 1)
                    for (half, batch), at in late.items():
                        if at == i:
                            values(c, half, batch)
                values(c, 1, 2)
                if c < NCH - 1:
                    maxima(c + 1)

            def fold(c):
                pe.wait_ge(att_made, 2 * c + 2)
                if c == 0:
                    pe.wait_ge(l_small, 64)
                for t in range(TT):
                    ps = open_small(("fold", c, t))
                    for k in range(KC):
                        ins = mm(ps[:, 0:D], att[:, k, t * P:(t + 1) * P], wp_sb[:, k, :], start=(k == 0), stop=(k == KC - 1))
                    ins.then_inc(small_full, 1)

            def turn_small():
                pe.wait_ge(l_small, 64)
                ps = open_small(("rT",))
                for k in range(KC):
                    ins = tr(ps[:, k * E:(k + 1) * E], r_sb[:, k * P:(k + 1) * P], ident[0:E, 0:E])
                ins.then_inc(small_full, 1)
                ps = open_small(("b1T",))
                tr(ps[:, 0:E * FC], b1_sb[:, :], ident[0:E * FC, 0:E * FC]).then_inc(small_full, 1)

            def assign():
                pe.wait_ge(onehot_made, NCH)
                ps = open_small(("cum",))
                all_ = onehot[:, :, :].rearrange("p t e -> p (t e)")
                mm(ps[:, 0:T * E], trib[:, :], all_, start=True, stop=False, skip_group_check=True)
                for t in range(T - 1):
                    ins = mm(ps[:, (t + 1) * E:T * E], onesb[:, :], onehot[:, t, :].unsqueeze(1).to_broadcast([P, T - 1 - t, E]),
                             start=False, stop=(t == T - 2), skip_group_check=True)
                ins.then_inc(small_full, 1)
                pe.wait_ge(what_made, 1)
                ps = open_small(("slots",))
                for t in range(T):
                    ins = mm(ps[:, 0:3 * J], psel[:, t, :], what[:, t, :, :].rearrange("p c j -> p (c j)"),
                             start=(t == 0), stop=(t == T - 1))
                ins.then_inc(small_full, 1)

            for stage, c in STAGES:
                if stage == "proj":
                    proj(c)
                if stage == "keys":
                    keys(c)
                if stage == "mask":
                    turn_mask(c)
                if stage == "scan":
                    for i in range(TT * AU):
                        scan(c, i)
                    maxima(c)
                if stage == "small":
                    turn_small()
                if stage == "mix":
                    mix(c)
                if stage == "fold":
                    fold(c)
                if stage == "route":
                    route(c)
                if stage == "assign":
                    assign()

            def turn(e, s):
                for j in range(JT):
                    if j == 0:
                        pe.wait_ge(gn_made, e + 1)
                    pe.wait_ge(gT_made, JT * e + j + 1)
                    ps = t_bank[(JT * s + j) % 2]
                    for k in range(KC):
                        ins = tr(ps[:, k * P:(k + 1) * P], gn[:, s, j, k * P:(k + 1) * P], ident[:, :])
                    ins.then_inc(t_full, 1)

            def expert(it, s, last):
                e = it * 2 + s
                pe.wait_ge(l_w[s], it * 32 + 32)
                pe.wait_ge(gT_made, e * JT + (JT + 2))
                for f in range(FC):
                    pe.wait_ge(h_made, e * FC + (f + 1))
                    ps = h_bank[f % 4]
                    for k in range(KC):
                        ins = mm(ps[:, 0:CAP], w1_sb[s][:, k, f * P:(f + 1) * P], gT[:, s, k, :], start=(k == 0), stop=(k == KC - 1))
                    ins.then_inc(h_full, 1)
                if not last:
                    turn(e + 1, 1 - s)
                for j in range(JT):
                    if j == 0:
                        pe.wait_ge(h_made, e * FC + (FC + 4))
                    pe.wait_ge(y_read, e * JT + (j + 1))
                    ps = y_bank[(JT * s + j) % 2]
                    for f in range(FC):
                        ins = mm(ps[:, 0:D], hT[:, f, j * P:(j + 1) * P], w2_sb[s][:, f, :], start=(f == 0), stop=(f == FC - 1))
                    ins.then_inc(y_full, 1)

            turn(0, 0)
            with pe.Fori(0, E // 2 - 1) as it:
                expert(it, 0, False)
                expert(it, 1, False)
            expert(E // 2 - 1, 0, False)
            expert(E // 2 - 1, 1, True)

        @block.scalar
        def _(act):
            a = nc.scalar

            def full(name):
                act.wait_ge(small_full, job_at[name] + 1)
                return small(name)

            def proj(c):
                if c:
                    act.wait_ge(small_full, job_at[("q", c - 1, KC - 1)] + 1)
                for k in range(KC):
                    ps = full(("xT", c, k))
                    a.activation(xT[:, k, :], ps[:, :], ACT.Copy).then_inc(small_act, 1)
                for half in range(KC):
                    ps = full(("q", c, half))
                    if c and half == 0:
                        act.wait_ge(scan_full, TT * AU * c)
                        act.wait_ge(l_qs[(c - 1) % 2], 16 * 3 * G * ((c - 1) // 2 + 1))
                        act.wait_ge(qlo_made, KC * c)
                    a.activation(q_hi[:, half, :], ps[:, :], ACT.Copy).then_inc(qhi_made, 1)

            def keys(b):
                ps = full(("ctxT", b))
                if b:
                    act.wait_ge(small_full, job_at[("vr", b - 1)] + 1)
                a.activation(ctxT[:, :, 0:M], ps[:, 0:KC * MP].rearrange("p (k m) -> p k m", k=KC)[:, :, 0:M],
                             ACT.Copy).then_inc(small_act, 1)
                for half in range(KC):
                    ps = full(("k", b, half))
                    if b:
                        act.wait_ge(kdhi_made, KC * b)
                        act.wait_ge(klo_made, KC * b)
                    a.activation(k_hi[:, half, :], ps[:, 0:MP], ACT.Copy).then_inc(khi_made, 1)

            def turn_mask(c):
                ps = full(("maskT", c))
                if c >= 2:
                    act.wait_ge(st_full, 2 * UN * (c - 1))
                a.activation(maskT[c % 2][:, :, :].rearrange("p r n -> p (r n)"), ps[:, :].bitcast(BF16), ACT.Copy).then_inc(small_act, 1)

            def maxima(c):
                ps = full(("max", c))
                if c:
                    act.wait_ge(l_max[(c - 1) % 2], 16 * G * ((c - 1) // 2 + 1))
                a.activation(nmT[:, :], ps[0:H, :], ACT.Copy, scale=-1.0).then_inc(small_act, 1)

            def exponentials(c, i):
                n = 2 * UN * c + i
                hf, u = divmod(n, UN)
                act.wait_ge(st_full, n + 1)
                if hf:
                    act.wait_ge(pv_done, 3 * (hf - 1) + pv_batch_of(u) + 1)
                a.activation(pt[:, n % UN, :], st_bank[n % 2][:, :], ACT.Exp, scale=SCALE).then_inc(exp_done, 1)

            def route(c):
                for t in range(TT):
                    ps = full(("nT", c, t))
                    if c and t == 0:
                        act.wait_ge(small_full, job_at[("logits", c - 1)] + 1)
                    a.activation(xn2T[:, t, :, :].rearrange("p k n -> p (k n)"), ps[:, 0:D], ACT.Copy).then_inc(small_act, 1)
                act.wait_ge(below_made, c + 1)
                a.activation(lex[:, :, :], below[:, :, :], ACT.Exp).then_inc(lex_made, 1)

            for stage, c in STAGES:
                if stage == "proj":
                    proj(c)
                if stage == "keys":
                    keys(c)
                if stage == "mask":
                    turn_mask(c)
                if stage == "scan":
                    maxima(c)
                if stage == "small":
                    ps = full(("rT",))
                    a.activation(rT[:, :, :].rearrange("p k e -> p (k e)"), ps[:, 0:KC * E], ACT.Copy).then_inc(small_act, 1)
                    ps = full(("b1T",))
                    a.activation(b1T[:, :], ps[:, 0:E * FC], ACT.Copy).then_inc(small_act, 1)
                if stage == "mix":
                    for i in range(2 * UN):
                        exponentials(c, i)
                        if c and i == ROUTE_AT:
                            route(c - 1)
                    if c < NCH - 1:
                        maxima(c + 1)
                if stage == "route":
                    route(c)

            def turned(e, s):
                for j in range(JT):
                    act.wait_ge(t_full, JT * e + j + 1)
                    if j == 0 and not (isinstance(e, int) and e == 0):
                        act.wait_ge(h_full, e * FC)
                    a.activation(gT[:, s, :, j * P:(j + 1) * P], t_bank[(JT * s + j) % 2][:, 0:D].rearrange("p (k n) -> p k n", k=KC),
                                 ACT.Copy).then_inc(gT_made, 1)

            def expert(it, s, last):
                e = it * 2 + s
                for f in range(FC):
                    act.wait_ge(h_full, e * FC + (f + 1))
                    a.activation(hT[:, f, :], h_bank[f % 4][:, 0:CAP], ACT.Gelu, bias=b1T[:, bass.ds(e * FC + f, 1)]
                                 if not isinstance(e, int) else b1T[:, e * FC + f:e * FC + f + 1]).then_inc(h_made, 1)
                if not last:
                    turned(e + 1, 1 - s)

            act.sem_inc(h_made, 4)
            act.sem_inc(gT_made, 2)
            turned(0, 0)
            with act.Fori(0, E // 2 - 1) as it:
                expert(it, 0, False)
                expert(it, 1, False)
            expert(E // 2 - 1, 0, False)
            expert(E // 2 - 1, 1, True)

        @block.vector
        def _(dve):
            steps = Count(dve, dve_step)
            v = nc.vector

            def full(name):
                dve.wait_ge(small_full, job_at[name] + 1)
                return small(name)

            def proj(c):
                dve.wait_ge(l_x[c], 16)
                if c:
                    dve.wait_ge(xn_made, c)
                for t in range(TT):
                    steps.up(v.bn_stats(stats[:, t, :], xr[:, c * TT + t, 0:D]))
                steps.settle()
                for t in range(TT):
                    ins = v.bn_aggr(mv[:, t, :], stats[:, t, :])
                ins.then_inc(stats_made, 1)
                for half in range(KC):
                    ps = full(("q", c, half))
                    dve.wait_ge(qhi_made, KC * c + half + 1)
                    if c and half == 0:
                        dve.wait_ge(l_qs[(c - 1) % 2], 16 * 3 * G * ((c - 1) // 2 + 1))
                    v.tensor_tensor(q_lo[:, half, :], ps[:, :], q_hi[:, half, :].bitcast(F32), ALU.subtract).then_inc(qlo_made, 1)
                    dve.wait_ge(qlo_made, KC * c + half + 1)
                    dve.engine_nop().then_inc(small_dve, 1)

            def keys(b):
                for half in range(KC):
                    ps = full(("k", b, half))
                    dve.wait_ge(khi_made, KC * b + half + 1)
                    if b:
                        dve.wait_ge(kdlo_made, KC * b)
                    v.tensor_tensor(k_lo[:, half, :], ps[:, 0:MP], k_hi[:, half, :].bitcast(F32), ALU.subtract).then_inc(klo_made, 1)
                    dve.wait_ge(klo_made, KC * b + half + 1)
                    dve.engine_nop().then_inc(small_dve, 1)
                    if b:
                        dve.wait_ge(scan_full, TT * AU * PER_B * b)
                        dve.wait_ge(l_ks[b - 1], 16 * 6 * G)
                    else:
                        dve.wait_ge(consts_made, 1)
                    v.tensor_tensor(kd_hi[:, half], k_hi[:, half, :].bitcast(F32).unsqueeze(1).to_broadcast([P, HH, MP]),
                                    headsel[:, :].unsqueeze(2).to_broadcast([P, HH, MP]), ALU.mult).then_inc(kdhi_made, 1)
                ps = full(("v", b))
                to = v_main[b][:, :, :].rearrange("p (g a) c -> p g a c", a=2)
                src = ps[:, 0:D].rearrange("p (g a d) -> p g a d", a=2, d=DH)
                v.tensor_copy(to[:, :, 0, 0:DH], src[:, :, 0, :])
                v.tensor_copy(to[:, :, 1, DH:2 * DH], src[:, :, 1, :]).then_inc(small_dve, 1)
                ps = full(("vr", b))
                src = ps[0:RP, 0:D].rearrange("p (r i d) -> p r i d", i=4, d=DH)
                for i in range(4):
                    ins = v.tensor_copy(v_rest[b][32 * i:32 * i + 32, :, i // 2, DH * (i % 2):DH * (i % 2) + DH], src[:, :, i, :])
                    if i < 3:
                        steps.up(ins)
                ins.then_inc(small_dve, 1)
                dve.wait_ge(small_dve, dve_count(("vr", b)))
                dve.engine_nop().then_inc(v_made, 1)

            def selectors(b):
                for g in range(G):
                    steps.up(v.tensor_copy(ks_main[b][96:P, g, :, :], pairsel[96:P, :, :]))
                    c0 = 2 * RP * (g % 2)
                    steps.up(v.tensor_copy(ks_rest[b][96:P, g, c0:c0 + 2 * RP].rearrange("p (a m) -> p a m", a=2),
                                           pairsel[96:P, :, 0:RP]))
                steps.settle()
                dve.engine_nop().then_inc(sel_made, 1)

            def scan(c, i):
                t, u = divmod(i, AU)
                n = c * TT * AU + i
                dve.wait_ge(scan_full, n + 1)
                if i == 0 and c:
                    dve.wait_ge(max_made, c)
                if u < 4:
                    v.tensor_reduce(mx[:, t, 4 * u:4 * u + 4], a_bank[n % 2][:, :].rearrange("p (h m) -> p h m", h=4),
                                    AX_X, ALU.max).then_inc(scan_read, 1)
                else:
                    v.tensor_reduce(mxr[:, t, :], a_bank[n % 2][:, :].rearrange("p (h m) -> p h m", h=H),
                                    AX_X, ALU.max).then_inc(scan_read, 1)

            def maxima(c):
                dve.wait_ge(scan_read, TT * AU * (c + 1))
                if c:
                    dve.wait_ge(small_full, job_at[("max", c - 1)] + 1)
                v.tensor_tensor(mxx[:, :, :], mx[:, :, :], mxr[:, :, :], ALU.max).then_inc(max_made, 1)

            def divide(c, half):
                hf = 2 * c + half
                dve.wait_ge(pv_done, 3 * hf + 3)
                if half == 0 and c:
                    dve.wait_ge(small_full, job_at[("fold", c - 1, TT - 1)] + 1)
                if hf:
                    dve.wait_ge(att_made, hf)
                steps.up(v.reciprocal(rz[:, :], z_bank[:, :]))
                steps.settle()
                v.tensor_tensor(att[:, half, :], o_bank[:, :], rz[:, :], ALU.mult).then_inc(att_made, 1)

            def fold(c):
                dve.wait_ge(xb_made, c + 1)
                for t in range(TT):
                    ps = full(("fold", c, t))
                    tt = c * TT + t
                    v.tensor_tensor(xr[:, tt, 0:D], ps[:, 0:D], xr[:, tt, 0:D], ALU.add).then_inc(small_dve, 1)
                dve.wait_ge(small_dve, dve_count(("fold", c, TT - 1)))
                dve.wait_ge(stats_made, min(NCH, c + 3))
                for t in range(TT):
                    steps.up(v.bn_stats(stats[:, t, :], xr[:, c * TT + t, 0:D]))
                steps.settle()
                for t in range(TT):
                    ins = v.bn_aggr(xr[:, c * TT + t, D:D + 2], stats[:, t, :])
                ins.then_inc(x1_made, 1)

            def route(c):
                sl = slice(c * TT, (c + 1) * TT)
                dve.wait_ge(rstd_made, c + 1)
                for t in range(TT):
                    tt = c * TT + t
                    if tt >= 2:
                        last = ("nT", (tt - 2) // TT, (tt - 2) % TT)
                        dve.wait_ge(small_full, job_at[last] + 1)
                    v.tensor_scalar(xn2[:, t % 2, :], xr[:, tt, 0:D], xr[:, tt, D:D + 1], xr[:, tt, D + 1:D + 2],
                                    ALU.subtract, ALU.mult).then_inc(xn2_made, 1)
                ps = full(("logits", c))
                if c:
                    dve.wait_ge(gate_made, c)
                    dve.wait_ge(onehot_made, c)
                v.tensor_copy(lg[:, :, :].rearrange("p t e -> p (t e)"), ps[:, 0:TT * E]).then_inc(small_dve, 1)
                dve.wait_ge(small_dve, dve_count(("logits", c)))
                steps.up(v.tensor_reduce(lmax[:, :], lg[:, :, :], AX_X, ALU.max))
                steps.settle()
                v.tensor_tensor(below[:, :, :], lg[:, :, :], lmax[:, :].unsqueeze(2).to_broadcast([P, TT, E]),
                                ALU.subtract).then_inc(below_made, 1)
                dve.wait_ge(below_made, c + 1)
                if c == 0:
                    dve.wait_ge(consts_made, 2)
                steps.up(v.scalar_tensor_tensor(out=rank[:, :, :], in0=below[:, :, :], scalar=0.0, in1=first[:, :, :],
                                                op0=ALU.is_ge, op1=ALU.mult))
                steps.settle()
                steps.up(v.tensor_reduce(best[:, :], rank[:, :, :], AX_X, ALU.max))
                steps.settle()
                v.tensor_tensor(onehot[:, sl, :], rank[:, :, :], best[:, :].unsqueeze(2).to_broadcast([P, TT, E]),
                                ALU.is_equal).then_inc(onehot_made, 1)
                dve.wait_ge(lex_made, c + 1)
                steps.up(v.tensor_reduce(lsum[:, :], lex[:, :, :], AX_X, ALU.add))
                steps.settle()
                v.reciprocal(xr[:, sl, D + 2], lsum[:, :]).then_inc(gate_made, 1)

            def assign():
                ps = full(("cum",))
                dve.wait_ge(onehot_made, NCH)
                v.tensor_tensor(cum[:, :, :], ps[:, 0:T * E].rearrange("p (t e) -> p t e", e=E), onehot[:, :, :],
                                ALU.mult).then_inc(small_dve, 1)
                steps.up(v.tensor_tensor(ebs[:, :, :], ebase[:, :, :], onehot[:, :, :], ALU.mult))
                dve.wait_ge(small_dve, dve_count(("cum",)))
                steps.settle()
                steps.up(v.tensor_reduce(pos[:, :], cum[:, :, :], AX_X, ALU.add))
                steps.up(v.tensor_reduce(jslot[:, :], ebs[:, :, :], AX_X, ALU.add))
                steps.settle()
                for m in range(1, JT + 1):
                    steps.up(v.tensor_scalar(over[:, :, m - 1], pos[:, :], float(m * P), None, ALU.is_ge))
                steps.settle()
                for m in range(1, JT + 1):
                    steps.up(v.tensor_tensor(jslot[:, :], jslot[:, :], over[:, :, m - 1], ALU.add))
                    steps.up(v.scalar_tensor_tensor(out=pos[:, :], in0=over[:, :, m - 1], scalar=-float(P) if m < JT else float(NTOK),
                                                    in1=pos[:, :], op0=ALU.mult, op1=ALU.add))
                    steps.settle()
                steps.up(v.tensor_tensor(psel[:, :, :], lane[:, :].unsqueeze(1).to_broadcast([P, T, P]),
                                         pos[:, :].unsqueeze(2).to_broadcast([P, T, P]), ALU.is_equal))
                steps.up(v.tensor_tensor(jsel[:, :, :], lane[:, 0:J].unsqueeze(1).to_broadcast([P, T, J]),
                                         jslot[:, :].unsqueeze(2).to_broadcast([P, T, J]), ALU.is_equal))
                steps.settle()
                steps.up(v.tensor_scalar(what[:, :, 0, :], jsel[:, :, :], part[:, 0:1], None, ALU.mult))
                steps.up(v.tensor_tensor(what[:, :, 1, :], jsel[:, :, :], tileno[:, :, :], ALU.mult))
                steps.up(v.tensor_copy(what[:, :, 2, :], jsel[:, :, :]))
                steps.settle()
                dve.engine_nop().then_inc(what_made, 1)
                ps = full(("slots",))
                v.tensor_copy(slots[:, :, :].rearrange("p c j -> p (c j)"), ps[:, 0:3 * J]).then_inc(small_dve, 1)
                dve.wait_ge(small_dve, dve_count(("slots",)))
                steps.up(v.scalar_tensor_tensor(out=tok[:, :], in0=slots[:, 1, :], scalar=float(P), in1=slots[:, 0, :],
                                                op0=ALU.mult, op1=ALU.add))
                steps.settle()
                steps.up(v.scalar_tensor_tensor(out=tokfar[:, :], in0=slots[:, 2, :], scalar=-FAR, in1=tok[:, :],
                                                op0=ALU.mult, op1=ALU.add))
                steps.settle()
                steps.up(v.tensor_scalar(tok_store[:, :], tokfar[:, :], FAR, None, ALU.add))
                steps.up(v.tensor_scalar(tok_load[:, :], tokfar[:, :], FAR, float(NTOK - 1), ALU.add, ALU.min))
                steps.settle()
                dve.engine_nop().then_inc(tok_made, 1)

            for stage, c in STAGES:
                if stage == "proj":
                    proj(c)
                if stage == "keys":
                    keys(c)
                    if c:
                        selectors(c)
                if stage == "scan":
                    for i in range(TT * AU):
                        scan(c, i)
                    maxima(c)
                    selectors(0)
                if stage == "mix":
                    for i in range(2 * UN):
                        if c < NCH - 1:
                            scan(c + 1, i)
                        if c and i == ROUTE_AT:
                            route(c - 1)
                        if i == 11:
                            divide(c, 0)
                    if c < NCH - 1:
                        maxima(c + 1)
                    divide(c, 1)
                if stage == "fold":
                    fold(c)
                if stage == "route":
                    route(c)
                if stage == "assign":
                    assign()

            def at(t, e, j):
                return t[:, bass.ds(e * JT + j, 1), :] if not isinstance(e, int) else t[:, e * JT + j:e * JT + j + 1, :]

            def normalise(e, s, uses):
                for j in range(JT):
                    if j == 0:
                        dve.wait_ge(l_gather[s], uses * (16 * JT))
                        if not (isinstance(e, int) and e == 0):
                            dve.wait_ge(t_full, e * JT)
                    r = at(xg, e, j)
                    ins = v.tensor_scalar(gn[:, s, j, :], r[:, 0, 0:D], r[:, 0, D:D + 1], r[:, 0, D + 1:D + 2],
                                          ALU.subtract, ALU.mult)
                ins.then_inc(gn_made, 1)

            def expert(it, s, last):
                e = it * 2 + s
                if not last:
                    normalise(e + 1, 1 - s, it + (1 + s))
                for j in range(JT):
                    dve.wait_ge(y_full, e * JT + (j + 1))
                    dve.wait_ge(y_made, e * JT + (j + 1))
                    b2_e = b2_sb[:, bass.ds(e, 1), :] if not isinstance(e, int) else b2_sb[:, e:e + 1, :]
                    v.tensor_tensor(y1[:, j, :], y_bank[(JT * s + j) % 2][:, 0:D], b2_e[:, 0, :], ALU.add).then_inc(y_read, 1)
                    dve.wait_ge(y_read, e * JT + (j + 3))
                    r = at(xg, e, j)
                    v.scalar_tensor_tensor(out=r[:, 0, 0:D], in0=y1[:, j, :], scalar=r[:, 0, D + 2:D + 3], in1=r[:, 0, 0:D],
                                           op0=ALU.mult, op1=ALU.add).then_inc(y_made, 1)

            dve.sem_inc(y_read, 2)
            dve.sem_inc(y_made, JT)
            normalise(0, 0, 1)
            dve.wait_ge(l_b2, 16)
            with dve.Fori(0, E // 2 - 1) as it:
                expert(it, 0, False)
                expert(it, 1, False)
            expert(E // 2 - 1, 0, False)
            expert(E // 2 - 1, 1, True)


_INS = ['x', 'ctx_1024', 'mask_BxSxS2_bk0', 'L0_xattn_Wq', 'L0_xattn_Wkv', 'L0_xattn_Wproj', 'L0_xattn_bproj',
        'L0_ffn_router_w', 'L0_ffn_w1', 'L0_ffn_b1', 'L0_ffn_w2', 'L0_ffn_b2']
_OUTS = [((2, 1024, 256), 'float32')]


def kernel(**inputs):
    import numpy as _np
    import concourse.bacc as _bacc
    from concourse import mybir as _mybir
    from concourse.bass_utils import run_bass_kernel_spmd as _run

    nc = _bacc.Bacc("TRN2", target_bir_lowering=False, num_devices=1)
    arrays, args = {}, []
    for name in _INS:
        a = _np.ascontiguousarray(inputs[name])
        arrays[f"in_{name}_dram"] = a
        args.append(nc.dram_tensor(f"in_{name}_dram", a.shape, _mybir.dt.from_np(a.dtype), kind="ExternalInput").ap())
    for i, (shape, dtype) in enumerate(_OUTS):
        dt = _mybir.dt.from_np(_np.dtype(dtype))
        args.append(nc.dram_tensor(f"out_{i}_dram", shape, dt, kind="ExternalOutput").ap())
    build(nc, *args)
    r = _run(nc, [arrays], core_ids=[0])
    return r.results[0]["out_0_dram"]
```

```python
from contextlib import ExitStack

import concourse.bass as bass
from concourse import mybir

F32 = mybir.dt.float32
F32R = mybir.dt.float32r
BF16 = mybir.dt.bfloat16
I32 = mybir.dt.int32
U8 = mybir.dt.uint8
ALU = mybir.AluOpType
ACT = mybir.ActivationFunctionType
AX_X = mybir.AxisListType.X

P = 128
NEG = -1.0e30
EPS = 1e-5
HEADS = 16

STAGES = [
    ("norm", 0), ("proj", 0), ("keys", 0), ("mask", 0), ("norm", 1), ("scan", 0), ("proj", 1), ("mask", 1), ("small", 0),
    ("norm", 2), ("mix", 0), ("keys", 1), ("proj", 2), ("mask", 2), ("norm", 3), ("fold", 0),
    ("mix", 1), ("proj", 3), ("mask", 3), ("fold", 1),
    ("mix", 2), ("fold", 2), ("mix", 3), ("split", 0), ("fold", 3), ("route", 3), ("assign", 0),
]
ROUTE_AT = 8


class Count:

    def __init__(self, engine, semaphore):
        self.engine, self.semaphore, self.n = engine, semaphore, 0

    def up(self, instruction):
        instruction.then_inc(self.semaphore, 1)
        self.n += 1

    def settle(self):
        self.engine.wait_ge(self.semaphore, self.n)


def small_jobs(tiles):
    jobs = []
    for stage, c in STAGES:
        if stage == "proj":
            jobs += [(("xT", c, k), "act") for k in range(2)] + [(("q", c, k), "dve") for k in range(2)]
        if stage == "keys":
            jobs += [(("ctxT", c), "act"), (("k", c, 0), "dve"), (("k", c, 1), "dve"), (("v", c), "dve"), (("vr", c), "dve")]
        if stage == "mask":
            jobs += [(("maskT", c), "act")]
        if stage == "scan":
            jobs += [(("max", c), "act")]
        if stage == "small":
            jobs += [(("rT",), "act"), (("b1T",), "act")]
        if stage == "mix":
            if c:
                jobs += route_jobs(c - 1, tiles)
            if c < 3:
                jobs += [(("max", c + 1), "act")]
        if stage == "fold":
            jobs += [(("fold", c, t), "dve") for t in range(tiles)]
        if stage == "route":
            jobs += route_jobs(c, tiles)
        if stage == "assign":
            jobs += [(("cum",), "dve"), (("slots",), "dve")]
    return jobs


def route_jobs(c, tiles):
    return [(("nT", c, t), "act") for t in range(tiles)] + [(("logits", c), "dve")]


def build(nc, x, ctx, mask, wq, wkv, wproj, bproj, router, w1, b1, w2, b2, out):
    B, N, D = x.shape
    M = ctx.shape[1]
    H = HEADS
    DH = D // H
    E, _, F = w1.shape
    KC = D // P
    HH = H // KC
    G = H // 2
    CH = 512
    NCH = B * N // CH
    PER_B = N // CH
    TT = CH // P
    T = B * N // P
    MR = M - P
    RP = 32
    MP = P + RP
    UN = 10
    AU = 5
    CAP = max(-(-3 * B * N // (2 * E)), 1)
    JT = CAP // P
    J = E * JT
    TURNS = ((0, 1), (2,))
    FC = F // P
    ROW = D + 4
    NTOK = B * N
    SCALE = float(DH) ** -0.5
    assert JT == 3 and D == 256 and NCH == 4 and 0 < MR < RP and CAP % P == 0 and E % 2 == 0 and H * DH == D
    KS_DMAS = 16 * 3 * 2 * 3
    QS_DMAS = 16 * 3
    FAR = float(2 * NTOK)

    x_t = x.rearrange("b (t p) d -> p (b t) d", p=P)
    mask_t = mask.rearrange("b (t p) m -> p (b t) m", p=P)
    out_rows = out.rearrange("b n d -> (b n) d")
    out_t = out.rearrange("b (t p) d -> p (b t) d", p=P)
    rows = nc.dram_tensor("rows", [NTOK, ROW], F32, kind="Internal").ap()
    rows_t = rows.rearrange("(t p) d -> p t d", p=P)
    q_dram = nc.dram_tensor("q_dram", [2, 2, D, CH], F32, kind="Internal").ap()
    m_dram = nc.dram_tensor("m_dram", [2, H, CH], F32, kind="Internal").ap()
    k_dram = nc.dram_tensor("k_dram", [B, 2, D, MP], F32, kind="Internal").ap()

    jobs = small_jobs(TT)
    job_at = {name: n for n, (name, _) in enumerate(jobs)}

    with ExitStack() as stack:
        def make(scope):
            def sb(name, shape, dt=F32):
                return scope.enter_context(nc.sbuf_tensor(name, shape, dt))
            return sb

        sb = make(stack)

        def sem(name):
            return stack.enter_context(nc.semaphore(name))

        bank = [stack.enter_context(nc.psum_tensor(f"bank{i}", [P, 512], F32)) for i in range(8)]
        a_bank, st_bank, o_bank, z_bank, small_bank = bank[0:2], bank[2:4], bank[4], bank[5], bank[6:8]
        t_bank, y_bank, h_bank = bank[0:2], bank[2:4], bank[4:8]

        ident = sb("ident", [P, P])
        xr = sb("xr", [P, T, ROW])
        b1T = sb("b1T", [P, E * FC])
        tok = sb("tok", [P, J])
        tokfar = sb("tokfar", [P, J])
        tok_store = sb("tok_store", [P, J], I32)
        tok_load = sb("tok_load", [P, J], I32)
        warm = sb("warm", [P, 1])
        more = sb("more", [1, 1], I32)
        w1_sb = [sb("w1_sb0", [P, KC, F])]
        w2_sb = [sb("w2_sb0", [P, FC, D])]

        attention = ExitStack()
        sa = make(attention)
        qs = [sa(f"qs{i}", [P, G, CH], F32R) for i in range(2)]
        ks_main = [sa(f"ks_main{b}", [P, G, 2, P], F32R) for b in range(B)]
        ks_rest = [sa(f"ks_rest{b}", [P, G, P], F32R) for b in range(B)]
        kd_hi = sa("kd_hi", [P, KC, HH, MP], F32R)
        pt = sa("pt", [P, UN, CH])
        identb = sa("identb", [P, P], BF16)
        onesb = sa("onesb", [P, P], BF16)
        trib = sa("trib", [P, P], BF16)
        wq_sb = sa("wq_sb", [P, KC, D])
        wkv_sb = sa("wkv_sb", [P, KC, 2 * D])
        wp_sb = sa("wp_sb", [P, KC, D])
        bp_sb = sa("bp_sb", [P, D])
        r_sb = sa("r_sb", [E, D])
        rT = sa("rT", [P, KC, E])
        b1_sb = sa("b1_sb", [E * FC, P])
        headsel = sa("headsel", [P, HH])
        pairsel = sa("pairsel", [P, 2, P])
        z_main = sa("z_main", [P, 2, RP])
        z_rest = sa("z_rest", [P, 2, RP])
        neghalf = sa("neghalf", [P, TT])
        lane = sa("lane", [P, P])
        part = sa("part", [P, 1])
        tileno = sa("tileno", [P, T, J])
        first = sa("first", [P, TT, E])
        ebase = sa("ebase", [P, T, E])

        ctx_sb = sa("ctx_sb", [P, B, 2, D])
        ctxT = sa("ctxT", [P, KC, MP])
        k_hi = sa("k_hi", [P, KC, MP], F32R)
        k_lo = sa("k_lo", [P, KC, MP], F32R)
        v_main = [sa(f"v_main{b}", [P, H, RP]) for b in range(B)]
        v_rest = [sa(f"v_rest{b}", [P, H // 4, 2, RP]) for b in range(B)]
        mask_sb = sa("mask_sb", [P, T, M], U8)
        negm = sa("negm", [P, T, P + 4 * RP], BF16)
        maskT = [sa(f"maskT{i}", [P, 2, CH], BF16) for i in range(2)]
        stats = sa("stats", [P, TT, 6])
        mv = sa("mv", [P, TT, 2])
        var = sa("var", [P, TT])
        rstd = sa("rstd", [P, TT])
        var2 = sa("var2", [P, TT])
        xn = sa("xn", [P, TT, D])
        xT = sa("xT", [P, KC, CH])
        q_hi = sa("q_hi", [P, KC, CH], F32R)
        q_lo = sa("q_lo", [P, KC, CH], F32R)
        mx = sa("mx", [P, TT, H])
        mxr = sa("mxr", [P, TT, H])
        mxx = sa("mxx", [P, TT, H])
        nmT = sa("nmT", [H, CH], F32R)
        rz = sa("rz", [P, CH])
        att = sa("att", [P, KC, CH])
        xn2 = sa("xn2", [P, 2, D])
        xn2T = sa("xn2T", [P, TT, KC, P])

        lg = sa("lg", [P, TT, E])
        lmax = sa("lmax", [P, TT])
        below = sa("below", [P, TT, E])
        lex = sa("lex", [P, TT, E])
        lsum = sa("lsum", [P, TT])
        rank = sa("rank", [P, TT, E])
        best = sa("best", [P, TT])
        onehot = sa("onehot", [P, T, E], BF16)
        cum = sa("cum", [P, T, E])
        ebs = sa("ebs", [P, T, E])
        past = sa("past", [1, 2, E])
        bits = sa("bits", [1, 2, E])
        code = sa("code", [1, 1])
        pos = sa("pos", [P, T])
        jslot = sa("jslot", [P, T])
        over = sa("over", [P, T, JT])
        pslot = sa("pslot", [P, T])
        spare = negm[:, :, :].rearrange("p t m -> p (t m)")
        psel = spare[:, 0:T * P].rearrange("p (t m) -> p t m", t=T)
        what = spare[:, T * P:T * (P + 3 * J)].rearrange("p (t c j) -> p t c j", t=T, c=3)
        jsel = spare[:, T * (P + 3 * J):T * (P + 4 * J)].rearrange("p (t j) -> p t j", t=T)
        slots = sa("slots", [P, 3, J])
        attention.close()

        w1_hi, w1_lo, w2_hi, w2_lo = [], [], [], []
        for s_ in range(2):
            w1_hi.append(sb(f"w1_hi{s_}", [P, KC, F], F32R))
            w1_lo.append(sb(f"w1_lo{s_}", [P, KC, F], F32R))
            w2_hi.append(sb(f"w2_hi{s_}", [P, FC, D], F32R))
            w2_lo.append(sb(f"w2_lo{s_}", [P, FC, D], F32R))
            if s_ == 0:
                w1_sb.append(sb("w1_sb1", [P, KC, F]))
                w2_sb.append(sb("w2_sb1", [P, FC, D]))
        xg = sb("xg", [P, J, ROW])
        b2_sb = sb("b2_sb", [P, E, D])
        gn = sb("gn", [P, 2, JT, D])
        gT_hi = sb("gT_hi", [P, 2, KC, CAP], F32R)
        gT_lo = sb("gT_lo", [P, 2, KC, CAP], F32R)
        h32 = sb("h32", [P, 2, CAP])
        h_hi = sb("h_hi", [P, FC, CAP], F32R)
        h_lo = sb("h_lo", [P, FC, CAP], F32R)
        y1 = sb("y1", [P, JT, D])

        l_x = [sem(f"l_x{c}") for c in range(NCH)]
        l_ctx, l_wq, l_mask, l_small = sem("l_ctx"), sem("l_wq"), sem("l_mask"), sem("l_small")
        l_ks = [sem(f"l_ks{b}") for b in range(B)]
        l_qs = [sem(f"l_qs{i}") for i in range(2)]
        l_max = [sem(f"l_max{i}") for i in range(2)]
        l_qd, l_kd, l_md = sem("l_qd"), sem("l_kd"), sem("l_md")
        l_rows, l_out, l_b2 = sem("l_rows"), sem("l_out"), sem("l_b2")
        l_w1 = [sem(f"l_w1_{s}") for s in range(2)]
        l_w2 = [sem(f"l_w2_{s}") for s in range(2)]
        l_gather = [sem(f"l_gather{s}") for s in range(2)]
        l_store = [sem(f"l_store{j}") for j in range(JT)]
        pool_step, dve_step = sem("pool_step"), sem("dve_step")
        consts_made, mask_made, xn_made, rstd_made, xb_made, zeros_made = (
            sem("consts_made"), sem("mask_made"), sem("xn_made"), sem("rstd_made"), sem("xb_made"), sem("zeros_made"))
        small_full, small_act, small_dve = sem("small_full"), sem("small_act"), sem("small_dve")
        scan_full, scan_read = sem("scan_full"), sem("scan_read")
        st_full, exp_done, pv_done, att_made = sem("st_full"), sem("exp_done"), sem("pv_done"), sem("att_made")
        stats_made, qhi_made, qlo_made, khi_made, kdhi_made, klo_made = (
            sem("stats_made"), sem("qhi_made"), sem("qlo_made"), sem("khi_made"), sem("kdhi_made"), sem("klo_made"))
        v_made, sel_made, max_made, x1_made, xn2_made = sem("v_made"), sem("sel_made"), sem("max_made"), sem("x1_made"), sem("xn2_made")
        below_made, lex_made, gate_made, onehot_made, what_made, tok_made = (
            sem("below_made"), sem("lex_made"), sem("gate_made"), sem("onehot_made"), sem("what_made"), sem("tok_made"))
        gn_made, t_full, gT_made = sem("gn_made"), sem("t_full"), sem("gT_made")
        w1hi_made, w1lo_made, w2hi_made, w2lo_made, hlo_made, gTlo_made = (
            sem("w1hi_made"), sem("w1lo_made"), sem("w2hi_made"), sem("w2lo_made"), sem("hlo_made"), sem("gTlo_made"))
        h_full, h_made, y_full, y_read, y_made = sem("h_full"), sem("h_made"), sem("y_full"), sem("y_read"), sem("y_made")

        def unit_of(u):
            return (u // 4, u % 4) if u < 8 else (None, u - 8)

        def pv_batch_of(u):
            return min(u // 4, 2)

        def act_count(name):
            return sum(who == "act" for _, who in jobs[:job_at[name] + 1])

        def dve_count(name):
            return sum(who == "dve" for _, who in jobs[:job_at[name] + 1])

        def small(name):
            return small_bank[job_at[name] % 2]

        def turned_aps(t, s, part_, js):
            return (t[:, s, :, js[0] * P:(js[-1] + 1) * P].rearrange("p k (j n) -> p j k n", n=P),
                    t_bank[part_][:, 0:len(js) * D].rearrange("p (j k n) -> p j k n", k=KC, n=P))

        block = stack.enter_context(nc.Block())

        @block.sync
        def _(sp):
            def load_x(c):
                sp.dma_start(xr[:, c * TT:(c + 1) * TT, 0:D], x_t[:, c * TT:(c + 1) * TT, :]).then_inc(l_x[c], 16)

            def keys(b):
                for part_, (k_, made) in enumerate(((k_hi, khi_made), (k_lo, klo_made))):
                    sp.wait_ge(made, KC * (b + 1))
                    sp.dma_start(k_dram[b, part_].rearrange("(k p) m -> p k m", p=P), k_[:, :, :].bitcast(F32)).then_inc(l_kd, 16)
                if b == 0:
                    sp.wait_ge(zeros_made, 1)
                sp.wait_ge(l_kd, 32 * (b + 1))
                for blk, part_ in enumerate((0, 0, 1)):
                    src = k_dram[b, part_].rearrange("(g a r) m -> a r g m", a=2, r=DH)
                    for a in range(2):
                        to = slice(32 * blk + DH * a, 32 * blk + DH * (a + 1))
                        sp.dma_start(ks_main[b][to, :, a, :].bitcast(F32), src[a, :, :, 0:P]).then_inc(l_ks[b], 16)
                        for odd in range(2):
                            c0 = 2 * RP * odd + RP * a
                            sp.dma_start(ks_rest[b][to, odd:G:2, c0:c0 + RP].bitcast(F32),
                                         src[a, :, odd:G:2, P:MP]).then_inc(l_ks[b], 16)

            def proj(c):
                sp.wait_ge(qhi_made, KC * (c + 1))
                if c >= 2:
                    sp.wait_ge(l_qs[c % 2], QS_DMAS * (c // 2))
                sp.dma_start(q_dram[c % 2, 0].rearrange("(k p) n -> p k n", p=P), q_hi[:, :, :].bitcast(F32)).then_inc(l_qd, 16)
                sp.wait_ge(qlo_made, KC * (c + 1))
                sp.dma_start(q_dram[c % 2, 1].rearrange("(k p) n -> p k n", p=P), q_lo[:, :, :].bitcast(F32)).then_inc(l_qd, 16)
                if c >= 2:
                    sp.wait_ge(st_full, 2 * UN * (c - 1))
                sp.wait_ge(l_qd, 32 * (c + 1))
                for blk, part_ in enumerate((0, 1, 0)):
                    sp.dma_start(qs[c % 2][32 * blk:32 * blk + 32, :, :].bitcast(F32),
                                 q_dram[c % 2, part_].rearrange("(g r) n -> r g n", r=32)).then_inc(l_qs[c % 2], 16)

            def maxima(c):
                sp.wait_ge(small_act, act_count(("max", c)))
                if c == 0:
                    sp.wait_ge(consts_made, 2)
                if c >= 2:
                    sp.wait_ge(st_full, 2 * UN * (c - 1))
                if c >= 2:
                    sp.wait_ge(l_max[c % 2], 16 * (c // 2))
                sp.dma_start(m_dram[c % 2], nmT[:, :].bitcast(F32)).then_inc(l_md, 16)
                sp.wait_ge(l_md, 16 * (c + 1))
                sp.dma_start(qs[c % 2][96:98, :, :].bitcast(F32), m_dram[c % 2].rearrange("(g a) n -> a g n", a=2)).then_inc(l_max[c % 2], 16)

            def store_rows(c):
                sp.wait_ge(gate_made, c + 1)
                sl = slice(c * TT, (c + 1) * TT)
                sp.dma_start(rows_t[:, sl, :], xr[:, sl, :]).then_inc(l_rows, 16)
                sp.dma_start(out_t[:, sl, :], xr[:, sl, 0:D]).then_inc(l_out, 16)

            def load_w1(e, s):
                e_ = bass.ds(e, 1) if not isinstance(e, int) else slice(e, e + 1)
                sp.dma_start(w1_sb[s][:, :, :], w1[e_].rearrange("e (k p) f -> p (e k) f", p=P)).then_inc(l_w1[s], 16)

            def load_w2(e, s):
                e_ = bass.ds(e, 1) if not isinstance(e, int) else slice(e, e + 1)
                sp.dma_start(w2_sb[s][:, :, :], w2[e_].rearrange("e (k p) d -> p (e k) d", p=P)).then_inc(l_w2[s], 16)

            load_x(0)
            sp.dma_start(wq_sb[:, :, :], wq.rearrange("(k p) d -> p k d", p=P)).then_inc(l_wq, 16)
            sp.dma_start(ctx_sb[:, :, 0, :], ctx[:, 0:P, :].rearrange("b p d -> p b d")).then_inc(l_ctx, 16)
            sp.dma_start(ctx_sb[0:MR, :, 1, :], ctx[:, P:M, :].rearrange("b p d -> p b d")).then_inc(l_ctx, 16)
            sp.dma_start(wkv_sb[:, :, :], wkv.rearrange("(k p) d -> p k d", p=P)).then_inc(l_ctx, 16)
            sp.dma_start(mask_sb[:, :, :], mask_t).then_inc(l_mask, 16)
            load_x(1)
            sp.dma_start(wp_sb[:, :, :], wproj.rearrange("(k p) d -> p k d", p=P)).then_inc(l_small, 16)
            sp.dma_start(bp_sb[:, :], bproj.rearrange("(a d) -> a d", a=1).to_broadcast([P, D])).then_inc(l_small, 16)
            sp.dma_start(r_sb[:, :], router).then_inc(l_small, 16)
            sp.dma_start(b1_sb[:, :], b1.rearrange("e (f p) -> (e f) p", p=P)).then_inc(l_small, 16)
            load_x(2)
            load_x(3)
            load_w1(0, 0)
            load_w2(0, 0)
            for stage, c in STAGES:
                if stage == "keys":
                    keys(c)
                if stage == "proj":
                    proj(c)
                if stage == "scan":
                    maxima(c)
                if stage == "mix":
                    if c:
                        store_rows(c - 1)
                    if c < NCH - 1:
                        maxima(c + 1)
                if stage == "split":
                    sp.wait_ge(st_full, 2 * UN * NCH)
                    sp.wait_ge(pv_done, 3 * 2 * NCH)
                    load_w1(1, 1)
                    load_w2(1, 1)
                if stage == "route":
                    store_rows(c)
            sp.wait_ge(tok_made, 1)
            sp.wait_ge(l_gather[0], 16 * JT)
            sp.dma_start(b2_sb[:, :, :], b2.rearrange("(a e) d -> a e d", a=1).to_broadcast([P, E, D])).then_inc(l_b2, 16)
            with sp.Fori(1, E // 2) as it:
                for s in range(2):
                    sp.wait_ge(w1lo_made, (it * 2 + (s - 1)) * 4)
                    load_w1(it * 2 + s, s)
                    sp.wait_ge(w2lo_made, it * 2 + (s - 1))
                    load_w2(it * 2 + s, s)

        @block.gpsimd
        def _(pool):
            steps = Count(pool, pool_step)
            p = nc.gpsimd

            def make_consts():
                steps.up(p.memset(ident[:, :], 0.0))
                steps.up(p.memset(neghalf[:, :], -0.5))
                steps.settle()
                steps.up(p.affine_select(out=ident[:, :], in_=ident[:, :], compare_op=ALU.not_equal, fill=1.0,
                                         base=0, pattern=[[-1, P]], channel_multiplier=1))
                steps.up(p.memset(ctxT[:, :, M:MP], 0.0))
                steps.up(p.memset(headsel[:, :], 1.0))
                steps.settle()
                steps.up(p.affine_select(out=headsel[:, :], in_=headsel[:, :], compare_op=ALU.is_ge, fill=0.0,
                                         base=0, pattern=[[-DH, HH]], channel_multiplier=1))
                steps.settle()
                steps.up(p.affine_select(out=headsel[:, :], in_=headsel[:, :], compare_op=ALU.is_ge, fill=0.0,
                                         base=DH - 1, pattern=[[DH, HH]], channel_multiplier=-1))
                steps.up(p.tensor_copy(identb[:, :], ident[:, :]))
                steps.settle()
                p.memset(var2[:, :], 0.0).then_inc(consts_made, 1)

            def make_more_consts():
                steps.up(p.memset(negm[:, :, P:], 0.0))
                steps.settle()
                make_mask(0)
                steps.up(p.memset(onesb[:, :], 1.0))
                steps.up(p.memset(pairsel[:, :, :], 1.0))
                steps.settle()
                steps.up(p.affine_select(out=trib[:, :], in_=onesb[:, :], compare_op=ALU.is_ge, fill=0.0,
                                         base=-1, pattern=[[1, P]], channel_multiplier=-1))
                steps.up(p.affine_select(out=pairsel[:, :, :], in_=pairsel[:, :, :], compare_op=ALU.is_equal, fill=0.0,
                                         base=-96, pattern=[[-1, 2], [0, P]], channel_multiplier=1))
                steps.settle()
                for t in (z_main, z_rest):
                    steps.up(p.memset(t[:, :, :], 0.0))
                for i in range(2):
                    steps.settle()
                    steps.up(p.memset(qs[i][96:P, :, :].bitcast(F32), 0.0))
                steps.settle()
                for a in range(2):
                    steps.up(p.memset(z_main[:, a, DH * a:DH * a + DH], 1.0))
                for i in range(4):
                    steps.settle()
                    steps.up(p.memset(z_rest[32 * i:32 * i + MR + 1, i // 2, DH * (i % 2):DH * (i % 2) + DH], 1.0))
                steps.settle()
                p.memset(var2[:, :], 0.0).then_inc(consts_made, 1)

            def make_late_consts():
                steps.up(p.iota(lane[:, :], pattern=[[1, P]], base=0, channel_multiplier=0,
                                allow_small_or_imprecise_dtypes=True))
                steps.up(p.iota(part[:, :], pattern=[[0, 1]], base=0, channel_multiplier=1,
                                allow_small_or_imprecise_dtypes=True))
                steps.up(p.iota(tileno[:, :, :], pattern=[[1, T], [0, J]], base=0, channel_multiplier=0,
                                allow_small_or_imprecise_dtypes=True))
                steps.up(p.iota(first[:, :, :], pattern=[[0, TT], [-1, E]], base=E, channel_multiplier=0,
                                allow_small_or_imprecise_dtypes=True))
                steps.up(p.iota(ebase[:, :, :], pattern=[[0, T], [JT, E]], base=0, channel_multiplier=0,
                                allow_small_or_imprecise_dtypes=True))
                for e in range(E):
                    steps.up(p.memset(bits[:, :, e:e + 1], float(4 ** e)))
                steps.up(p.memset(xr[:, :, D + 2:ROW], 0.0))
                steps.settle()
                p.memset(var2[:, :], 0.0).then_inc(consts_made, 1)

            def make_mask(c):
                sl = slice(c * TT, (c + 1) * TT)
                if c == 0:
                    pool.wait_ge(l_mask, 16)
                p.tensor_scalar(negm[:, sl, 0:P], mask_sb[:, sl, 0:P], NEG, None, ALU.mult)
                for i in range(4):
                    ins = p.tensor_scalar(negm[:, sl, P + RP * i:P + RP * i + MR], mask_sb[:, sl, P:M], NEG, None, ALU.mult)
                ins.then_inc(mask_made, 1)

            def norm(c):
                pool.wait_ge(stats_made, c + 1)
                steps.up(p.tensor_scalar(var[:, :], mv[:, :, 1], EPS, None, ALU.add))
                steps.settle()
                steps.up(p.tensor_tensor(rstd[:, :], var[:, :], neghalf[:, :], ALU.pow))
                steps.settle()
                if c:
                    pool.wait_ge(small_full, job_at[("xT", c - 1, KC - 1)] + 1)
                for t in range(TT):
                    ins = p.tensor_scalar(xn[:, t, :], xr[:, c * TT + t, 0:D], mv[:, t, 0:1], rstd[:, t:t + 1],
                                          ALU.subtract, ALU.mult)
                ins.then_inc(xn_made, 1)
                if c == 0:
                    make_more_consts()
                if c == 1:
                    make_mask(1)
                    make_mask(2)
                    make_mask(3)
                    pool.wait_ge(l_small, 64)
                for cc in {0: [], 1: [0, 1], 2: [2], 3: [3]}[c]:
                    pool.wait_ge(xn_made, cc + 1)
                    for t in range(cc * TT, (cc + 1) * TT):
                        ins = p.tensor_tensor(xr[:, t, 0:D], xr[:, t, 0:D], bp_sb[:, :], ALU.add)
                    ins.then_inc(xb_made, 1)

            def fold(c):
                sl = slice(c * TT, (c + 1) * TT)
                pool.wait_ge(x1_made, c + 1)
                steps.up(p.tensor_scalar(var2[:, :], xr[:, sl, D + 1], EPS, None, ALU.add))
                steps.settle()
                p.tensor_tensor(xr[:, sl, D + 1], var2[:, :], neghalf[:, :], ALU.pow).then_inc(rstd_made, 1)

            make_consts()
            for stage, c in STAGES:
                if stage == "norm":
                    norm(c)
                if stage == "scan":
                    make_late_consts()
                if stage == "fold":
                    fold(c)

            pool.wait_ge(tok_made, 1)
            pool.wait_ge(l_rows, 16 * NCH)

            def low2(e):
                pool.wait_ge(w2hi_made, e + 1)
                p.tensor_tensor(w2_lo[e % 2][:, :, :], w2_sb[e % 2][:, :, :], w2_hi[e % 2][:, :, :].bitcast(F32),
                                ALU.subtract).then_inc(w2lo_made, 1)

            def gather(e):
                if e >= 2:
                    pool.wait_ge(l_gather[e % 2], 16 * JT * (e // 2))
                for j in range(JT * e, JT * (e + 1)):
                    p.indirect_dma_start(xg[:, j, :], None, rows, bass.IndirectOffsetOnAxis(ap=tok_load[:, j:j + 1], axis=0),
                                         bounds_check=NTOK - 1, oob_is_err=False).then_inc(l_gather[e % 2], 16)

            gather(0)
            gather(1)
            pool.wait_ge(l_out, 16 * NCH)
            for e in range(E):
                if e + 2 < E:
                    gather(e + 2)
                if e + 1 < E:
                    low2(e + 1)
                for j in range(JT):
                    pool.wait_ge(y_made, JT * (e + 1) + j + 1)
                    p.indirect_dma_start(out_rows, bass.IndirectOffsetOnAxis(ap=tok_store[:, JT * e + j:JT * e + j + 1], axis=0),
                                         xg[:, JT * e + j, 0:D], None, bounds_check=NTOK - 1, oob_is_err=False).then_inc(l_store[j], 16)
            for j in range(JT):
                pool.wait_ge(l_store[j], 16 * E)

        @block.tensor
        def _(pe):
            mm, tr = nc.tensor.matmul, nc.tensor.transpose

            def open_small(name):
                n = job_at[name]
                if n >= 2:
                    before = jobs[n - 2][0]
                    if jobs[n - 2][1] == "act":
                        pe.wait_ge(small_act, act_count(before))
                    else:
                        pe.wait_ge(small_dve, dve_count(before))
                return small(name)

            def proj(c):
                pe.wait_ge(xn_made, c + 1)
                if c == 0:
                    pe.wait_ge(consts_made, 1)
                for k in range(KC):
                    ps = open_small(("xT", c, k))
                    for t in range(TT):
                        ins = tr(ps[:, t * P:(t + 1) * P], xn[:, t, k * P:(k + 1) * P], ident[:, :])
                    ins.then_inc(small_full, 1)
                if c == 0:
                    pe.wait_ge(l_wq, 16)
                pe.wait_ge(small_act, act_count(("xT", c, KC - 1)))
                for half in range(KC):
                    ps = open_small(("q", c, half))
                    for k in range(KC):
                        ins = mm(ps[:, :], wq_sb[:, k, half * P:(half + 1) * P], xT[:, k, :], start=(k == 0), stop=(k == KC - 1))
                    ins.then_inc(small_full, 1)

            def keys(b):
                if b == 0:
                    pe.wait_ge(l_ctx, 48)
                ps = open_small(("ctxT", b))
                for k in range(KC):
                    tr(ps[:, k * MP:k * MP + P], ctx_sb[:, b, 0, k * P:(k + 1) * P], ident[:, :])
                    ins = tr(ps[:, k * MP + P:k * MP + M], ctx_sb[0:MR, b, 1, k * P:(k + 1) * P], ident[0:MR, 0:MR])
                ins.then_inc(small_full, 1)
                pe.wait_ge(small_act, act_count(("ctxT", b)))
                for half in range(KC):
                    ps = open_small(("k", b, half))
                    for k in range(KC):
                        ins = mm(ps[:, 0:MP], wkv_sb[:, k, half * P:(half + 1) * P], ctxT[:, k, :], start=(k == 0), stop=(k == KC - 1))
                    ins.then_inc(small_full, 1)
                ps = open_small(("v", b))
                for k in range(KC):
                    ins = mm(ps[:, 0:D], ctxT[:, k, 0:P], wkv_sb[:, k, D:2 * D], start=(k == 0), stop=(k == KC - 1))
                ins.then_inc(small_full, 1)
                ps = open_small(("vr", b))
                for k in range(KC):
                    ins = mm(ps[0:RP, 0:D], ctxT[:, k, P:MP], wkv_sb[:, k, D:2 * D], start=(k == 0), stop=(k == KC - 1))
                ins.then_inc(small_full, 1)

            def turn_mask(c):
                pe.wait_ge(mask_made, c + 1)
                ps = open_small(("maskT", c))[:, :].bitcast(BF16)
                for t in range(TT):
                    for r in range(2):
                        ins = tr(ps[:, r * CH + t * P:r * CH + (t + 1) * P], negm[:, c * TT + t, r * P:(r + 1) * P], identb[:, :])
                ins.then_inc(small_full, 1)

            def scan(c, i):
                t, u = divmod(i, AU)
                n = c * TT * AU + i
                if i == 0:
                    pe.wait_ge(qhi_made, KC * (c + 1))
                    pe.wait_ge(kdhi_made, KC * (c // PER_B + 1))
                    pe.wait_ge(mask_made, c + 1)
                if n >= 2:
                    pe.wait_ge(scan_read, n - 1)
                ps = a_bank[n % 2]
                tok_ = slice(t * P, (t + 1) * P)
                if u < 4:
                    half, h4 = divmod(u, 2)
                    m_ = negm[:, c * TT + t, 0:P].unsqueeze(1).to_broadcast([P, 4, P])
                    mm(ps[:, :], identb[:, :], m_, start=True, stop=False)
                    ins = mm(ps[:, :], q_hi[:, half, tok_], kd_hi[:, half, 4 * h4:4 * h4 + 4, 0:P], start=False, stop=True)
                else:
                    m_ = negm[:, c * TT + t, P:MP].unsqueeze(1).to_broadcast([P, H, RP])
                    mm(ps[:, :], identb[:, :], m_, start=True, stop=False)
                    for half in range(KC):
                        ins = mm(ps[:, half * HH * RP:(half + 1) * HH * RP], q_hi[:, half, tok_],
                                 kd_hi[:, half, :, P:MP], start=False, stop=(half == KC - 1))
                ins.then_inc(scan_full, 1)

            def maxima(c):
                pe.wait_ge(max_made, c + 1)
                ps = open_small(("max", c))
                for t in range(TT):
                    ins = tr(ps[0:H, t * P:(t + 1) * P], mxx[:, t, :], ident[:, :])
                ins.then_inc(small_full, 1)

            def scores(c, i):
                b, n = c // PER_B, 2 * UN * c + i
                half, u = divmod(i, UN)
                a, pair = unit_of(u)
                if i == 0:
                    pe.wait_ge(l_qs[c % 2], QS_DMAS * (c // 2 + 1))
                    pe.wait_ge(l_max[c % 2], 16 * (c // 2 + 1))
                    pe.wait_ge(small_act, act_count(("maskT", c)))
                    if c == 0:
                        pe.wait_ge(consts_made, 2)
                    if c % PER_B == 0:
                        pe.wait_ge(l_ks[b], KS_DMAS)
                        pe.wait_ge(sel_made, b + 1)
                if n >= 2:
                    pe.wait_ge(exp_done, n - 1)
                ps = st_bank[n % 2]
                mm(ps[:, :], identb[:, :], maskT[c % 2][:, 0 if a is not None else 1, :], start=True, stop=False)
                if a is not None:
                    g = half * (G // KC) + pair
                    ins = mm(ps[:, :], ks_main[b][:, g, a, :], qs[c % 2][:, g, :], start=False, stop=True)
                else:
                    for k in range(2):
                        g = half * (G // KC) + 2 * pair + k
                        ins = mm(ps[:, :], ks_rest[b][:, g, :], qs[c % 2][:, g, :], start=False, stop=(k == 1))
                ins.then_inc(st_full, 1)

            def values(c, half, batch):
                b, hf = c // PER_B, 2 * c + half
                pe.wait_ge(exp_done, UN * hf + (4, 8, 10)[batch])
                if batch == 0:
                    if hf:
                        pe.wait_ge(att_made, hf)
                    if c % PER_B == 0 and half == 0:
                        pe.wait_ge(v_made, b + 1)
                for ps, main, rest in ((o_bank, v_main[b], v_rest[b]), (z_bank, None, None)):
                    for pair in range(G // KC):
                        rows_ = ps[32 * pair:32 * pair + 32, :]
                        if batch < 2:
                            h = half * HH + 2 * pair + batch
                            w = z_main[:, batch, :] if main is None else main[:, h, :]
                            ins = mm(rows_, w, pt[:, (UN * hf + 4 * batch + pair) % UN, :], start=(batch == 0), stop=False,
                                     skip_group_check=True)
                        else:
                            r = pair // 2
                            w = z_rest[:, pair % 2, :] if rest is None else rest[:, half * 2 + r, pair % 2, :]
                            ins = mm(rows_, w, pt[:, (UN * hf + 8 + r) % UN, :], start=False, stop=True, skip_group_check=True)
                ins.then_inc(pv_done, 1)

            def route(c):
                for t in range(TT):
                    pe.wait_ge(xn2_made, c * TT + t + 1)
                    ps = open_small(("nT", c, t))
                    for k in range(KC):
                        ins = tr(ps[:, k * P:(k + 1) * P], xn2[:, t % 2, k * P:(k + 1) * P], ident[:, :])
                    ins.then_inc(small_full, 1)
                pe.wait_ge(small_act, act_count(("nT", c, TT - 1)))
                ps = open_small(("logits", c))
                for t in range(TT):
                    for k in range(KC):
                        ins = mm(ps[:, t * E:(t + 1) * E], xn2T[:, t, k, :], rT[:, k, :], start=(k == 0), stop=(k == KC - 1))
                ins.then_inc(small_full, 1)

            def mix(c):
                late = {(0, 0): 5, (0, 1): 9, (0, 2): 11, (1, 0): 15, (1, 1): 19}
                for i in range(2 * UN):
                    scores(c, i)
                    if c < NCH - 1:
                        scan(c + 1, i)
                    if c and i == ROUTE_AT:
                        route(c - 1)
                    for (half, batch), at in late.items():
                        if at == i:
                            values(c, half, batch)
                values(c, 1, 2)
                if c < NCH - 1:
                    maxima(c + 1)

            def fold(c):
                pe.wait_ge(att_made, 2 * c + 2)
                if c == 0:
                    pe.wait_ge(l_small, 64)
                for t in range(TT):
                    ps = open_small(("fold", c, t))
                    for k in range(KC):
                        ins = mm(ps[:, 0:D], att[:, k, t * P:(t + 1) * P], wp_sb[:, k, :], start=(k == 0), stop=(k == KC - 1))
                    ins.then_inc(small_full, 1)

            def turn_small():
                pe.wait_ge(l_small, 64)
                ps = open_small(("rT",))
                for k in range(KC):
                    ins = tr(ps[:, k * E:(k + 1) * E], r_sb[:, k * P:(k + 1) * P], ident[0:E, 0:E])
                ins.then_inc(small_full, 1)
                ps = open_small(("b1T",))
                tr(ps[:, 0:E * FC], b1_sb[:, :], ident[0:E * FC, 0:E * FC]).then_inc(small_full, 1)

            def assign():
                pe.wait_ge(onehot_made, NCH)
                ps = open_small(("cum",))
                all_ = onehot[:, :, :].rearrange("p t e -> p (t e)")
                mm(ps[:, 0:T * E], trib[:, :], all_, start=True, stop=False, skip_group_check=True)
                for t in range(T - 1):
                    ins = mm(ps[:, (t + 1) * E:T * E], onesb[:, :], onehot[:, t, :].unsqueeze(1).to_broadcast([P, T - 1 - t, E]),
                             start=False, stop=(t == T - 2), skip_group_check=True)
                for t in range(T):
                    ins = mm(ps[:, T * E:(T + 1) * E], onesb[:, :], onehot[:, t, :], start=False, stop=(t == T - 1),
                             skip_group_check=True)
                ins.then_inc(small_full, 1)
                pe.wait_ge(what_made, 1)
                ps = open_small(("slots",))
                for t in range(T):
                    ins = mm(ps[:, 0:3 * J], psel[:, t, :], what[:, t, :, :].rearrange("p c j -> p (c j)"),
                             start=(t == 0), stop=(t == T - 1))
                ins.then_inc(small_full, 1)

            for stage, c in STAGES:
                if stage == "proj":
                    proj(c)
                if stage == "keys":
                    keys(c)
                if stage == "mask":
                    turn_mask(c)
                if stage == "scan":
                    for i in range(TT * AU):
                        scan(c, i)
                    maxima(c)
                if stage == "small":
                    turn_small()
                if stage == "mix":
                    mix(c)
                if stage == "fold":
                    fold(c)
                if stage == "route":
                    route(c)
                if stage == "assign":
                    assign()

            def turn(e, s):
                pe.wait_ge(gn_made, e + 1)
                for part_, js in enumerate(TURNS):
                    pe.wait_ge(gTlo_made, len(TURNS) * e + (part_ + 1))
                    for j in js:
                        for k in range(KC):
                            c0 = (j - js[0]) * D + k * P
                            ins = tr(t_bank[part_][:, c0:c0 + P], gn[:, s, j, k * P:(k + 1) * P], ident[:, :])
                    ins.then_inc(t_full, 1)

            def hidden(it, s, f, width):
                ps = h_bank[f % 4]
                chunk = slice(f * P, (f + 1) * P)
                n = 0
                for w_, g_ in ((w1_hi, gT_hi), (w1_hi, gT_lo), (w1_lo, gT_hi)):
                    for k in range(KC):
                        ins = mm(ps[:, 0:width], w_[s][:, k, chunk], g_[:, s, k, 0:width], start=(n == 0), stop=(n == 3 * KC - 1))
                        n += 1
                ins.then_inc(h_full, 1)

            def result(e, s, j):
                ps = y_bank[(JT * s + j) % 2]
                tile_ = slice(j * P, (j + 1) * P)
                n = 0
                for f in range(FC):
                    if j == 0:
                        pe.wait_ge(hlo_made, e * FC + (f + 3))
                    for h_, w_ in ((h_hi, w2_hi), (h_hi, w2_lo), (h_lo, w2_hi)):
                        ins = mm(ps[:, 0:D], h_[:, f, tile_], w_[s][:, f, :], start=(n == 0), stop=(n == 3 * FC - 1))
                        n += 1
                ins.then_inc(y_full, 1)

            def expert(it, s, left):
                e = it * 2 + s
                tiles = (tiles_code >> (e * 2)) & 3
                pe.wait_ge(gTlo_made, (e + 2) * len(TURNS))
                pe.wait_ge(w1lo_made, (e + 1) * 4)
                with pe.If(tiles > JT - 2):
                    for f in range(FC):
                        pe.wait_ge(h_made, e * FC + (f + 1))
                        hidden(it, s, f, CAP)
                with pe.Else():
                    for f in range(FC):
                        pe.wait_ge(h_made, e * FC + (f + 1))
                        hidden(it, s, f, CAP - P)
                pe.wait_ge(w2lo_made, e + 1)
                pe.wait_ge(y_read, e * JT + 1)
                result(e, s, 0)
                if left:
                    turn(e + 1, 1 - s)
                for j in range(1, JT):
                    pe.wait_ge(y_read, e * JT + (j + 1))
                    with pe.If(tiles > j - 1):
                        result(e, s, j)
                    with pe.Else():
                        pe.drain().then_inc(y_full, 1)

            pe.sem_inc(y_full, JT)
            pe.wait_ge(tok_made, 1)
            tiles_code = pe.value_load(more[0:1, 0:1], min_val=0, max_val=4 ** E - 1)
            turn(0, 0)
            with pe.Fori(0, E // 2 - 1) as it:
                
                expert(it, 0, 2)
                expert(it, 1, 2)
            expert(E // 2 - 1, 0, 1)
            expert(E // 2 - 1, 1, 0)

        @block.scalar
        def _(act):
            a = nc.scalar

            def full(name):
                act.wait_ge(small_full, job_at[name] + 1)
                return small(name)

            def proj(c):
                if c:
                    act.wait_ge(small_full, job_at[("q", c - 1, KC - 1)] + 1)
                for k in range(KC):
                    ps = full(("xT", c, k))
                    a.activation(xT[:, k, :], ps[:, :], ACT.Copy).then_inc(small_act, 1)
                for half in range(KC):
                    ps = full(("q", c, half))
                    if c and half == 0:
                        act.wait_ge(scan_full, TT * AU * c)
                        act.wait_ge(l_qd, 32 * c)
                        act.wait_ge(qlo_made, KC * c)
                    a.activation(q_hi[:, half, :], ps[:, :], ACT.Copy).then_inc(qhi_made, 1)

            def keys(b):
                ps = full(("ctxT", b))
                if b:
                    act.wait_ge(small_full, job_at[("vr", b - 1)] + 1)
                a.activation(ctxT[:, :, 0:M], ps[:, 0:KC * MP].rearrange("p (k m) -> p k m", k=KC)[:, :, 0:M],
                             ACT.Copy).then_inc(small_act, 1)
                for half in range(KC):
                    ps = full(("k", b, half))
                    if b:
                        act.wait_ge(kdhi_made, KC * b)
                        act.wait_ge(l_kd, 32 * b)
                    a.activation(k_hi[:, half, :], ps[:, 0:MP], ACT.Copy).then_inc(khi_made, 1)

            def turn_mask(c):
                ps = full(("maskT", c))
                if c >= 2:
                    act.wait_ge(st_full, 2 * UN * (c - 1))
                a.activation(maskT[c % 2][:, :, :].rearrange("p r n -> p (r n)"), ps[:, :].bitcast(BF16), ACT.Copy).then_inc(small_act, 1)

            def maxima(c):
                ps = full(("max", c))
                if c:
                    act.wait_ge(l_md, 16 * c)
                a.activation(nmT[:, :], ps[0:H, :], ACT.Copy, scale=-1.0).then_inc(small_act, 1)

            def exponentials(c, i):
                n = 2 * UN * c + i
                hf, u = divmod(n, UN)
                act.wait_ge(st_full, n + 1)
                if hf:
                    act.wait_ge(pv_done, 3 * (hf - 1) + pv_batch_of(u) + 1)
                a.activation(pt[:, n % UN, :], st_bank[n % 2][:, :], ACT.Exp, scale=SCALE).then_inc(exp_done, 1)

            def route(c):
                for t in range(TT):
                    ps = full(("nT", c, t))
                    if c and t == 0:
                        act.wait_ge(small_full, job_at[("logits", c - 1)] + 1)
                    a.activation(xn2T[:, t, :, :].rearrange("p k n -> p (k n)"), ps[:, 0:D], ACT.Copy).then_inc(small_act, 1)
                act.wait_ge(below_made, c + 1)
                a.activation(lex[:, :, :], below[:, :, :], ACT.Exp).then_inc(lex_made, 1)

            for stage, c in STAGES:
                if stage == "proj":
                    proj(c)
                if stage == "keys":
                    keys(c)
                if stage == "mask":
                    turn_mask(c)
                if stage == "scan":
                    maxima(c)
                if stage == "small":
                    ps = full(("rT",))
                    a.activation(rT[:, :, :].rearrange("p k e -> p (k e)"), ps[:, 0:KC * E], ACT.Copy).then_inc(small_act, 1)
                    ps = full(("b1T",))
                    a.activation(b1T[:, :], ps[:, 0:E * FC], ACT.Copy).then_inc(small_act, 1)
                if stage == "mix":
                    for i in range(2 * UN):
                        exponentials(c, i)
                        if c and i == ROUTE_AT:
                            route(c - 1)
                    if c < NCH - 1:
                        maxima(c + 1)
                if stage == "split":
                    act.wait_ge(l_w1[0], 16)
                    act.wait_ge(l_w2[0], 16)
                    act.wait_ge(st_full, 2 * UN * NCH)
                    act.wait_ge(pv_done, 3 * 2 * NCH)
                    a.activation(w1_hi[0][:, :, :], w1_sb[0][:, :, :], ACT.Copy).then_inc(w1hi_made, 1)
                    a.activation(w2_hi[0][:, :, :], w2_sb[0][:, :, :], ACT.Copy).then_inc(w2hi_made, 1)
                if stage == "route":
                    route(c)
                    a.activation(warm[:, :], neghalf[:, 0:1], ACT.Gelu)

            def turned(e, s):
                for part_, js in enumerate(TURNS):
                    act.wait_ge(t_full, len(TURNS) * e + (part_ + 1))
                    if part_ == 0 and not (isinstance(e, int) and e == 0):
                        act.wait_ge(h_full, e * FC)
                    to, src = turned_aps(gT_hi, s, part_, js)
                    a.activation(to, src, ACT.Copy).then_inc(gT_made, 1)

            def expert(it, s, left):
                e = it * 2 + s
                for f in range(FC):
                    act.wait_ge(h_full, e * FC + (f + 1))
                    act.wait_ge(hlo_made, e * FC + (f + 1))
                    b_ = b1T[:, bass.ds(e * FC + f, 1)] if not isinstance(e, int) else b1T[:, e * FC + f:e * FC + f + 1]
                    a.activation(h32[:, f % 2, :], h_bank[f % 4][:, 0:CAP], ACT.Gelu, bias=b_)
                    a.activation(h_hi[:, f, :], h_bank[f % 4][:, 0:CAP], ACT.Gelu, bias=b_).then_inc(h_made, 1)
                if left:
                    turned(e + 1, 1 - s)
                    act.wait_ge(l_w2[1 - s], (it + s) * 16 + 16)
                    act.wait_ge(y_full, (e + 1) * JT)
                    high2(1 - s)
                if left > 1:
                    act.wait_ge(l_w1[s], it * 16 + 32)
                    high1(s)

            def high1(s):
                a.activation(w1_hi[s][:, :, :], w1_sb[s][:, :, :], ACT.Copy).then_inc(w1hi_made, 1)

            def high2(s):
                a.activation(w2_hi[s][:, :, :], w2_sb[s][:, :, :], ACT.Copy).then_inc(w2hi_made, 1)

            act.sem_inc(h_made, 4)
            act.wait_ge(tok_made, 1)
            act.wait_ge(l_w1[1], 16)
            high1(1)
            turned(0, 0)
            with act.Fori(0, E // 2 - 1) as it:
                expert(it, 0, 2)
                expert(it, 1, 2)
            expert(E // 2 - 1, 0, 1)
            expert(E // 2 - 1, 1, 0)

        @block.vector
        def _(dve):
            steps = Count(dve, dve_step)
            v = nc.vector

            def full(name):
                dve.wait_ge(small_full, job_at[name] + 1)
                return small(name)

            def zeros():
                for t in v_main + v_rest:
                    steps.up(v.memset(t[:], 0.0))
                for t in ks_main + ks_rest:
                    ins = v.memset(t[:].bitcast(F32), 0.0)
                    steps.up(ins)
                steps.settle()
                dve.engine_nop().then_inc(zeros_made, 1)

            def norm(c):
                dve.wait_ge(l_x[c], 16)
                if c:
                    dve.wait_ge(xn_made, c)
                for t in range(TT):
                    steps.up(v.bn_stats(stats[:, t, :], xr[:, c * TT + t, 0:D]))
                steps.settle()
                for t in range(TT):
                    ins = v.bn_aggr(mv[:, t, :], stats[:, t, :])
                ins.then_inc(stats_made, 1)
                if c == 0:
                    zeros()

            def proj(c):
                for half in range(KC):
                    ps = full(("q", c, half))
                    dve.wait_ge(qhi_made, KC * c + half + 1)
                    if c and half == 0:
                        dve.wait_ge(l_qd, 32 * c)
                    v.tensor_tensor(q_lo[:, half, :], ps[:, :], q_hi[:, half, :].bitcast(F32), ALU.subtract).then_inc(qlo_made, 1)
                    dve.wait_ge(qlo_made, KC * c + half + 1)
                    dve.engine_nop().then_inc(small_dve, 1)

            def keys(b):
                for half in range(KC):
                    ps = full(("k", b, half))
                    dve.wait_ge(khi_made, KC * b + half + 1)
                    if b:
                        dve.wait_ge(l_kd, 32 * b)
                    v.tensor_tensor(k_lo[:, half, :], ps[:, 0:MP], k_hi[:, half, :].bitcast(F32), ALU.subtract).then_inc(klo_made, 1)
                    dve.wait_ge(klo_made, KC * b + half + 1)
                    dve.engine_nop().then_inc(small_dve, 1)
                    if b:
                        dve.wait_ge(scan_full, TT * AU * PER_B * b)
                    else:
                        dve.wait_ge(consts_made, 1)
                    v.tensor_tensor(kd_hi[:, half], k_hi[:, half, :].bitcast(F32).unsqueeze(1).to_broadcast([P, HH, MP]),
                                    headsel[:, :].unsqueeze(2).to_broadcast([P, HH, MP]), ALU.mult).then_inc(kdhi_made, 1)
                ps = full(("v", b))
                to = v_main[b][:, :, :].rearrange("p (g a) c -> p g a c", a=2)
                src = ps[:, 0:D].rearrange("p (g a d) -> p g a d", a=2, d=DH)
                v.tensor_copy(to[:, :, 0, 0:DH], src[:, :, 0, :])
                v.tensor_copy(to[:, :, 1, DH:2 * DH], src[:, :, 1, :]).then_inc(small_dve, 1)
                ps = full(("vr", b))
                src = ps[0:RP, 0:D].rearrange("p (r i d) -> p r i d", i=4, d=DH)
                for i in range(4):
                    ins = v.tensor_copy(v_rest[b][32 * i:32 * i + 32, :, i // 2, DH * (i % 2):DH * (i % 2) + DH], src[:, :, i, :])
                    if i < 3:
                        steps.up(ins)
                ins.then_inc(small_dve, 1)
                dve.wait_ge(small_dve, dve_count(("vr", b)))
                dve.engine_nop().then_inc(v_made, 1)

            def selectors(b):
                dve.wait_ge(consts_made, 2)
                for g in range(G):
                    steps.up(v.tensor_copy(ks_main[b][96:P, g, :, :], pairsel[96:P, :, :]))
                    c0 = 2 * RP * (g % 2)
                    steps.up(v.tensor_copy(ks_rest[b][96:P, g, c0:c0 + 2 * RP].rearrange("p (a m) -> p a m", a=2),
                                           pairsel[96:P, :, 0:RP]))
                steps.settle()
                dve.engine_nop().then_inc(sel_made, 1)

            def scan(c, i):
                t, u = divmod(i, AU)
                n = c * TT * AU + i
                dve.wait_ge(scan_full, n + 1)
                if i == 0 and c:
                    dve.wait_ge(max_made, c)
                if u < 4:
                    v.tensor_reduce(mx[:, t, 4 * u:4 * u + 4], a_bank[n % 2][:, :].rearrange("p (h m) -> p h m", h=4),
                                    AX_X, ALU.max).then_inc(scan_read, 1)
                else:
                    v.tensor_reduce(mxr[:, t, :], a_bank[n % 2][:, :].rearrange("p (h m) -> p h m", h=H),
                                    AX_X, ALU.max).then_inc(scan_read, 1)

            def maxima(c):
                dve.wait_ge(scan_read, TT * AU * (c + 1))
                if c:
                    dve.wait_ge(small_full, job_at[("max", c - 1)] + 1)
                v.tensor_tensor(mxx[:, :, :], mx[:, :, :], mxr[:, :, :], ALU.max).then_inc(max_made, 1)

            def divide(c, half):
                hf = 2 * c + half
                dve.wait_ge(pv_done, 3 * hf + 3)
                if half == 0 and c:
                    dve.wait_ge(small_full, job_at[("fold", c - 1, TT - 1)] + 1)
                if hf:
                    dve.wait_ge(att_made, hf)
                steps.up(v.reciprocal(rz[:, :], z_bank[:, :]))
                steps.settle()
                v.tensor_tensor(att[:, half, :], o_bank[:, :], rz[:, :], ALU.mult).then_inc(att_made, 1)

            def fold(c):
                dve.wait_ge(xb_made, c + 1)
                for t in range(TT):
                    ps = full(("fold", c, t))
                    tt = c * TT + t
                    v.tensor_tensor(xr[:, tt, 0:D], ps[:, 0:D], xr[:, tt, 0:D], ALU.add).then_inc(small_dve, 1)
                dve.wait_ge(small_dve, dve_count(("fold", c, TT - 1)))
                for t in range(TT):
                    steps.up(v.bn_stats(stats[:, t, :], xr[:, c * TT + t, 0:D]))
                steps.settle()
                for t in range(TT):
                    ins = v.bn_aggr(xr[:, c * TT + t, D:D + 2], stats[:, t, :])
                ins.then_inc(x1_made, 1)

            def route(c):
                sl = slice(c * TT, (c + 1) * TT)
                dve.wait_ge(rstd_made, c + 1)
                for t in range(TT):
                    tt = c * TT + t
                    if tt >= 2:
                        last = ("nT", (tt - 2) // TT, (tt - 2) % TT)
                        dve.wait_ge(small_full, job_at[last] + 1)
                    v.tensor_scalar(xn2[:, t % 2, :], xr[:, tt, 0:D], xr[:, tt, D:D + 1], xr[:, tt, D + 1:D + 2],
                                    ALU.subtract, ALU.mult).then_inc(xn2_made, 1)
                ps = full(("logits", c))
                if c:
                    dve.wait_ge(gate_made, c)
                    dve.wait_ge(onehot_made, c)
                v.tensor_copy(lg[:, :, :].rearrange("p t e -> p (t e)"), ps[:, 0:TT * E]).then_inc(small_dve, 1)
                dve.wait_ge(small_dve, dve_count(("logits", c)))
                steps.up(v.tensor_reduce(lmax[:, :], lg[:, :, :], AX_X, ALU.max))
                steps.settle()
                v.tensor_tensor(below[:, :, :], lg[:, :, :], lmax[:, :].unsqueeze(2).to_broadcast([P, TT, E]),
                                ALU.subtract).then_inc(below_made, 1)
                dve.wait_ge(below_made, c + 1)
                if c == 0:
                    dve.wait_ge(consts_made, 3)
                steps.up(v.scalar_tensor_tensor(out=rank[:, :, :], in0=below[:, :, :], scalar=0.0, in1=first[:, :, :],
                                                op0=ALU.is_ge, op1=ALU.mult))
                steps.settle()
                steps.up(v.tensor_reduce(best[:, :], rank[:, :, :], AX_X, ALU.max))
                steps.settle()
                v.tensor_tensor(onehot[:, sl, :], rank[:, :, :], best[:, :].unsqueeze(2).to_broadcast([P, TT, E]),
                                ALU.is_equal).then_inc(onehot_made, 1)
                dve.wait_ge(lex_made, c + 1)
                steps.up(v.tensor_reduce(lsum[:, :], lex[:, :, :], AX_X, ALU.add))
                steps.settle()
                v.reciprocal(xr[:, sl, D + 2], lsum[:, :]).then_inc(gate_made, 1)

            def assign():
                ps = full(("cum",))
                dve.wait_ge(onehot_made, NCH)
                for m in range(1, JT):
                    steps.up(v.tensor_scalar(past[:, m - 1, :], ps[0:1, T * E:(T + 1) * E], float(m * P + 1), None, ALU.is_ge))
                v.tensor_tensor(cum[:, :, :], ps[:, 0:T * E].rearrange("p (t e) -> p t e", e=E), onehot[:, :, :],
                                ALU.mult).then_inc(small_dve, 1)
                steps.up(v.tensor_tensor(ebs[:, :, :], ebase[:, :, :], onehot[:, :, :], ALU.mult))
                dve.wait_ge(small_dve, dve_count(("cum",)))
                steps.settle()
                steps.up(v.tensor_reduce(pos[:, :], cum[:, :, :], AX_X, ALU.add))
                steps.up(v.tensor_reduce(jslot[:, :], ebs[:, :, :], AX_X, ALU.add))
                steps.settle()
                for m in range(1, JT + 1):
                    steps.up(v.tensor_scalar(over[:, :, m - 1], pos[:, :], float(m * P), None, ALU.is_ge))
                steps.settle()
                for m in range(1, JT + 1):
                    steps.up(v.tensor_tensor(jslot[:, :], jslot[:, :], over[:, :, m - 1], ALU.add))
                    steps.up(v.scalar_tensor_tensor(out=pos[:, :], in0=over[:, :, m - 1], scalar=-float(P) if m < JT else float(NTOK),
                                                    in1=pos[:, :], op0=ALU.mult, op1=ALU.add))
                    steps.settle()
                steps.up(v.tensor_tensor(psel[:, :, :], lane[:, :].unsqueeze(1).to_broadcast([P, T, P]),
                                         pos[:, :].unsqueeze(2).to_broadcast([P, T, P]), ALU.is_equal))
                steps.up(v.tensor_tensor(jsel[:, :, :], lane[:, 0:J].unsqueeze(1).to_broadcast([P, T, J]),
                                         jslot[:, :].unsqueeze(2).to_broadcast([P, T, J]), ALU.is_equal))
                steps.settle()
                steps.up(v.tensor_scalar(what[:, :, 0, :], jsel[:, :, :], part[:, 0:1], None, ALU.mult))
                steps.up(v.tensor_tensor(what[:, :, 1, :], jsel[:, :, :], tileno[:, :, :], ALU.mult))
                steps.up(v.tensor_copy(what[:, :, 2, :], jsel[:, :, :]))
                steps.settle()
                dve.engine_nop().then_inc(what_made, 1)
                steps.up(v.tensor_tensor(past[:, :, :], past[:, :, :], bits[:, :, :], ALU.mult))
                steps.settle()
                steps.up(v.tensor_reduce(code[:, :], past[:, :, :].rearrange("p m e -> p (m e)"), AX_X, ALU.add))
                steps.settle()
                steps.up(v.tensor_copy(more[:, :], code[:, :]))
                ps = full(("slots",))
                v.tensor_copy(slots[:, :, :].rearrange("p c j -> p (c j)"), ps[:, 0:3 * J]).then_inc(small_dve, 1)
                dve.wait_ge(small_dve, dve_count(("slots",)))
                steps.up(v.scalar_tensor_tensor(out=tok[:, :], in0=slots[:, 1, :], scalar=float(P), in1=slots[:, 0, :],
                                                op0=ALU.mult, op1=ALU.add))
                steps.settle()
                steps.up(v.scalar_tensor_tensor(out=tokfar[:, :], in0=slots[:, 2, :], scalar=-FAR, in1=tok[:, :],
                                                op0=ALU.mult, op1=ALU.add))
                steps.settle()
                steps.up(v.tensor_scalar(tok_store[:, :], tokfar[:, :], FAR, None, ALU.add))
                steps.up(v.tensor_scalar(tok_load[:, :], tokfar[:, :], FAR, float(NTOK - 1), ALU.add, ALU.min))
                steps.settle()
                dve.engine_nop().then_inc(tok_made, 1)

            def low1(s, n, quarter):
                if quarter == 0:
                    dve.wait_ge(w1hi_made, n)
                fs = slice(quarter * (F // 4), (quarter + 1) * (F // 4))
                v.tensor_tensor(w1_lo[s][:, :, fs], w1_sb[s][:, :, fs], w1_hi[s][:, :, fs].bitcast(F32), ALU.subtract).then_inc(w1lo_made, 1)

            def low2(s, n):
                dve.wait_ge(w2hi_made, n)
                v.tensor_tensor(w2_lo[s][:, :, :], w2_sb[s][:, :, :], w2_hi[s][:, :, :].bitcast(F32), ALU.subtract).then_inc(w2lo_made, 1)

            for stage, c in STAGES:
                if stage == "norm":
                    norm(c)
                if stage == "proj":
                    proj(c)
                if stage == "keys":
                    keys(c)
                    if c:
                        selectors(c)
                if stage == "scan":
                    for i in range(TT * AU):
                        scan(c, i)
                    maxima(c)
                    selectors(0)
                if stage == "mix":
                    for i in range(2 * UN):
                        if c < NCH - 1:
                            scan(c + 1, i)
                        if c and i == ROUTE_AT:
                            route(c - 1)
                        if i == 11:
                            divide(c, 0)
                    if c < NCH - 1:
                        maxima(c + 1)
                    divide(c, 1)
                if stage == "fold":
                    fold(c)
                if stage == "route":
                    route(c)
                if stage == "assign":
                    assign()
                    for quarter in range(4):
                        low1(0, 1, quarter)
                    low2(0, 1)

            def at(t, e, j):
                return t[:, bass.ds(e * JT + j, 1), :] if not isinstance(e, int) else t[:, e * JT + j:e * JT + j + 1, :]

            def normalise(e, s, uses):
                for j in range(JT):
                    if j == 0:
                        if isinstance(e, int) and e == 0:
                            dve.wait_ge(tok_made, 1)
                        dve.wait_ge(l_gather[s], uses * (16 * JT))
                        if not (isinstance(e, int) and e == 0):
                            dve.wait_ge(t_full, e * len(TURNS))
                    r = at(xg, e, j)
                    ins = v.tensor_scalar(gn[:, s, j, :], r[:, 0, 0:D], r[:, 0, D:D + 1], r[:, 0, D + 1:D + 2],
                                          ALU.subtract, ALU.mult)
                ins.then_inc(gn_made, 1)

            def turned(e, s):
                for part_, js in enumerate(TURNS):
                    dve.wait_ge(gT_made, len(TURNS) * e + (part_ + 1))
                    to, src = turned_aps(gT_lo, s, part_, js)
                    v.tensor_tensor(to, src, turned_aps(gT_hi, s, part_, js)[0].bitcast(F32), ALU.subtract).then_inc(gTlo_made, 1)

            def expert(it, s, left):
                e = it * 2 + s
                if left:
                    normalise(e + 1, 1 - s, it + (1 + s))
                for f in range(FC):
                    dve.wait_ge(h_made, e * FC + (f + 5))
                    v.tensor_tensor(h_lo[:, f, :], h32[:, f % 2, :], h_hi[:, f, :].bitcast(F32), ALU.subtract).then_inc(hlo_made, 1)
                    if left and f % 2:
                        low1(1 - s, e + 2, f // 2)
                for j in range(JT):
                    dve.wait_ge(y_full, e * JT + (j + JT + 1))
                    dve.wait_ge(y_made, e * JT + (j + 1))
                    b2_e = b2_sb[:, bass.ds(e, 1), :] if not isinstance(e, int) else b2_sb[:, e:e + 1, :]
                    v.tensor_tensor(y1[:, j, :], y_bank[(JT * s + j) % 2][:, 0:D], b2_e[:, 0, :], ALU.add).then_inc(y_read, 1)
                    dve.wait_ge(y_read, e * JT + (j + 3))
                    r = at(xg, e, j)
                    v.scalar_tensor_tensor(out=r[:, 0, 0:D], in0=y1[:, j, :], scalar=r[:, 0, D + 2:D + 3], in1=r[:, 0, 0:D],
                                           op0=ALU.mult, op1=ALU.add).then_inc(y_made, 1)
                    if j == 0 and left:
                        turned(e + 1, 1 - s)
            dve.sem_inc(y_read, 2)
            dve.sem_inc(y_made, JT)
            dve.sem_inc(hlo_made, 2)
            dve.sem_inc(gTlo_made, len(TURNS))
            normalise(0, 0, 1)
            turned(0, 0)
            dve.wait_ge(l_b2, 16)
            with dve.Fori(0, E // 2 - 1) as it:
                expert(it, 0, 2)
                expert(it, 1, 2)
            expert(E // 2 - 1, 0, 1)
            expert(E // 2 - 1, 1, 0)


_INS = ['x', 'ctx_1024', 'mask_BxSxS2_bk0', 'L0_xattn_Wq', 'L0_xattn_Wkv', 'L0_xattn_Wproj', 'L0_xattn_bproj',
        'L0_ffn_router_w', 'L0_ffn_w1', 'L0_ffn_b1', 'L0_ffn_w2', 'L0_ffn_b2']
_OUTS = [((2, 1024, 256), 'float32')]


def kernel(**inputs):
    import numpy as _np
    import concourse.bacc as _bacc
    from concourse import mybir as _mybir
    from concourse.bass_utils import run_bass_kernel_spmd as _run

    nc = _bacc.Bacc("TRN2", target_bir_lowering=False, num_devices=1)
    arrays, args = {}, []
    for name in _INS:
        a = _np.ascontiguousarray(inputs[name])
        arrays[f"in_{name}_dram"] = a
        args.append(nc.dram_tensor(f"in_{name}_dram", a.shape, _mybir.dt.from_np(a.dtype), kind="ExternalInput").ap())
    for i, (shape, dtype) in enumerate(_OUTS):
        dt = _mybir.dt.from_np(_np.dtype(dtype))
        args.append(nc.dram_tensor(f"out_{i}_dram", shape, dt, kind="ExternalOutput").ap())
    build(nc, *args)
    r = _run(nc, [arrays], core_ids=[0])
    return r.results[0]["out_0_dram"]
```

```python
from contextlib import ExitStack

import concourse.bass as bass
from concourse import mybir

F32 = mybir.dt.float32
F32R = mybir.dt.float32r
BF16 = mybir.dt.bfloat16
I32 = mybir.dt.int32
U8 = mybir.dt.uint8
ALU = mybir.AluOpType
ACT = mybir.ActivationFunctionType
AX_X = mybir.AxisListType.X

P = 128
NEG = -1.0e30
EPS = 1e-5
HEADS = 16

STAGES = [
    ("stats", 0), ("norm", 0), ("keys", 0), ("stats", 1), ("turn", 0), ("norm", 1), ("proj", 0), ("scan", 0), ("proj", 1),
    ("mix", 0), ("mix", 1), ("mix", 2), ("mix", 3), ("split", 0), ("tail", 3),
]
TT = 4
AU = 5
UN = 10
SCANS_AT = ([0, 1, 1, 2, 3, 3, 4, 5, 5, 6, 7, 9, 9, 10, 12, 14, 15, 15, 16, 17],
            [0, 1, 2, 3, 4, 5, 5, 6, 7, 7, 8, 8, 9, 10, 12, 13, 14, 15, 16, 17])
VALUES_AT = ([4, 8, 10, 17, 19, 20], [4, 8, 10, 16, 19, 19])
DIVIDE_AT = ([11, 12, 13, 14], [10, 11, 12, 12])
LAST_DIVIDE_AT = ([0, 0, 1, 1], [0, 0, 0, 0])
FOLD_AT = ([1, 2, 3, 4], [1, 3, 4, 5])
ROUTE_AT = (10, 9)
EARLY_DIVIDES = (2, 0)
PROJ_AT = 20
MASK_AT = 20
KEYS_AT = 12
STATS_AT = (4, 7)
NORM_AT = (8, 8)
MAX_AT = 17
TURN_AT = 18
PLACE_AT, SLOT_AT = (3, 6, 18), (6, 11, 19)


def mix_steps(c):
    steps = []
    last = c == 3
    for i in range(2 * UN + 1):
        if i < 2 * UN:
            steps.append(("scores", c, i))
        if not last:
            steps += [("scan", c + 1, n) for n in range(TT * AU) if SCANS_AT[c > 0][n] == i]
        if c:
            steps += [("divide", c - 1, (1, t)) for t in range(0 if last else sum(EARLY_DIVIDES), TT) if LAST_DIVIDE_AT[last][t] == i]
            steps += [("fold", c - 1, t) for t in range(TT) if FOLD_AT[last][t] == i]
            if FOLD_AT[last][-1] == i:
                steps.append(("std", c - 1, None))
            steps += route_steps(c - 1, i - ROUTE_AT[last])
        steps += [("values", c, divmod(n, 3)) for n in range(6) if VALUES_AT[last][n] == i]
        steps += [("divide", c, (0, t)) for t in range(TT) if DIVIDE_AT[last][t] == i]
        if last:
            steps += [("place", k, 0) for k in range(3) if PLACE_AT[k] == i]
            steps += [("slot", k, 0) for k in range(3) if SLOT_AT[k] == i]
        if c == 0 and i == KEYS_AT:
            steps.append(("keys", 1, 0))
        if c == 0 and i == 2 * UN:
            steps.append(("spread", 1, 0))
        if c < 2 and i == 2 * UN:
            steps += [("divide", c, (1, t)) for t in range(EARLY_DIVIDES[0])]
        if c < 2 and i == STATS_AT[c]:
            steps.append(("stats", c + 2, 0))
        if c < 2 and i == NORM_AT[c]:
            steps.append(("norm", c + 2, 0))
        if not last and i == MAX_AT:
            steps.append(("max", c + 1, 0))
        if c < 2 and i == TURN_AT:
            steps.append(("turn", c + 2, 0))
        if c < 2 and i == PROJ_AT:
            steps.append(("proj", c + 2, 0))
        if c < 2 and i == MASK_AT:
            steps.append(("mask", c + 2, 0))
    if c < 2:
        steps += [("divide", c, (1, t)) for t in range(EARLY_DIVIDES[0], sum(EARLY_DIVIDES))]
    return steps


def scan_steps():
    steps = []
    between = {4: ("small", 0, 0), 7: ("mask", 0, 0), 10: ("turn", 1, 0), 14: ("mask", 1, 0)}
    for n in range(TT * AU):
        steps.append(("scan", 0, n))
        if n in between:
            steps.append(between[n])
    return steps + [("max", 0, 0)]


def route_steps(c, i):
    steps = []
    if 0 <= i < TT:
        steps.append(("xn2", c, i))
    if 1 <= i < 1 + TT:
        steps.append(("nT", c, i - 1))
    if 2 <= i < 2 + TT:
        steps.append(("logits", c, i - 2))
    if 2 + TT <= i < 5 + TT:
        steps.append(("pick", c, i - 2 - TT))
    return steps


def tail_steps(c):
    steps = []
    for i in range(7 + TT):
        if i < TT:
            steps.append(("divide", c, (1, i)))
        if 1 <= i < 1 + TT:
            steps += [("fold", c, i - 1), ("std", c, i - 1)]
        steps += route_steps(c, i - 2)
    return steps + [("place", c, 0), ("slot", c, 0)]


class Count:

    def __init__(self, engine, semaphore):
        self.engine, self.semaphore, self.n = engine, semaphore, 0

    def up(self, instruction):
        instruction.then_inc(self.semaphore, 1)
        self.n += 1

    def settle(self):
        self.engine.wait_ge(self.semaphore, self.n)


def small_jobs():
    jobs = []
    for stage, c in STAGES:
        if stage == "proj":
            jobs += proj_jobs(c)
        if stage == "turn":
            jobs += turn_jobs(c)
        if stage == "keys":
            jobs += key_jobs(c)
        if stage == "mask":
            jobs += [(("maskT", c), "act")]
        if stage == "scan":
            jobs += step_jobs(scan_steps())
        if stage == "mix":
            jobs += step_jobs(mix_steps(c))
        if stage == "tail":
            jobs += step_jobs(tail_steps(c))
    return jobs


def key_jobs(b):
    return [(("ctxT", b), "act"), (("k", b, 0), "dve"), (("k", b, 1), "dve"), (("v", b), "act"), (("vr", b), "act")]


def proj_jobs(c):
    return [(("q", c, k), "dve") for k in range(2)]


def turn_jobs(c):
    return [(("xT", c, k), "act") for k in range(2)]


def step_jobs(steps):
    jobs = []
    for step, c, t in steps:
        if step in ("fold", "logits", "place"):
            jobs.append(((step, c, t), "dve"))
        if step == "turn":
            jobs += turn_jobs(c)
        if step == "keys":
            jobs += key_jobs(c)
        if step == "proj":
            jobs += proj_jobs(c)
        if step == "mask":
            jobs.append((("maskT", c), "act"))
        if step == "small":
            jobs += [(("rT",), "act"), (("b1T",), "act")]
        if step == "nT":
            jobs.append(((step, c, t), "act"))
        if step == "max":
            jobs.append(((step, c), "act"))
    return jobs


def build(nc, x, ctx, mask, wq, wkv, wproj, bproj, router, w1, b1, w2, b2, out):
    B, N, D = x.shape
    M = ctx.shape[1]
    H = HEADS
    DH = D // H
    E, _, F = w1.shape
    KC = D // P
    HH = H // KC
    G = H // 2
    CH = 512
    NCH = B * N // CH
    PER_B = N // CH
    T = B * N // P
    MR = M - P
    RP = 32
    MP = P + RP
    CAP = max(-(-3 * B * N // (2 * E)), 1)
    JT = CAP // P
    J = E * JT
    TURNS = ((0, 1), (2,))
    FC = F // P
    ROW = D + 4
    NTOK = B * N
    SCALE = float(DH) ** -0.5
    assert TT == CH // P and JT == 3 and D == 256 and NCH == 4 and 0 < MR < RP and CAP % P == 0 and E % 2 == 0 and H * DH == D
    KS_DMAS = 16 * 3 * 2 * 3
    QS_DMAS = 16 * 3
    FAR = float(2 * NTOK)

    x_t = x.rearrange("b (t p) d -> p (b t) d", p=P)
    mask_t = mask.rearrange("b (t p) m -> p (b t) m", p=P)
    out_rows = out.rearrange("b n d -> (b n) d")
    out_t = out.rearrange("b (t p) d -> p (b t) d", p=P)
    rows = nc.dram_tensor("rows", [NTOK, ROW], F32, kind="Internal").ap()
    rows_t = rows.rearrange("(t p) d -> p t d", p=P)
    q_dram = nc.dram_tensor("q_dram", [2, 2, D, CH], F32, kind="Internal").ap()
    k_dram = nc.dram_tensor("k_dram", [B, 2, D, MP], F32, kind="Internal").ap()

    jobs = small_jobs()
    job_at = {name: n for n, (name, _) in enumerate(jobs)}

    with ExitStack() as stack:
        def make(scope):
            def sb(name, shape, dt=F32):
                return scope.enter_context(nc.sbuf_tensor(name, shape, dt))
            return sb

        sb = make(stack)

        def sem(name):
            return stack.enter_context(nc.semaphore(name))

        bank = [stack.enter_context(nc.psum_tensor(f"bank{i}", [P, 512], F32)) for i in range(8)]
        a_bank, st_bank, o_bank, z_bank, small_bank = bank[0:2], bank[2:4], bank[4], bank[5], bank[6:8]
        t_bank, y_bank, h_bank = bank[0:2], bank[2:4], bank[4:8]

        ident = sb("ident", [P, P])
        xr = sb("xr", [P, T, ROW])
        b1T = sb("b1T", [P, E * FC])
        tok_store = sb("tok_store", [P, J], I32)
        tok_load = sb("tok_load", [P, J], I32)
        past = sb("past", [1, 2, E])
        bits = sb("bits", [1, 2, E])
        code = sb("code", [1, 1])
        warm = sb("warm", [P, 1])
        more = sb("more", [1, 1], I32)
        w1_sb = [sb("w1_sb0", [P, KC, F])]
        w2_sb = [sb("w2_sb0", [P, FC, D])]

        attention = ExitStack()
        sa = make(attention)
        qs = [sa(f"qs{i}", [P, G, CH], F32R) for i in range(2)]
        ks_main = [sa(f"ks_main{b}", [P, G, 2, P], F32R) for b in range(B)]
        ks_rest = [sa(f"ks_rest{b}", [P, G, P], F32R) for b in range(B)]
        kd_hi = sa("kd_hi", [P, KC, HH, MP], F32R)
        pt = sa("pt", [P, UN, CH])
        identb = sa("identb", [P, P], BF16)
        onesb = sa("onesb", [P, P], BF16)
        trib = sa("trib", [P, P], BF16)
        wq_sb = sa("wq_sb", [P, KC, D])
        wkv_sb = sa("wkv_sb", [P, KC, 2 * D])
        wp_sb = sa("wp_sb", [P, KC, D])
        bp_sb = sa("bp_sb", [P, D])
        r_sb = sa("r_sb", [E, D])
        rT = sa("rT", [P, KC, E])
        b1_sb = sa("b1_sb", [E * FC, P])
        headsel = sa("headsel", [P, HH])
        pairsel = sa("pairsel", [P, 2, P])
        z_main = sa("z_main", [P, 2, RP])
        z_rest = sa("z_rest", [P, 2, RP])
        zero = sa("zero", [P, 1])
        neghalf = sa("neghalf", [P, TT])
        lane = sa("lane", [P, P])
        part = sa("part", [P, 1])
        tilefirst = sa("tilefirst", [P, T, J])
        first = sa("first", [P, TT, E])
        ebase = sa("ebase", [P, T, E])

        ctx_sb = sa("ctx_sb", [P, B, 2, D])
        ctxT = sa("ctxT", [P, KC, MP])
        k_hi = sa("k_hi", [P, KC, MP], F32R)
        k_lo = sa("k_lo", [P, KC, MP], F32R)
        v_main = [sa(f"v_main{b}", [P, H, RP]) for b in range(B)]
        v_rest = [sa(f"v_rest{b}", [P, H // 4, 2, RP]) for b in range(B)]
        mask_sb = sa("mask_sb", [P, T, M], U8)
        negm = sa("negm", [P, T, P + 4 * RP], BF16)
        maskT = [sa(f"maskT{i}", [P, 2, CH], BF16) for i in range(2)]
        stats = sa("stats", [P, TT, 6])
        mv = sa("mv", [P, TT, 2])
        var = sa("var", [P, TT])
        rstd = sa("rstd", [P, TT])
        var2 = sa("var2", [P, TT])
        xn = sa("xn", [P, TT, D])
        xT = sa("xT", [P, KC, CH])
        q_hi = [sa(f"q_hi{i}", [P, KC, CH], F32R) for i in range(2)]
        q_lo = sa("q_lo", [P, KC, CH], F32R)
        mx = sa("mx", [P, TT, H])
        mxr = sa("mxr", [P, TT, H])
        mxx = sa("mxx", [P, TT, H])
        nmT = sa("nmT", [H, CH], F32R)
        rz = sa("rz", [P, CH])
        att = sa("att", [P, KC, CH])
        xn2 = sa("xn2", [P, 2, D])
        xn2T = sa("xn2T", [P, TT, KC, P])

        lg = sa("lg", [P, TT, E])
        lmax = sa("lmax", [P, TT])
        below = sa("below", [P, TT, E])
        lex = sa("lex", [P, TT, E])
        lsum = sa("lsum", [P, TT])
        rank = sa("rank", [P, TT, E])
        best = sa("best", [P, TT])
        onehot = sa("onehot", [P, T, E], BF16)
        count = sa("count", [P, E])
        before = sa("before", [P, NCH - 1, E], BF16)
        cum = sa("cum", [P, T, E])
        ebs = sa("ebs", [P, T, E])
        pos = sa("pos", [P, T])
        jslot = sa("jslot", [P, T])
        over = sa("over", [P, T, JT])
        spare = negm[:, :, :].rearrange("p t m -> p (t m)")
        psel = spare[:, 0:T * P].rearrange("p (t m) -> p t m", t=T)
        what = spare[:, T * P:T * (P + 2 * J)].rearrange("p (t c j) -> p t c j", t=T, c=2)
        jsel = spare[:, T * (P + 2 * J):T * (P + 3 * J)].rearrange("p (t j) -> p t j", t=T)
        attention.close()

        w1_hi, w1_lo, w2_hi, w2_lo = [], [], [], []
        for s_ in range(2):
            w1_hi.append(sb(f"w1_hi{s_}", [P, KC, F], F32R))
            w1_lo.append(sb(f"w1_lo{s_}", [P, KC, F], F32R))
            w2_hi.append(sb(f"w2_hi{s_}", [P, FC, D], F32R))
            w2_lo.append(sb(f"w2_lo{s_}", [P, FC, D], F32R))
            if s_ == 0:
                w1_sb.append(sb("w1_sb1", [P, KC, F]))
                w2_sb.append(sb("w2_sb1", [P, FC, D]))
        xg = sb("xg", [P, J, ROW])
        b2_sb = sb("b2_sb", [P, E, D])
        gn = sb("gn", [P, 2, JT, D])
        gT_hi = sb("gT_hi", [P, 2, KC, CAP], F32R)
        gT_lo = sb("gT_lo", [P, 2, KC, CAP], F32R)
        h32 = sb("h32", [P, 2, CAP])
        h_hi = sb("h_hi", [P, FC, CAP], F32R)
        h_lo = sb("h_lo", [P, FC, CAP], F32R)
        y1 = sb("y1", [P, JT, D])

        l_x = [sem(f"l_x{c}") for c in range(NCH)]
        l_ctx, l_wkv, l_wq, l_mask, l_small = sem("l_ctx"), sem("l_wkv"), sem("l_wq"), sem("l_mask"), sem("l_small")
        l_ks = [sem(f"l_ks{b}") for b in range(B)]
        l_qs = [sem(f"l_qs{i}") for i in range(2)]
        l_max = [sem(f"l_max{i}") for i in range(2)]
        l_qd, l_kd = sem("l_qd"), sem("l_kd")
        l_rows, l_out, l_b2 = sem("l_rows"), sem("l_out"), sem("l_b2")
        l_w1 = [sem(f"l_w1_{s}") for s in range(2)]
        l_w2 = [sem(f"l_w2_{s}") for s in range(2)]
        l_first = [sem(f"l_first{j}") for j in range(JT)]
        l_gather = [sem(f"l_gather{s}") for s in range(2)]
        l_store = [sem(f"l_store{j}") for j in range(JT)]
        pool_step, dve_step = sem("pool_step"), sem("dve_step")
        consts_made, mask_made, xn_made, rstd_made, xb_made, keys_zeroed, maxima_zeroed, std_made = (
            sem("consts_made"), sem("mask_made"), sem("xn_made"), sem("rstd_made"), sem("xb_made"), sem("keys_zeroed"),
            sem("maxima_zeroed"), sem("std_made"))
        small_full, small_act, small_dve = sem("small_full"), sem("small_act"), sem("small_dve")
        scan_full, scan_read = sem("scan_full"), sem("scan_read")
        st_full, exp_done, pv_done, att_made = sem("st_full"), sem("exp_done"), sem("pv_done"), sem("att_made")
        stats_made, qhi_made, qlo_made, khi_made, kdhi_made, klo_made = (
            sem("stats_made"), sem("qhi_made"), sem("qlo_made"), sem("khi_made"), sem("kdhi_made"), sem("klo_made"))
        values_zeroed, sel_made, max_made, x1_made, xn2_made = sem("values_zeroed"), sem("sel_made"), sem("max_made"), sem("x1_made"), sem("xn2_made")
        below_made, lex_made, gate_made, onehot_made, before_made, what_made, slots_full, tok_made, more_made = (
            sem("below_made"), sem("lex_made"), sem("gate_made"), sem("onehot_made"), sem("before_made"), sem("what_made"), sem("slots_full"), sem("tok_made"), sem("more_made"))
        gn_made, t_full, gT_made = sem("gn_made"), sem("t_full"), sem("gT_made")
        w1hi_made, w1lo_made, w2hi_made, w2lo_made, hlo_made, gTlo_made = (
            sem("w1hi_made"), sem("w1lo_made"), sem("w2hi_made"), sem("w2lo_made"), sem("hlo_made"), sem("gTlo_made"))
        h_full, h_made, y_full, y_read, y_made = sem("h_full"), sem("h_made"), sem("y_full"), sem("y_read"), sem("y_made")

        def unit_of(u):
            return (u // 4, u % 4) if u < 8 else (None, u - 8)

        def pv_batch_of(u):
            return min(u // 4, 2)

        def act_count(name):
            return sum(who == "act" for _, who in jobs[:job_at[name] + 1])

        def dve_count(name):
            return sum(who == "dve" for _, who in jobs[:job_at[name] + 1])

        def small(name):
            return small_bank[job_at[name] % 2]

        def scan_bank(c, n):
            return bank[n % 4] if c == 0 else a_bank[n % 2]

        def turned_aps(t, s, part_, js):
            return (t[:, s, :, js[0] * P:(js[-1] + 1) * P].rearrange("p k (j n) -> p j k n", n=P),
                    t_bank[part_][:, 0:len(js) * D].rearrange("p (j k n) -> p j k n", k=KC, n=P))

        block = stack.enter_context(nc.Block())

        @block.sync
        def _(sp):
            def load_x(c):
                sp.dma_start(xr[:, c * TT:(c + 1) * TT, 0:D], x_t[:, c * TT:(c + 1) * TT, :]).then_inc(l_x[c], 16)

            def keys(b):
                for part_, (k_, made) in enumerate(((k_hi, khi_made), (k_lo, klo_made))):
                    sp.wait_ge(made, KC * (b + 1))
                    sp.dma_start(k_dram[b, part_].rearrange("(k p) m -> p k m", p=P), k_[:, :, :].bitcast(F32)).then_inc(l_kd, 16)
                sp.wait_ge(keys_zeroed, b + 1)
                sp.wait_ge(l_kd, 32 * (b + 1))
                for blk, part_ in enumerate((0, 0, 1)):
                    src = k_dram[b, part_].rearrange("(g a r) m -> a r g m", a=2, r=DH)
                    for a in range(2):
                        to = slice(32 * blk + DH * a, 32 * blk + DH * (a + 1))
                        sp.dma_start(ks_main[b][to, :, a, :].bitcast(F32), src[a, :, :, 0:P]).then_inc(l_ks[b], 16)
                        for odd in range(2):
                            c0 = 2 * RP * odd + RP * a
                            sp.dma_start(ks_rest[b][to, odd:G:2, c0:c0 + RP].bitcast(F32),
                                         src[a, :, odd:G:2, P:MP]).then_inc(l_ks[b], 16)

            def proj(c):
                sp.wait_ge(qhi_made, KC * (c + 1))
                if c >= 2:
                    sp.wait_ge(l_qs[c % 2], QS_DMAS * (c // 2))
                sp.dma_start(q_dram[c % 2, 0].rearrange("(k p) n -> p k n", p=P), q_hi[c % 2][:, :, :].bitcast(F32)).then_inc(l_qd, 16)
                sp.wait_ge(qlo_made, KC * (c + 1))
                sp.dma_start(q_dram[c % 2, 1].rearrange("(k p) n -> p k n", p=P), q_lo[:, :, :].bitcast(F32)).then_inc(l_qd, 16)
                if c >= 2:
                    sp.wait_ge(st_full, 2 * UN * (c - 1))
                sp.wait_ge(l_qd, 32 * (c + 1))
                for blk, part_ in enumerate((0, 1, 0)):
                    sp.dma_start(qs[c % 2][32 * blk:32 * blk + 32, :, :].bitcast(F32),
                                 q_dram[c % 2, part_].rearrange("(g r) n -> r g n", r=32)).then_inc(l_qs[c % 2], 16)

            def maxima(c):
                sp.wait_ge(small_act, act_count(("max", c)))
                if c < 2:
                    sp.wait_ge(maxima_zeroed, c + 1)
                if c >= 2:
                    sp.wait_ge(st_full, 2 * UN * (c - 1))
                for a in range(2):
                    sp.dma_start(qs[c % 2][96 + a:97 + a, :, :].bitcast(F32), nmT[a:H:2, :].bitcast(F32)).then_inc(l_max[c % 2], 16)

            def store_rows(c):
                sp.wait_ge(gate_made, c + 1)
                sl = slice(c * TT, (c + 1) * TT)
                sp.dma_start(rows_t[:, sl, :], xr[:, sl, :]).then_inc(l_rows, 16)
                sp.dma_start(out_t[:, sl, :], xr[:, sl, 0:D]).then_inc(l_out, 16)

            def load_w1(e, s):
                e_ = bass.ds(e, 1) if not isinstance(e, int) else slice(e, e + 1)
                sp.dma_start(w1_sb[s][:, :, :], w1[e_].rearrange("e (k p) f -> p (e k) f", p=P)).then_inc(l_w1[s], 16)

            def load_w2(e, s):
                e_ = bass.ds(e, 1) if not isinstance(e, int) else slice(e, e + 1)
                sp.dma_start(w2_sb[s][:, :, :], w2[e_].rearrange("e (k p) d -> p (e k) d", p=P)).then_inc(l_w2[s], 16)

            load_x(0)
            sp.dma_start(ctx_sb[:, :, 0, :], ctx[:, 0:P, :].rearrange("b p d -> p b d")).then_inc(l_ctx, 16)
            sp.dma_start(ctx_sb[0:MR, :, 1, :], ctx[:, P:M, :].rearrange("b p d -> p b d")).then_inc(l_ctx, 16)
            sp.dma_start(wkv_sb[:, :, :], wkv.rearrange("(k p) d -> p k d", p=P)).then_inc(l_wkv, 16)
            sp.dma_start(wq_sb[:, :, :], wq.rearrange("(k p) d -> p k d", p=P)).then_inc(l_wq, 16)
            sp.dma_start(mask_sb[:, :, :], mask_t).then_inc(l_mask, 16)
            load_x(1)
            sp.dma_start(wp_sb[:, :, :], wproj.rearrange("(k p) d -> p k d", p=P)).then_inc(l_small, 16)
            sp.dma_start(bp_sb[:, :], bproj.rearrange("(a d) -> a d", a=1).to_broadcast([P, D])).then_inc(l_small, 16)
            sp.dma_start(r_sb[:, :], router).then_inc(l_small, 16)
            sp.dma_start(b1_sb[:, :], b1.rearrange("e (f p) -> (e f) p", p=P)).then_inc(l_small, 16)
            load_x(2)
            load_x(3)
            for stage, c in STAGES:
                if stage == "keys":
                    keys(c)
                if stage == "proj":
                    proj(c)
                if stage == "scan":
                    maxima(c)
                if stage == "mix":
                    if c:
                        store_rows(c - 1)
                    else:
                        load_w1(0, 0)
                        load_w2(0, 0)
                    if c < NCH - 1:
                        maxima(c + 1)
                    if c == 0:
                        keys(1)
                    if c < 2:
                        proj(c + 2)
                if stage == "split":
                    sp.wait_ge(st_full, 2 * UN * NCH)
                    sp.wait_ge(pv_done, 3 * 2 * NCH)
                    load_w1(1, 1)
                    load_w2(1, 1)
                if stage == "tail":
                    store_rows(c)
            sp.wait_ge(tok_made, 1)
            sp.wait_ge(l_first[JT - 1], 16)
            sp.dma_start(b2_sb[:, :, :], b2.rearrange("(a e) d -> a e d", a=1).to_broadcast([P, E, D])).then_inc(l_b2, 16)
            with sp.Fori(1, E // 2) as it:
                for s in range(2):
                    sp.wait_ge(w1lo_made, (it * 2 + (s - 1)) * 4)
                    load_w1(it * 2 + s, s)
                    sp.wait_ge(w2lo_made, it * 2 + (s - 1))
                    load_w2(it * 2 + s, s)

        @block.gpsimd
        def _(pool):
            steps = Count(pool, pool_step)
            p = nc.gpsimd

            def make_consts():
                steps.up(p.memset(ident[:, :], 0.0))
                steps.up(p.memset(neghalf[:, :], -0.5))
                steps.up(p.memset(zero[:, :], 0.0))
                steps.settle()
                steps.up(p.affine_select(out=ident[:, :], in_=ident[:, :], compare_op=ALU.not_equal, fill=1.0,
                                         base=0, pattern=[[-1, P]], channel_multiplier=1))
                steps.up(p.memset(ctxT[:, :, M:MP], 0.0))
                steps.up(p.memset(headsel[:, :], 1.0))
                steps.settle()
                steps.up(p.affine_select(out=headsel[:, :], in_=headsel[:, :], compare_op=ALU.is_ge, fill=0.0,
                                         base=0, pattern=[[-DH, HH]], channel_multiplier=1))
                steps.settle()
                steps.up(p.affine_select(out=headsel[:, :], in_=headsel[:, :], compare_op=ALU.is_ge, fill=0.0,
                                         base=DH - 1, pattern=[[DH, HH]], channel_multiplier=-1))
                steps.up(p.tensor_copy(identb[:, :], ident[:, :]))
                steps.settle()
                p.memset(var2[:, :], 0.0).then_inc(consts_made, 1)

            def zero_keys(b):
                p.memset(ks_main[b][:, :, :, :].bitcast(F32), 0.0)
                p.memset(ks_rest[b][:, :, :].bitcast(F32), 0.0).then_inc(keys_zeroed, 1)

            def make_more_consts():
                steps.up(p.memset(onesb[:, :], 1.0))
                steps.up(p.memset(pairsel[:, :, :], 1.0))
                steps.settle()
                steps.up(p.affine_select(out=trib[:, :], in_=onesb[:, :], compare_op=ALU.is_ge, fill=0.0,
                                         base=-1, pattern=[[1, P]], channel_multiplier=-1))
                steps.up(p.affine_select(out=pairsel[:, :, :], in_=pairsel[:, :, :], compare_op=ALU.is_equal, fill=0.0,
                                         base=-96, pattern=[[-1, 2], [0, P]], channel_multiplier=1))
                steps.settle()
                for t in (z_main, z_rest):
                    steps.up(p.memset(t[:, :, :], 0.0))
                steps.settle()
                for a in range(2):
                    steps.up(p.memset(z_main[:, a, DH * a:DH * a + DH], 1.0))
                for i in range(4):
                    steps.settle()
                    steps.up(p.memset(z_rest[32 * i:32 * i + MR + 1, i // 2, DH * (i % 2):DH * (i % 2) + DH], 1.0))
                steps.settle()
                p.memset(var2[:, :], 0.0).then_inc(consts_made, 1)

            def make_late_consts():
                steps.up(p.iota(lane[:, :], pattern=[[1, P]], base=0, channel_multiplier=0,
                                allow_small_or_imprecise_dtypes=True))
                steps.up(p.iota(part[:, :], pattern=[[0, 1]], base=0, channel_multiplier=1,
                                allow_small_or_imprecise_dtypes=True))
                steps.up(p.iota(tilefirst[:, :, :], pattern=[[P, T], [0, J]], base=-int(FAR), channel_multiplier=0,
                                allow_small_or_imprecise_dtypes=True))
                steps.up(p.iota(first[:, :, :], pattern=[[0, TT], [-1, E]], base=E, channel_multiplier=0,
                                allow_small_or_imprecise_dtypes=True))
                steps.up(p.iota(ebase[:, :, :], pattern=[[0, T], [JT, E]], base=0, channel_multiplier=0,
                                allow_small_or_imprecise_dtypes=True))
                for e in range(E):
                    steps.up(p.memset(bits[:, :, e:e + 1], float(4 ** e)))
                steps.up(p.memset(xr[:, :, D + 2:ROW], 0.0))
                steps.settle()
                p.memset(var2[:, :], 0.0).then_inc(consts_made, 1)

            def make_mask(c):
                sl = slice(c * TT, (c + 1) * TT)
                if c == 0:
                    pool.wait_ge(l_mask, 16)
                p.tensor_scalar(negm[:, sl, 0:P], mask_sb[:, sl, 0:P], NEG, None, ALU.mult)
                for i in range(4):
                    ins = p.tensor_scalar(negm[:, sl, P + RP * i:P + RP * i + MR], mask_sb[:, sl, P:M], NEG, None, ALU.mult)
                ins.then_inc(mask_made, 1)

            def stats_(c):
                pool.wait_ge(stats_made, c + 1)
                steps.up(p.tensor_scalar(var[:, :], mv[:, :, 1], EPS, None, ALU.add))
                steps.settle()
                p.tensor_tensor(rstd[:, :], var[:, :], neghalf[:, :], ALU.pow).then_inc(std_made, 1)
                if c == 0:
                    steps.up(p.memset(negm[:, :, P:], 0.0))
                    steps.settle()
                    make_mask(0)

            def norm(c):
                if c == 1:
                    make_more_consts()
                    make_mask(1)
                    zero_keys(1)
                    pool.wait_ge(l_small, 64)
                for cc in {0: [], 1: [0, 1], 2: [2], 3: [3]}[c]:
                    pool.wait_ge(xn_made, cc + 1)
                    for t in range(cc * TT, (cc + 1) * TT):
                        ins = p.tensor_tensor(xr[:, t, 0:D], xr[:, t, 0:D], bp_sb[:, :], ALU.add)
                    ins.then_inc(xb_made, 1)
                if c in (1, 2):
                    make_mask(c + 1)

            def std_x1(c, t):
                first_, last_ = (0, TT) if t is None else (t, t + 1)
                pool.wait_ge(x1_made, c * TT + last_)
                sl = slice(c * TT + first_, c * TT + last_)
                steps.up(p.tensor_scalar(var2[:, first_:last_], xr[:, sl, D + 1], EPS, None, ALU.add))
                steps.settle()
                p.tensor_tensor(xr[:, sl, D + 1], var2[:, first_:last_], neghalf[:, first_:last_], ALU.pow).then_inc(rstd_made, last_ - first_)

            def run(list_):
                for step, c, i in list_:
                    if step == "stats":
                        stats_(c)
                    if step == "norm":
                        norm(c)
                    if step == "std":
                        std_x1(c, i)

            make_consts()
            zero_keys(0)
            for stage, c in STAGES:
                if stage == "stats":
                    stats_(c)
                if stage == "norm":
                    norm(c)
                if stage == "scan":
                    run(scan_steps())
                    make_late_consts()
                if stage == "mix":
                    run(mix_steps(c))
                if stage == "tail":
                    run(tail_steps(c))

            pool.wait_ge(tok_made, 1)
            pool.wait_ge(l_rows, 16 * NCH)

            def low2(e):
                pool.wait_ge(w2hi_made, e + 1)
                p.tensor_tensor(w2_lo[e % 2][:, :, :], w2_sb[e % 2][:, :, :], w2_hi[e % 2][:, :, :].bitcast(F32),
                                ALU.subtract).then_inc(w2lo_made, 1)

            def gather(e):
                if e >= 4 or e == 3:
                    pool.wait_ge(l_gather[e % 2], 16 * JT * ((e - 1) // 2 if e % 2 == 0 else e // 2))
                for j in range(JT * e, JT * (e + 1)):
                    p.indirect_dma_start(xg[:, j, :], None, rows, bass.IndirectOffsetOnAxis(ap=tok_load[:, j:j + 1], axis=0),
                                         bounds_check=NTOK - 1, oob_is_err=False).then_inc(l_gather[e % 2] if e else l_first[j], 16)

            gather(0)
            gather(1)
            pool.wait_ge(l_out, 16 * NCH)
            for e in range(E):
                if e + 2 < E:
                    gather(e + 2)
                if e + 1 < E:
                    low2(e + 1)
                for j in range(JT):
                    pool.wait_ge(y_made, JT * (e + 1) + j + 1)
                    p.indirect_dma_start(out_rows, bass.IndirectOffsetOnAxis(ap=tok_store[:, JT * e + j:JT * e + j + 1], axis=0),
                                         xg[:, JT * e + j, 0:D], None, bounds_check=NTOK - 1, oob_is_err=False).then_inc(l_store[j], 16)
            for j in range(JT):
                pool.wait_ge(l_store[j], 16 * E)

        @block.tensor
        def _(pe):
            mm, tr = nc.tensor.matmul, nc.tensor.transpose

            def open_small(name):
                n = job_at[name]
                if n >= 2:
                    before = jobs[n - 2][0]
                    if jobs[n - 2][1] == "act":
                        pe.wait_ge(small_act, act_count(before))
                    else:
                        pe.wait_ge(small_dve, dve_count(before))
                return small(name)

            def turn_x(c):
                pe.wait_ge(xn_made, c + 1)
                if c == 0:
                    pe.wait_ge(consts_made, 1)
                for k in range(KC):
                    ps = open_small(("xT", c, k))
                    for t in range(TT):
                        ins = tr(ps[:, t * P:(t + 1) * P], xn[:, t, k * P:(k + 1) * P], ident[:, :])
                    ins.then_inc(small_full, 1)

            def proj(c):
                if c == 0:
                    pe.wait_ge(l_wq, 16)
                pe.wait_ge(small_act, act_count(("xT", c, KC - 1)))
                for half in range(KC):
                    ps = open_small(("q", c, half))
                    for k in range(KC):
                        ins = mm(ps[:, :], wq_sb[:, k, half * P:(half + 1) * P], xT[:, k, :], start=(k == 0), stop=(k == KC - 1))
                    ins.then_inc(small_full, 1)

            def keys(b):
                if b == 0:
                    pe.wait_ge(l_ctx, 32)
                    pe.wait_ge(consts_made, 1)
                ps = open_small(("ctxT", b))
                for k in range(KC):
                    tr(ps[:, k * MP:k * MP + P], ctx_sb[:, b, 0, k * P:(k + 1) * P], ident[:, :])
                    ins = tr(ps[:, k * MP + P:k * MP + M], ctx_sb[0:MR, b, 1, k * P:(k + 1) * P], ident[0:MR, 0:MR])
                ins.then_inc(small_full, 1)
                if b == 0:
                    pe.wait_ge(l_wkv, 16)
                pe.wait_ge(small_act, act_count(("ctxT", b)))
                for half in range(KC):
                    ps = open_small(("k", b, half))
                    for k in range(KC):
                        ins = mm(ps[:, 0:MP], wkv_sb[:, k, half * P:(half + 1) * P], ctxT[:, k, :], start=(k == 0), stop=(k == KC - 1))
                    ins.then_inc(small_full, 1)
                ps = open_small(("v", b))
                for k in range(KC):
                    ins = mm(ps[:, 0:D], ctxT[:, k, 0:P], wkv_sb[:, k, D:2 * D], start=(k == 0), stop=(k == KC - 1))
                ins.then_inc(small_full, 1)
                ps = open_small(("vr", b))
                for k in range(KC):
                    ins = mm(ps[0:RP, 0:D], ctxT[:, k, P:MP], wkv_sb[:, k, D:2 * D], start=(k == 0), stop=(k == KC - 1))
                ins.then_inc(small_full, 1)

            def turn_mask(c):
                pe.wait_ge(mask_made, c + 1)
                ps = open_small(("maskT", c))[:, :].bitcast(BF16)
                for t in range(TT):
                    for r in range(2):
                        ins = tr(ps[:, r * CH + t * P:r * CH + (t + 1) * P], negm[:, c * TT + t, r * P:(r + 1) * P], identb[:, :])
                ins.then_inc(small_full, 1)

            def scan(c, i):
                t, u = divmod(i, AU)
                n = c * TT * AU + i
                if i == 0:
                    pe.wait_ge(qhi_made, KC * (c + 1))
                    pe.wait_ge(kdhi_made, KC * (c // PER_B + 1))
                    pe.wait_ge(mask_made, c + 1)
                if c == 0 and n >= 4:
                    pe.wait_ge(scan_read, n - 3)
                if c:
                    pe.wait_ge(scan_read, n - 1)
                ps = scan_bank(c, n)
                tok_ = slice(t * P, (t + 1) * P)
                if u < 4:
                    half, h4 = divmod(u, 2)
                    m_ = negm[:, c * TT + t, 0:P].unsqueeze(1).to_broadcast([P, 4, P])
                    mm(ps[:, :], identb[:, :], m_, start=True, stop=False)
                    ins = mm(ps[:, :], q_hi[c % 2][:, half, tok_], kd_hi[:, half, 4 * h4:4 * h4 + 4, 0:P], start=False, stop=True)
                else:
                    m_ = negm[:, c * TT + t, P:MP].unsqueeze(1).to_broadcast([P, H, RP])
                    mm(ps[:, :], identb[:, :], m_, start=True, stop=False)
                    for half in range(KC):
                        ins = mm(ps[:, half * HH * RP:(half + 1) * HH * RP], q_hi[c % 2][:, half, tok_],
                                 kd_hi[:, half, :, P:MP], start=False, stop=(half == KC - 1))
                ins.then_inc(scan_full, 1)

            def maxima(c):
                pe.wait_ge(max_made, c + 1)
                ps = open_small(("max", c))
                for t in range(TT):
                    ins = tr(ps[0:H, t * P:(t + 1) * P], mxx[:, t, :], ident[:, :])
                ins.then_inc(small_full, 1)

            def scores(c, i):
                b, n = c // PER_B, 2 * UN * c + i
                half, u = divmod(i, UN)
                a, pair = unit_of(u)
                if i == 0:
                    pe.wait_ge(l_qs[c % 2], QS_DMAS * (c // 2 + 1))
                    pe.wait_ge(l_max[c % 2], 32 * (c // 2 + 1))
                    pe.wait_ge(small_act, act_count(("maskT", c)))
                    if c == 0:
                        pe.wait_ge(consts_made, 2)
                    if c % PER_B == 0:
                        pe.wait_ge(l_ks[b], KS_DMAS)
                        pe.wait_ge(sel_made, b + 1)
                if n == 0:
                    pe.wait_ge(scan_read, TT * AU)
                if n >= 2:
                    pe.wait_ge(exp_done, n - 1)
                ps = st_bank[n % 2]
                mm(ps[:, :], identb[:, :], maskT[c % 2][:, 0 if a is not None else 1, :], start=True, stop=False)
                if a is not None:
                    g = half * (G // KC) + pair
                    ins = mm(ps[:, :], ks_main[b][:, g, a, :], qs[c % 2][:, g, :], start=False, stop=True)
                else:
                    for k in range(2):
                        g = half * (G // KC) + 2 * pair + k
                        ins = mm(ps[:, :], ks_rest[b][:, g, :], qs[c % 2][:, g, :], start=False, stop=(k == 1))
                ins.then_inc(st_full, 1)

            def values(c, half, batch):
                b, hf = c // PER_B, 2 * c + half
                pe.wait_ge(exp_done, UN * hf + (4, 8, 10)[batch])
                if batch == 0:
                    if hf:
                        pe.wait_ge(att_made, TT * hf)
                    if c % PER_B == 0 and half == 0:
                        pe.wait_ge(small_act, act_count(("vr", b)))
                for ps, main, rest in ((o_bank, v_main[b], v_rest[b]), (z_bank, None, None)):
                    for pair in range(G // KC):
                        rows_ = ps[32 * pair:32 * pair + 32, :]
                        if batch < 2:
                            h = half * HH + 2 * pair + batch
                            w = z_main[:, batch, :] if main is None else main[:, h, :]
                            ins = mm(rows_, w, pt[:, (UN * hf + 4 * batch + pair) % UN, :], start=(batch == 0), stop=False,
                                     skip_group_check=True)
                        else:
                            r = pair // 2
                            w = z_rest[:, pair % 2, :] if rest is None else rest[:, half * 2 + r, pair % 2, :]
                            ins = mm(rows_, w, pt[:, (UN * hf + 8 + r) % UN, :], start=False, stop=True, skip_group_check=True)
                ins.then_inc(pv_done, 1)

            def turn_row(c, t):
                pe.wait_ge(xn2_made, c * TT + t + 1)
                ps = open_small(("nT", c, t))
                for k in range(KC):
                    ins = tr(ps[:, k * P:(k + 1) * P], xn2[:, t % 2, k * P:(k + 1) * P], ident[:, :])
                ins.then_inc(small_full, 1)

            def logits(c, t):
                pe.wait_ge(small_act, act_count(("nT", c, t)))
                ps = open_small(("logits", c, t))
                for k in range(KC):
                    ins = mm(ps[:, 0:E], xn2T[:, t, k, :], rT[:, k, :], start=(k == 0), stop=(k == KC - 1))
                ins.then_inc(small_full, 1)

            def fold(c, t):
                pe.wait_ge(att_made, TT * (2 * c + 1) + t + 1)
                if c == 0 and t == 0:
                    pe.wait_ge(l_small, 64)
                ps = open_small(("fold", c, t))
                for k in range(KC):
                    ins = mm(ps[:, 0:D], att[:, k, t * P:(t + 1) * P], wp_sb[:, k, :], start=(k == 0), stop=(k == KC - 1))
                ins.then_inc(small_full, 1)

            def run(steps):
                for step, c, i in steps:
                    if step == "scores":
                        scores(c, i)
                    if step == "turn":
                        turn_x(c)
                    if step == "proj":
                        proj(c)
                    if step == "mask":
                        turn_mask(c)
                    if step == "keys":
                        keys(c)
                    if step == "small":
                        turn_small()
                    if step == "place":
                        place(c)
                    if step == "slot":
                        slot(c)
                    if step == "scan":
                        scan(c, i)
                    if step == "fold":
                        fold(c, i)
                    if step == "nT":
                        turn_row(c, i)
                    if step == "logits":
                        logits(c, i)
                    if step == "values":
                        values(c, *i)
                    if step == "max":
                        maxima(c)

            def turn_small():
                pe.wait_ge(l_small, 64)
                ps = open_small(("rT",))
                for k in range(KC):
                    ins = tr(ps[:, k * E:(k + 1) * E], r_sb[:, k * P:(k + 1) * P], ident[0:E, 0:E])
                ins.then_inc(small_full, 1)
                ps = open_small(("b1T",))
                tr(ps[:, 0:E * FC], b1_sb[:, :], ident[0:E * FC, 0:E * FC]).then_inc(small_full, 1)

            def place(c):
                pe.wait_ge(onehot_made, c + 1)
                if c:
                    pe.wait_ge(before_made, c)
                ps = open_small(("place", c, 0))
                t0, width = c * TT, TT * E
                terms = [(trib, onehot[:, t0:t0 + TT, :], 0)]
                if c:
                    terms.append((onesb, before[:, c - 1, :].unsqueeze(1).to_broadcast([P, TT, E]), 0))
                for t in range(TT - 1):
                    terms.append((onesb, onehot[:, t0 + t, :].unsqueeze(1).to_broadcast([P, TT - 1 - t, E]), t + 1))
                for n, (w, which, t) in enumerate(terms):
                    ins = mm(ps[:, t * E:width], w[:, :], which, start=(n == 0), stop=(n == len(terms) - 1), skip_group_check=True)
                ins.then_inc(small_full, 1)

            def slot(c):
                if c == 0:
                    pe.wait_ge(scan_read, TT * AU * NCH)
                if c == NCH - 1:
                    for n, which in enumerate([before[:, c - 1, :]] + [onehot[:, c * TT + t, :] for t in range(TT)]):
                        mm(a_bank[1][:, 0:E], onesb[:, :], which, start=(n == 0), stop=(n == TT))
                pe.wait_ge(what_made, c + 1)
                for t in range(c * TT, (c + 1) * TT):
                    for k in range(2):
                        ins = mm(a_bank[0][:, 0:J], psel[:, t, :], what[:, t, k, :], start=(t == 0 and k == 0),
                                 stop=(t == T - 1 and k == 1), skip_group_check=True)
                if c == NCH - 1:
                    ins.then_inc(slots_full, 1)

            for stage, c in STAGES:
                if stage == "turn":
                    turn_x(c)
                if stage == "proj":
                    proj(c)
                if stage == "keys":
                    keys(c)
                if stage == "mask":
                    turn_mask(c)
                if stage == "scan":
                    run(scan_steps())
                if stage == "mix":
                    run(mix_steps(c))
                if stage == "tail":
                    run(tail_steps(c))

            def turn(e, s):
                for part_, js in enumerate(TURNS):
                    pe.wait_ge(gn_made, JT * e + (js[-1] + 1))
                    pe.wait_ge(gTlo_made, len(TURNS) * e + (part_ + 1))
                    for j in js:
                        for k in range(KC):
                            c0 = (j - js[0]) * D + k * P
                            ins = tr(t_bank[part_][:, c0:c0 + P], gn[:, s, j, k * P:(k + 1) * P], ident[:, :])
                    ins.then_inc(t_full, 1)

            def hidden(it, s, f, width):
                ps = h_bank[f % 4]
                chunk = slice(f * P, (f + 1) * P)
                n = 0
                for w_, g_ in ((w1_hi, gT_hi), (w1_hi, gT_lo), (w1_lo, gT_hi)):
                    for k in range(KC):
                        ins = mm(ps[:, 0:width], w_[s][:, k, chunk], g_[:, s, k, 0:width], start=(n == 0), stop=(n == 3 * KC - 1))
                        n += 1
                ins.then_inc(h_full, 1)

            def result(e, s, j):
                ps = y_bank[(JT * s + j) % 2]
                tile_ = slice(j * P, (j + 1) * P)
                n = 0
                for f in range(FC):
                    if j == 0:
                        pe.wait_ge(hlo_made, e * FC + (f + 3))
                    for h_, w_ in ((h_hi, w2_hi), (h_hi, w2_lo), (h_lo, w2_hi)):
                        ins = mm(ps[:, 0:D], h_[:, f, tile_], w_[s][:, f, :], start=(n == 0), stop=(n == 3 * FC - 1))
                        n += 1
                ins.then_inc(y_full, 1)

            def expert(it, s, left):
                e = it * 2 + s
                tiles = (tiles_code >> (e * 2)) & 3
                pe.wait_ge(gTlo_made, (e + 2) * len(TURNS))
                pe.wait_ge(w1lo_made, (e + 1) * 4)
                with pe.If(tiles > JT - 2):
                    for f in range(FC):
                        pe.wait_ge(h_made, e * FC + (f + 1))
                        hidden(it, s, f, CAP)
                with pe.Else():
                    for f in range(FC):
                        pe.wait_ge(h_made, e * FC + (f + 1))
                        hidden(it, s, f, CAP - P)
                pe.wait_ge(w2lo_made, e + 1)
                pe.wait_ge(y_read, e * JT + 1)
                result(e, s, 0)
                if left:
                    turn(e + 1, 1 - s)
                for j in range(1, JT):
                    pe.wait_ge(y_read, e * JT + (j + 1))
                    with pe.If(tiles > j - 1):
                        result(e, s, j)
                    with pe.Else():
                        pe.drain().then_inc(y_full, 1)

            pe.sem_inc(y_full, JT)
            pe.wait_ge(tok_made, 1)
            pe.wait_ge(more_made, 1)
            tiles_code = pe.value_load(more[0:1, 0:1], min_val=0, max_val=4 ** E - 1)
            turn(0, 0)
            with pe.Fori(0, E // 2 - 1) as it:
                
                expert(it, 0, 2)
                expert(it, 1, 2)
            expert(E // 2 - 1, 0, 1)
            expert(E // 2 - 1, 1, 0)

        @block.scalar
        def _(act):
            a = nc.scalar

            def full(name):
                act.wait_ge(small_full, job_at[name] + 1)
                return small(name)

            def turned_x(c):
                if c:
                    act.wait_ge(small_full, job_at[("q", c - 1, KC - 1)] + 1)
                for k in range(KC):
                    ps = full(("xT", c, k))
                    a.activation(xT[:, k, :], ps[:, :], ACT.Copy).then_inc(small_act, 1)

            def proj(c):
                for half in range(KC):
                    ps = full(("q", c, half))
                    if c >= 2 and half == 0:
                        act.wait_ge(scan_full, TT * AU * (c - 1))
                        act.wait_ge(l_qd, 32 * (c - 1))
                        act.wait_ge(qlo_made, KC * (c - 1))
                    a.activation(q_hi[c % 2][:, half, :], ps[:, :], ACT.Copy).then_inc(qhi_made, 1)

            def keys(b):
                ps = full(("ctxT", b))
                if b:
                    act.wait_ge(small_full, job_at[("vr", b - 1)] + 1)
                a.activation(ctxT[:, :, 0:M], ps[:, 0:KC * MP].rearrange("p (k m) -> p k m", k=KC)[:, :, 0:M],
                             ACT.Copy).then_inc(small_act, 1)
                for half in range(KC):
                    ps = full(("k", b, half))
                    if b:
                        act.wait_ge(kdhi_made, KC * b)
                        act.wait_ge(l_kd, 32 * b)
                    a.activation(k_hi[:, half, :], ps[:, 0:MP], ACT.Copy).then_inc(khi_made, 1)
                if b == 0:
                    act.wait_ge(values_zeroed, 1)
                ps = full(("v", b))
                to = v_main[b][:, :, :].rearrange("p (g a) c -> p g a c", a=2)
                src = ps[:, 0:D].rearrange("p (g a d) -> p g a d", a=2, d=DH)
                a.activation(to[:, :, 0, 0:DH], src[:, :, 0, :], ACT.Copy)
                a.activation(to[:, :, 1, DH:2 * DH], src[:, :, 1, :], ACT.Copy).then_inc(small_act, 1)
                ps = full(("vr", b))
                src = ps[0:RP, 0:D].rearrange("p (r i d) -> p r i d", i=4, d=DH)
                for i in range(4):
                    ins = a.activation(v_rest[b][32 * i:32 * i + 32, :, i // 2, DH * (i % 2):DH * (i % 2) + DH], src[:, :, i, :], ACT.Copy)
                ins.then_inc(small_act, 1)

            def turn_mask(c):
                ps = full(("maskT", c))
                if c >= 2:
                    act.wait_ge(st_full, 2 * UN * (c - 1))
                a.activation(maskT[c % 2][:, :, :].rearrange("p r n -> p (r n)"), ps[:, :].bitcast(BF16), ACT.Copy).then_inc(small_act, 1)

            def maxima(c):
                ps = full(("max", c))
                if c:
                    act.wait_ge(l_max[(c - 1) % 2], 32 * ((c - 1) // 2 + 1))
                a.activation(nmT[:, :], ps[0:H, :], ACT.Copy, scale=-1.0).then_inc(small_act, 1)

            def exponentials(c, i):
                n = 2 * UN * c + i
                hf, u = divmod(n, UN)
                act.wait_ge(st_full, n + 1)
                if hf:
                    act.wait_ge(pv_done, 3 * (hf - 1) + pv_batch_of(u) + 1)
                a.activation(pt[:, n % UN, :], st_bank[n % 2][:, :], ACT.Exp, scale=SCALE).then_inc(exp_done, 1)

            def turned_row(c, t):
                ps = full(("nT", c, t))
                if c:
                    act.wait_ge(small_full, job_at[("logits", c - 1, t)] + 1)
                a.activation(xn2T[:, t, :, :].rearrange("p k n -> p (k n)"), ps[:, 0:D], ACT.Copy).then_inc(small_act, 1)

            def likely(c):
                act.wait_ge(below_made, c + 1)
                a.activation(lex[:, :, :], below[:, :, :], ACT.Exp).then_inc(lex_made, 1)

            def run(steps):
                for step, c, i in steps:
                    if step == "scores":
                        exponentials(c, i)
                    if step == "turn":
                        turned_x(c)
                    if step == "proj":
                        proj(c)
                    if step == "mask":
                        turn_mask(c)
                    if step == "keys":
                        keys(c)
                    if step == "small":
                        ps = full(("rT",))
                        a.activation(rT[:, :, :].rearrange("p k e -> p (k e)"), ps[:, 0:KC * E], ACT.Copy).then_inc(small_act, 1)
                        ps = full(("b1T",))
                        a.activation(b1T[:, :], ps[:, 0:E * FC], ACT.Copy).then_inc(small_act, 1)
                    if step == "nT":
                        turned_row(c, i)
                    if step == "pick" and i == 1:
                        likely(c)
                    if step == "max":
                        maxima(c)

            def zero_maxima(i):
                a.activation(qs[i][96:P, :, :], zero[96:P, 0:1].unsqueeze(2).to_broadcast([P - 96, G, CH]), ACT.Copy).then_inc(maxima_zeroed, 1)

            act.wait_ge(consts_made, 1)
            zero_maxima(0)
            for stage, c in STAGES:
                if stage == "turn":
                    turned_x(c)
                if stage == "proj":
                    proj(c)
                    if c == 0:
                        zero_maxima(1)
                if stage == "keys":
                    keys(c)
                if stage == "mask":
                    turn_mask(c)
                if stage == "scan":
                    run(scan_steps())
                if stage == "mix":
                    run(mix_steps(c))
                if stage == "split":
                    act.wait_ge(l_w1[0], 16)
                    act.wait_ge(l_w2[0], 16)
                    act.wait_ge(st_full, 2 * UN * NCH)
                    act.wait_ge(pv_done, 3 * 2 * NCH)
                    a.activation(w1_hi[0][:, :, :], w1_sb[0][:, :, :], ACT.Copy).then_inc(w1hi_made, 1)
                    a.activation(w2_hi[0][:, :, :], w2_sb[0][:, :, :], ACT.Copy).then_inc(w2hi_made, 1)
                if stage == "tail":
                    run(tail_steps(c))
                    a.activation(warm[:, :], neghalf[:, 0:1], ACT.Gelu)

            def turned(e, s):
                for part_, js in enumerate(TURNS):
                    act.wait_ge(t_full, len(TURNS) * e + (part_ + 1))
                    if part_ == 0 and not (isinstance(e, int) and e == 0):
                        act.wait_ge(h_full, e * FC)
                    to, src = turned_aps(gT_hi, s, part_, js)
                    a.activation(to, src, ACT.Copy).then_inc(gT_made, 1)

            def expert(it, s, left):
                e = it * 2 + s
                tiles = (tiles_code >> (e * 2)) & 3
                with act.If(tiles > JT - 2):
                    gelus(e, CAP)
                with act.Else():
                    gelus(e, CAP - P)
                if left:
                    turned(e + 1, 1 - s)
                    act.wait_ge(l_w2[1 - s], (it + s) * 16 + 16)
                    act.wait_ge(y_full, (e + 1) * JT)
                    high2(1 - s)
                if left > 1:
                    act.wait_ge(l_w1[s], it * 16 + 32)
                    high1(s)

            def gelus(e, width):
                for f in range(FC):
                    act.wait_ge(h_full, e * FC + (f + 1))
                    act.wait_ge(hlo_made, e * FC + (f + 1))
                    b_ = b1T[:, bass.ds(e * FC + f, 1)] if not isinstance(e, int) else b1T[:, e * FC + f:e * FC + f + 1]
                    a.activation(h32[:, f % 2, 0:width], h_bank[f % 4][:, 0:width], ACT.Gelu, bias=b_)
                    a.activation(h_hi[:, f, 0:width], h_bank[f % 4][:, 0:width], ACT.Gelu, bias=b_).then_inc(h_made, 1)

            def high1(s):
                a.activation(w1_hi[s][:, :, :], w1_sb[s][:, :, :], ACT.Copy).then_inc(w1hi_made, 1)

            def high2(s):
                a.activation(w2_hi[s][:, :, :], w2_sb[s][:, :, :], ACT.Copy).then_inc(w2hi_made, 1)

            act.sem_inc(h_made, 4)
            act.wait_ge(tok_made, 1)
            act.wait_ge(more_made, 1)
            tiles_code = act.value_load(more[0:1, 0:1], min_val=0, max_val=4 ** E - 1)
            act.wait_ge(l_w1[1], 16)
            high1(1)
            turned(0, 0)
            with act.Fori(0, E // 2 - 1) as it:
                expert(it, 0, 2)
                expert(it, 1, 2)
            expert(E // 2 - 1, 0, 1)
            expert(E // 2 - 1, 1, 0)

        @block.vector
        def _(dve):
            steps = Count(dve, dve_step)
            v = nc.vector

            def full(name):
                dve.wait_ge(small_full, job_at[name] + 1)
                return small(name)

            def stats_(c):
                dve.wait_ge(l_x[c], 16)
                if c:
                    dve.wait_ge(xn_made, c)
                for t in range(TT):
                    steps.up(v.bn_stats(stats[:, t, :], xr[:, c * TT + t, 0:D]))
                steps.settle()
                for t in range(TT):
                    ins = v.bn_aggr(mv[:, t, :], stats[:, t, :])
                ins.then_inc(stats_made, 1)

            def norm(c):
                dve.wait_ge(std_made, c + 1)
                if c:
                    dve.wait_ge(small_full, job_at[("xT", c - 1, KC - 1)] + 1)
                for t in range(TT):
                    ins = v.tensor_scalar(xn[:, t, :], xr[:, c * TT + t, 0:D], mv[:, t, 0:1], rstd[:, t:t + 1],
                                          ALU.subtract, ALU.mult)
                ins.then_inc(xn_made, 1)

            def proj(c):
                for half in range(KC):
                    ps = full(("q", c, half))
                    dve.wait_ge(qhi_made, KC * c + half + 1)
                    if c and half == 0:
                        dve.wait_ge(l_qd, 32 * c)
                    v.tensor_tensor(q_lo[:, half, :], ps[:, :], q_hi[c % 2][:, half, :].bitcast(F32), ALU.subtract).then_inc(qlo_made, 1)
                    dve.wait_ge(qlo_made, KC * c + half + 1)
                    dve.engine_nop().then_inc(small_dve, 1)

            def keys(b):
                for half in range(KC):
                    ps = full(("k", b, half))
                    dve.wait_ge(khi_made, KC * b + half + 1)
                    if b:
                        dve.wait_ge(l_kd, 32 * b)
                    v.tensor_tensor(k_lo[:, half, :], ps[:, 0:MP], k_hi[:, half, :].bitcast(F32), ALU.subtract).then_inc(klo_made, 1)
                    dve.wait_ge(klo_made, KC * b + half + 1)
                    dve.engine_nop().then_inc(small_dve, 1)
                    if b == 0:
                        spread(b, half)

            def spread(b, half):
                if b:
                    dve.wait_ge(scan_full, TT * AU * PER_B * b)
                    dve.wait_ge(khi_made, KC * b + half + 1)
                else:
                    dve.wait_ge(consts_made, 1)
                v.tensor_tensor(kd_hi[:, half], k_hi[:, half, :].bitcast(F32).unsqueeze(1).to_broadcast([P, HH, MP]),
                                headsel[:, :].unsqueeze(2).to_broadcast([P, HH, MP]), ALU.mult).then_inc(kdhi_made, 1)

            def selectors(b):
                dve.wait_ge(consts_made, 2)
                dve.wait_ge(keys_zeroed, b + 1)
                for g in range(G):
                    steps.up(v.tensor_copy(ks_main[b][96:P, g, :, :], pairsel[96:P, :, :]))
                    c0 = 2 * RP * (g % 2)
                    steps.up(v.tensor_copy(ks_rest[b][96:P, g, c0:c0 + 2 * RP].rearrange("p (a m) -> p a m", a=2),
                                           pairsel[96:P, :, 0:RP]))
                steps.settle()
                dve.engine_nop().then_inc(sel_made, 1)

            def scan(c, i):
                t, u = divmod(i, AU)
                n = c * TT * AU + i
                dve.wait_ge(scan_full, n + 1)
                if i == 0 and c:
                    dve.wait_ge(max_made, c)
                if u < 4:
                    v.tensor_reduce(mx[:, t, 4 * u:4 * u + 4], scan_bank(c, n)[:, :].rearrange("p (h m) -> p h m", h=4),
                                    AX_X, ALU.max).then_inc(scan_read, 1)
                else:
                    v.tensor_reduce(mxr[:, t, :], scan_bank(c, n)[:, :].rearrange("p (h m) -> p h m", h=H),
                                    AX_X, ALU.max).then_inc(scan_read, 1)

            def maxima(c):
                dve.wait_ge(scan_read, TT * AU * (c + 1))
                if c:
                    dve.wait_ge(small_full, job_at[("max", c - 1)] + 1)
                v.tensor_tensor(mxx[:, :, :], mx[:, :, :], mxr[:, :, :], ALU.max).then_inc(max_made, 1)

            def divide(c, half, t):
                hf = 2 * c + half
                toks = slice(t * P, (t + 1) * P)
                if t == 0:
                    dve.wait_ge(pv_done, 3 * hf + 3)
                if half == 0 and c:
                    dve.wait_ge(small_full, job_at[("fold", c - 1, t)] + 1)
                if hf:
                    dve.wait_ge(att_made, TT * (hf - 1) + t + 1)
                steps.up(v.reciprocal(rz[:, toks], z_bank[:, toks]))
                steps.settle()
                v.tensor_tensor(att[:, half, toks], o_bank[:, toks], rz[:, toks], ALU.mult).then_inc(att_made, 1)

            def fold(c, t):
                if t == 0:
                    dve.wait_ge(xb_made, c + 1)
                ps = full(("fold", c, t))
                tt = c * TT + t
                v.tensor_tensor(xr[:, tt, 0:D], ps[:, 0:D], xr[:, tt, 0:D], ALU.add).then_inc(small_dve, 1)
                dve.wait_ge(small_dve, dve_count(("fold", c, t)))
                steps.up(v.bn_stats(stats[:, t, :], xr[:, tt, 0:D]))
                steps.settle()
                v.bn_aggr(xr[:, tt, D:D + 2], stats[:, t, :]).then_inc(x1_made, 1)

            def row(c, t):
                tt = c * TT + t
                dve.wait_ge(rstd_made, tt + 1)
                if tt >= 2:
                    dve.wait_ge(small_full, job_at[("nT", (tt - 2) // TT, (tt - 2) % TT)] + 1)
                v.tensor_scalar(xn2[:, t % 2, :], xr[:, tt, 0:D], xr[:, tt, D:D + 1], xr[:, tt, D + 1:D + 2],
                                ALU.subtract, ALU.mult).then_inc(xn2_made, 1)

            def logits(c, t):
                ps = full(("logits", c, t))
                if c and t == 0:
                    dve.wait_ge(gate_made, c)
                    dve.wait_ge(onehot_made, c)
                v.tensor_copy(lg[:, t, :], ps[:, 0:E]).then_inc(small_dve, 1)

            def pick(c, i):
                sl = slice(c * TT, (c + 1) * TT)
                if i == 0:
                    dve.wait_ge(small_dve, dve_count(("logits", c, TT - 1)))
                    steps.up(v.tensor_reduce(lmax[:, :], lg[:, :, :], AX_X, ALU.max))
                    steps.settle()
                    v.tensor_tensor(below[:, :, :], lg[:, :, :], lmax[:, :].unsqueeze(2).to_broadcast([P, TT, E]),
                                    ALU.subtract).then_inc(below_made, 1)
                if i == 1:
                    dve.wait_ge(below_made, c + 1)
                    if c == 0:
                        dve.wait_ge(consts_made, 3)
                    steps.up(v.scalar_tensor_tensor(out=rank[:, :, :], in0=below[:, :, :], scalar=0.0, in1=first[:, :, :],
                                                    op0=ALU.is_ge, op1=ALU.mult))
                    steps.settle()
                    steps.up(v.tensor_reduce(best[:, :], rank[:, :, :], AX_X, ALU.max))
                    steps.settle()
                    v.tensor_tensor(onehot[:, sl, :], rank[:, :, :], best[:, :].unsqueeze(2).to_broadcast([P, TT, E]),
                                    ALU.is_equal).then_inc(onehot_made, 1)
                    if c < NCH - 1:
                        dve.wait_ge(onehot_made, c + 1)
                        steps.up(v.tensor_reduce(count[:, :], onehot[:, 0:(c + 1) * TT, :].rearrange("p t e -> p e t"), AX_X, ALU.add))
                        steps.settle()
                        v.tensor_copy(before[:, c, :], count[:, :]).then_inc(before_made, 1)
                if i == 2:
                    dve.wait_ge(lex_made, c + 1)
                    steps.up(v.tensor_reduce(lsum[:, :], lex[:, :, :], AX_X, ALU.add))
                    steps.settle()
                    v.reciprocal(xr[:, sl, D + 2], lsum[:, :]).then_inc(gate_made, 1)

            def run(list_):
                for step, c, i in list_:
                    if step == "stats":
                        stats_(c)
                    if step == "norm":
                        norm(c)
                    if step == "scan":
                        scan(c, i)
                    if step == "max":
                        maxima(c)
                    if step == "divide":
                        divide(c, *i)
                    if step == "fold":
                        fold(c, i)
                    if step == "xn2":
                        row(c, i)
                    if step == "logits":
                        logits(c, i)
                    if step == "pick":
                        pick(c, i)
                    if step == "place":
                        place(c)
                    if step == "proj":
                        proj(c)
                    if step == "keys":
                        keys(c)
                    if step == "spread":
                        for half in range(KC):
                            spread(c, half)
                        selectors(c)

            def place(c):
                sl = slice(c * TT, (c + 1) * TT)
                ps = full(("place", c, 0))
                dve.wait_ge(onehot_made, c + 1)
                v.tensor_tensor(cum[:, sl, :], ps[:, 0:TT * E].rearrange("p (t e) -> p t e", e=E), onehot[:, sl, :],
                                ALU.mult).then_inc(small_dve, 1)
                steps.up(v.tensor_tensor(ebs[:, sl, :], ebase[:, sl, :], onehot[:, sl, :], ALU.mult))
                dve.wait_ge(small_dve, dve_count(("place", c, 0)))
                steps.settle()
                steps.up(v.tensor_reduce(pos[:, sl], cum[:, sl, :], AX_X, ALU.add))
                steps.up(v.tensor_reduce(jslot[:, sl], ebs[:, sl, :], AX_X, ALU.add))
                steps.settle()
                for m in range(1, JT + 1):
                    steps.up(v.tensor_scalar(over[:, sl, m - 1], pos[:, sl], float(m * P), None, ALU.is_ge))
                steps.settle()
                for m in range(1, JT + 1):
                    steps.up(v.tensor_tensor(jslot[:, sl], jslot[:, sl], over[:, sl, m - 1], ALU.add))
                    steps.up(v.scalar_tensor_tensor(out=pos[:, sl], in0=over[:, sl, m - 1], scalar=-float(P) if m < JT else float(NTOK),
                                                    in1=pos[:, sl], op0=ALU.mult, op1=ALU.add))
                    steps.settle()
                steps.up(v.tensor_tensor(psel[:, sl, :], lane[:, :].unsqueeze(1).to_broadcast([P, TT, P]),
                                         pos[:, sl].unsqueeze(2).to_broadcast([P, TT, P]), ALU.is_equal))
                steps.up(v.tensor_tensor(jsel[:, sl, :], lane[:, 0:J].unsqueeze(1).to_broadcast([P, TT, J]),
                                         jslot[:, sl].unsqueeze(2).to_broadcast([P, TT, J]), ALU.is_equal))
                steps.settle()
                steps.up(v.tensor_scalar(what[:, sl, 0, :], jsel[:, sl, :], part[:, 0:1], None, ALU.mult))
                steps.up(v.tensor_tensor(what[:, sl, 1, :], jsel[:, sl, :], tilefirst[:, sl, :], ALU.mult))
                steps.settle()
                dve.engine_nop().then_inc(what_made, 1)

            def fill():
                dve.wait_ge(slots_full, 1)
                v.tensor_scalar(tok_load[:, :], a_bank[0][:, 0:J], FAR, float(NTOK - 1), ALU.add, ALU.min).then_inc(tok_made, 1)
                steps.up(v.tensor_scalar(tok_store[:, :], a_bank[0][:, 0:J], FAR, None, ALU.add))
                for m in range(1, JT):
                    steps.up(v.tensor_scalar(past[:, m - 1, :], a_bank[1][0:1, 0:E], float(m * P + 1), None, ALU.is_ge))
                steps.settle()
                steps.up(v.tensor_tensor(past[:, :, :], past[:, :, :], bits[:, :, :], ALU.mult))
                steps.settle()
                steps.up(v.tensor_reduce(code[:, :], past[:, :, :].rearrange("p m e -> p (m e)"), AX_X, ALU.add))
                steps.settle()
                v.tensor_copy(more[:, :], code[:, :]).then_inc(more_made, 1)

            def low1(s, n, quarter):
                if quarter == 0:
                    dve.wait_ge(w1hi_made, n)
                fs = slice(quarter * (F // 4), (quarter + 1) * (F // 4))
                v.tensor_tensor(w1_lo[s][:, :, fs], w1_sb[s][:, :, fs], w1_hi[s][:, :, fs].bitcast(F32), ALU.subtract).then_inc(w1lo_made, 1)

            def low2(s, n):
                dve.wait_ge(w2hi_made, n)
                v.tensor_tensor(w2_lo[s][:, :, :], w2_sb[s][:, :, :], w2_hi[s][:, :, :].bitcast(F32), ALU.subtract).then_inc(w2lo_made, 1)

            for t in v_main + v_rest:
                ins = v.memset(t[:], 0.0)
            ins.then_inc(values_zeroed, 1)
            for stage, c in STAGES:
                if stage == "stats":
                    stats_(c)
                if stage == "norm":
                    norm(c)
                if stage == "proj":
                    proj(c)
                if stage == "keys":
                    keys(c)
                if stage == "scan":
                    run(scan_steps())
                    selectors(0)
                if stage == "mix":
                    run(mix_steps(c))
                if stage == "tail":
                    run(tail_steps(c))
                if stage == "tail":
                    fill()
                    for quarter in range(4):
                        low1(0, 1, quarter)

            def at(t, e, j):
                return t[:, bass.ds(e * JT + j, 1), :] if not isinstance(e, int) else t[:, e * JT + j:e * JT + j + 1, :]

            def normalise_first():
                for j in range(JT):
                    dve.wait_ge(l_first[j], 16)
                    v.tensor_scalar(gn[:, 0, j, :], xg[:, j, 0:D], xg[:, j, D:D + 1], xg[:, j, D + 1:D + 2],
                                    ALU.subtract, ALU.mult).then_inc(gn_made, 1)

            def normalise(e, s, uses):
                dve.wait_ge(l_gather[s], uses * (16 * JT))
                dve.wait_ge(t_full, e * len(TURNS))
                for j in range(JT):
                    r = at(xg, e, j)
                    v.tensor_scalar(gn[:, s, j, :], r[:, 0, 0:D], r[:, 0, D:D + 1], r[:, 0, D + 1:D + 2],
                                    ALU.subtract, ALU.mult).then_inc(gn_made, 1)

            def turned(e, s):
                for part_, js in enumerate(TURNS):
                    dve.wait_ge(gT_made, len(TURNS) * e + (part_ + 1))
                    to, src = turned_aps(gT_lo, s, part_, js)
                    v.tensor_tensor(to, src, turned_aps(gT_hi, s, part_, js)[0].bitcast(F32), ALU.subtract).then_inc(gTlo_made, 1)

            def expert(it, s, left):
                e = it * 2 + s
                if left:
                    normalise(e + 1, 1 - s, it + 1)
                tiles = (tiles_code >> (e * 2)) & 3
                with dve.If(tiles > JT - 2):
                    lows(e, s, left, CAP)
                with dve.Else():
                    lows(e, s, left, CAP - P)
                for j in range(JT):
                    dve.wait_ge(y_full, e * JT + (j + JT + 1))
                    dve.wait_ge(y_made, e * JT + (j + 1))
                    b2_e = b2_sb[:, bass.ds(e, 1), :] if not isinstance(e, int) else b2_sb[:, e:e + 1, :]
                    v.tensor_tensor(y1[:, j, :], y_bank[(JT * s + j) % 2][:, 0:D], b2_e[:, 0, :], ALU.add).then_inc(y_read, 1)
                    dve.wait_ge(y_read, e * JT + (j + 3))
                    r = at(xg, e, j)
                    v.scalar_tensor_tensor(out=r[:, 0, 0:D], in0=y1[:, j, :], scalar=r[:, 0, D + 2:D + 3], in1=r[:, 0, 0:D],
                                           op0=ALU.mult, op1=ALU.add).then_inc(y_made, 1)
                    if j == 0 and left:
                        turned(e + 1, 1 - s)
            def lows(e, s, left, width):
                for f in range(FC):
                    dve.wait_ge(h_made, e * FC + (f + 5))
                    v.tensor_tensor(h_lo[:, f, 0:width], h32[:, f % 2, 0:width], h_hi[:, f, 0:width].bitcast(F32),
                                    ALU.subtract).then_inc(hlo_made, 1)
                    if left and f % 2:
                        low1(1 - s, e + 2, f // 2)

            dve.wait_ge(more_made, 1)
            tiles_code = dve.value_load(more[0:1, 0:1], min_val=0, max_val=4 ** E - 1)
            dve.sem_inc(y_read, 2)
            dve.sem_inc(y_made, JT)
            dve.sem_inc(hlo_made, 2)
            dve.sem_inc(gTlo_made, len(TURNS))
            dve.wait_ge(tok_made, 1)
            normalise_first()
            turned(0, 0)
            low2(0, 1)
            dve.wait_ge(l_b2, 16)
            with dve.Fori(0, E // 2 - 1) as it:
                expert(it, 0, 2)
                expert(it, 1, 2)
            expert(E // 2 - 1, 0, 1)
            expert(E // 2 - 1, 1, 0)


_INS = ['x', 'ctx_1024', 'mask_BxSxS2_bk0', 'L0_xattn_Wq', 'L0_xattn_Wkv', 'L0_xattn_Wproj', 'L0_xattn_bproj',
        'L0_ffn_router_w', 'L0_ffn_w1', 'L0_ffn_b1', 'L0_ffn_w2', 'L0_ffn_b2']
_OUTS = [((2, 1024, 256), 'float32')]


def kernel(**inputs):
    import numpy as _np
    import concourse.bacc as _bacc
    from concourse import mybir as _mybir
    from concourse.bass_utils import run_bass_kernel_spmd as _run

    nc = _bacc.Bacc("TRN2", target_bir_lowering=False, num_devices=1)
    arrays, args = {}, []
    for name in _INS:
        a = _np.ascontiguousarray(inputs[name])
        arrays[f"in_{name}_dram"] = a
        args.append(nc.dram_tensor(f"in_{name}_dram", a.shape, _mybir.dt.from_np(a.dtype), kind="ExternalInput").ap())
    for i, (shape, dtype) in enumerate(_OUTS):
        dt = _mybir.dt.from_np(_np.dtype(dtype))
        args.append(nc.dram_tensor(f"out_{i}_dram", shape, dt, kind="ExternalOutput").ap())
    build(nc, *args)
    r = _run(nc, [arrays], core_ids=[0])
    return r.results[0]["out_0_dram"]
```
